# Optimizing a Trainium2 kernel written in Bass

```python
import numpy as np
import jax
import jax.numpy as jnp

def _softmax(x, axis=-1):
    return jax.nn.softmax(x, axis=axis)

def _gelu(x):
    return jax.nn.gelu(x, approximate=True)

def _silu(x):
    return jax.nn.silu(x)

def _sigmoid(x):
    return jax.nn.sigmoid(x)

def _layernorm(x, axis=-1, eps=1e-05):
    m = jnp.mean(x, axis=axis, keepdims=True)
    v = jnp.var(x, axis=axis, keepdims=True)
    return (x - m) / jnp.sqrt(v + eps)

def _scatter_add(tgt, idx, src, axis=0):
    return tgt.at[idx].add(src)

def _segment_sum(src, seg, n):
    return jax.ops.segment_sum(src, seg, n)
kernel_name = 'mk_recurrent_d2_jaxref_r8_048c99'

def setup_inputs(seed: int=0):
    np.random.seed(seed)
    _w = jnp.asarray

    def _L0_attn_setup():
        import jax, jax.numpy as jnp
        import numpy as np
        D_MODEL = 256
        N_HEADS = 16
        D_K = D_MODEL // N_HEADS
        EPS = 1e-06
        key = jax.random.key(seed)
        ks = jax.random.split(key, 9)
        s = 1.0 / np.sqrt(D_MODEL)
        return {'x': jax.random.normal(ks[0], (4, 512, D_MODEL), dtype=jnp.float32), 'Wq': jax.random.normal(ks[1], (D_MODEL, D_MODEL), dtype=jnp.float32) * s, 'bq': jnp.zeros((D_MODEL,), dtype=jnp.float32), 'Wk': jax.random.normal(ks[2], (D_MODEL, D_MODEL), dtype=jnp.float32) * s, 'bk': jnp.zeros((D_MODEL,), dtype=jnp.float32), 'Wv': jax.random.normal(ks[3], (D_MODEL, D_MODEL), dtype=jnp.float32) * s, 'bv': jnp.zeros((D_MODEL,), dtype=jnp.float32), 'Wo': jax.random.normal(ks[4], (D_MODEL, D_MODEL), dtype=jnp.float32) * s, 'bo': jnp.zeros((D_MODEL,), dtype=jnp.float32)}
    _L0_attn_in = _L0_attn_setup()

    def _L0_ffn_setup():
        import jax, jax.numpy as jnp
        import numpy as np
        E = 8
        TOP_K = 2
        H = 256
        I_MOE = 176
        I_SH = 704
        B, S = (2, 256)

        def _moe_forward(hidden_states, router_weight, gate_up_proj, down_proj, sh_gate_w, sh_up_w, sh_down_w, shared_gate_w):
            b, s, h = hidden_states.shape
            x = hidden_states.reshape(-1, h)
            shared = jnp.einsum('ti,hi->th', jax.nn.silu(x @ sh_gate_w.T) * (x @ sh_up_w.T), sh_down_w)
            logits = x @ router_weight.T
            probs = jax.nn.softmax(logits.astype(jnp.float32), axis=-1)
            top_v, top_i = jax.lax.top_k(probs, TOP_K)
            top_v = top_v / top_v.sum(axis=-1, keepdims=True)
            combine = (jax.nn.one_hot(top_i, E, dtype=top_v.dtype) * top_v[..., None]).sum(axis=1)
            out = jnp.zeros_like(x)
            for e in range(E):
                gu = x @ gate_up_proj[e].T
                gate, up = (gu[:, :I_MOE], gu[:, I_MOE:])
                cur = jax.nn.silu(gate) * up @ down_proj[e].T
                out = out + cur * combine[:, e:e + 1]
            out = out + jax.nn.sigmoid(x @ shared_gate_w.T) * shared
            return out.reshape(b, s, h)
        key = jax.random.key(seed)
        ks = jax.random.split(key, 8)
        scale = 0.02
        return {'hidden_states': jax.random.normal(ks[0], (B, S, H), dtype=jnp.float32), 'router_weight': jax.random.normal(ks[1], (E, H), dtype=jnp.float32) * scale, 'gate_up_proj': jax.random.normal(ks[2], (E, 2 * I_MOE, H), dtype=jnp.float32) * scale, 'down_proj': jax.random.normal(ks[3], (E, H, I_MOE), dtype=jnp.float32) * scale, 'sh_gate_w': jax.random.normal(ks[4], (I_SH, H), dtype=jnp.float32) * scale, 'sh_up_w': jax.random.normal(ks[5], (I_SH, H), dtype=jnp.float32) * scale, 'sh_down_w': jax.random.normal(ks[6], (H, I_SH), dtype=jnp.float32) * scale, 'shared_gate_w': jax.random.normal(ks[7], (1, H), dtype=jnp.float32) * scale}
    _L0_ffn_in = _L0_ffn_setup()

    def _L1_attn_setup():
        import math
        import jax, jax.numpy as jnp
        import numpy as np

        def _alibi_slopes(n):

            def pow2_slopes(n):
                start = 2.0 ** (-2.0 ** (-(math.log2(n) - 3)))
                return [start * start ** i for i in range(n)]
            if math.log2(n).is_integer():
                return pow2_slopes(n)
            cp2 = 2 ** math.floor(math.log2(n))
            return pow2_slopes(cp2) + _alibi_slopes(2 * cp2)[0::2][:n - cp2]
        NUM_HEADS = 16
        key = jax.random.key(seed)
        ks = jax.random.split(key, 5)
        B, S, H = (2, 256, 256)
        return {'hidden_states': jax.random.normal(ks[0], (B, S, H), jnp.float32), 'w_qkv': jax.random.normal(ks[1], (H, 3 * H), jnp.float32) * H ** (-0.5), 'b_qkv': jax.random.normal(ks[2], (3 * H,), jnp.float32) * 0.02, 'w_proj': jax.random.normal(ks[3], (H, H), jnp.float32) * H ** (-0.5), 'b_proj': jax.random.normal(ks[4], (H,), jnp.float32) * 0.02}
    _L1_attn_in = _L1_attn_setup()

    def _L1_ffn_setup():
        import jax, jax.numpy as jnp
        import numpy as np
        TOPK = 2

        def _mlp(x, w1, w2, w3):
            a = jnp.dot(x, w1.T).astype(jnp.float32)
            b = jnp.dot(x, w3.T).astype(jnp.float32)
            h = (jax.nn.silu(a) * b).astype(x.dtype)
            return jnp.dot(h, w2.T)
        key = jax.random.key(seed)
        ks = jax.random.split(key, 8)
        B, S, D, I, E = (4, 256, 256, 176, 16)
        SI = I * 2
        sc = 0.02
        return {'x': jax.random.normal(ks[0], (B, S, D), jnp.bfloat16), 'gate_w': jax.random.normal(ks[1], (E, D), jnp.float32) * sc, 'w1': jax.random.normal(ks[2], (E, I, D), jnp.bfloat16) * sc, 'w2': jax.random.normal(ks[3], (E, D, I), jnp.bfloat16) * sc, 'w3': jax.random.normal(ks[4], (E, I, D), jnp.bfloat16) * sc, 'sw1': jax.random.normal(ks[5], (SI, D), jnp.bfloat16) * sc, 'sw2': jax.random.normal(ks[6], (D, SI), jnp.bfloat16) * sc, 'sw3': jax.random.normal(ks[7], (SI, D), jnp.bfloat16) * sc}
    _L1_ffn_in = _L1_ffn_setup()
    _d = {'L0_attn_x': _L0_attn_in['x'], 'L0_attn_Wq': _L0_attn_in['Wq'], 'L0_attn_bq': _L0_attn_in['bq'], 'L0_attn_Wk': _L0_attn_in['Wk'], 'L0_attn_bk': _L0_attn_in['bk'], 'L0_attn_Wv': _L0_attn_in['Wv'], 'L0_attn_bv': _L0_attn_in['bv'], 'L0_attn_Wo': _L0_attn_in['Wo'], 'L0_attn_bo': _L0_attn_in['bo'], 'L0_ffn_router_weight': _L0_ffn_in['router_weight'], 'L0_ffn_gate_up_proj': _L0_ffn_in['gate_up_proj'], 'L0_ffn_down_proj': _L0_ffn_in['down_proj'], 'L0_ffn_sh_gate_w': _L0_ffn_in['sh_gate_w'], 'L0_ffn_sh_up_w': _L0_ffn_in['sh_up_w'], 'L0_ffn_sh_down_w': _L0_ffn_in['sh_down_w'], 'L0_ffn_shared_gate_w': _L0_ffn_in['shared_gate_w'], 'L1_attn_w_qkv': _L1_attn_in['w_qkv'], 'L1_attn_b_qkv': _L1_attn_in['b_qkv'], 'L1_attn_w_proj': _L1_attn_in['w_proj'], 'L1_attn_b_proj': _L1_attn_in['b_proj'], 'L1_ffn_gate_w': _L1_ffn_in['gate_w'], 'L1_ffn_w1': _L1_ffn_in['w1'], 'L1_ffn_w2': _L1_ffn_in['w2'], 'L1_ffn_w3': _L1_ffn_in['w3'], 'L1_ffn_sw1': _L1_ffn_in['sw1'], 'L1_ffn_sw2': _L1_ffn_in['sw2'], 'L1_ffn_sw3': _L1_ffn_in['sw3']}
    _x0 = _d['L0_attn_x']
    _d['L0_attn_x'] = jax.random.normal(jax.random.fold_in(jax.random.key(seed), 1), (8, 256, 256), dtype=_x0.dtype)
    del _x0
    return _d

def reference(L0_attn_x, L0_attn_Wq, L0_attn_bq, L0_attn_Wk, L0_attn_bk, L0_attn_Wv, L0_attn_bv, L0_attn_Wo, L0_attn_bo, L0_ffn_router_weight, L0_ffn_gate_up_proj, L0_ffn_down_proj, L0_ffn_sh_gate_w, L0_ffn_sh_up_w, L0_ffn_sh_down_w, L0_ffn_shared_gate_w, L1_attn_w_qkv, L1_attn_b_qkv, L1_attn_w_proj, L1_attn_b_proj, L1_ffn_gate_w, L1_ffn_w1, L1_ffn_w2, L1_ffn_w3, L1_ffn_sw1, L1_ffn_sw2, L1_ffn_sw3):

    def _L0_attn_ref(x, Wq, bq, Wk, bk, Wv, bv, Wo, bo):
        import jax, jax.numpy as jnp
        import numpy as np
        D_MODEL = 256
        N_HEADS = 16
        D_K = D_MODEL // N_HEADS
        EPS = 1e-06
        b, n, _ = x.shape
        h, d = (N_HEADS, D_K)

        def proj(W, bias):
            y = jnp.einsum('bnm,dm->bnd', x, W) + bias
            return y.reshape(b, n, h, d).transpose(0, 2, 1, 3)
        Q = jax.nn.relu(proj(Wq, bq))
        K = jax.nn.relu(proj(Wk, bk))
        V = proj(Wv, bv)
        pos = jnp.arange(n, dtype=x.dtype)
        decay = jnp.exp(-pos / n)[None, None, :, None]
        Q = Q * decay
        K = K * decay
        KV = jnp.einsum('bhnd,bhne->bhde', K, V)
        Ksum = K.sum(axis=2)
        Z = 1.0 / (jnp.einsum('bhnd,bhd->bhn', Q, Ksum)[..., None] + EPS)
        out = jnp.einsum('bhnd,bhde->bhne', Q, KV) * Z
        out = out.transpose(0, 2, 1, 3).reshape(b, n, h * d)
        return jnp.einsum('bnm,dm->bnd', out, Wo) + bo

    def _L0_ffn_ref(hidden_states, router_weight, gate_up_proj, down_proj, sh_gate_w, sh_up_w, sh_down_w, shared_gate_w):
        import jax, jax.numpy as jnp
        import numpy as np
        E = 8
        TOP_K = 2
        H = 256
        I_MOE = 176
        I_SH = 704
        B, S = (2, 256)

        def _moe_forward(hidden_states, router_weight, gate_up_proj, down_proj, sh_gate_w, sh_up_w, sh_down_w, shared_gate_w):
            b, s, h = hidden_states.shape
            x = hidden_states.reshape(-1, h)
            shared = jnp.einsum('ti,hi->th', jax.nn.silu(x @ sh_gate_w.T) * (x @ sh_up_w.T), sh_down_w)
            logits = x @ router_weight.T
            probs = jax.nn.softmax(logits.astype(jnp.float32), axis=-1)
            top_v, top_i = jax.lax.top_k(probs, TOP_K)
            top_v = top_v / top_v.sum(axis=-1, keepdims=True)
            combine = (jax.nn.one_hot(top_i, E, dtype=top_v.dtype) * top_v[..., None]).sum(axis=1)
            out = jnp.zeros_like(x)
            for e in range(E):
                gu = x @ gate_up_proj[e].T
                gate, up = (gu[:, :I_MOE], gu[:, I_MOE:])
                cur = jax.nn.silu(gate) * up @ down_proj[e].T
                out = out + cur * combine[:, e:e + 1]
            out = out + jax.nn.sigmoid(x @ shared_gate_w.T) * shared
            return out.reshape(b, s, h)
        return _moe_forward(hidden_states, router_weight, gate_up_proj, down_proj, sh_gate_w, sh_up_w, sh_down_w, shared_gate_w)

    def _L1_attn_ref(hidden_states, w_qkv, b_qkv, w_proj, b_proj):
        import math
        import jax, jax.numpy as jnp
        import numpy as np

        def _alibi_slopes(n):

            def pow2_slopes(n):
                start = 2.0 ** (-2.0 ** (-(math.log2(n) - 3)))
                return [start * start ** i for i in range(n)]
            if math.log2(n).is_integer():
                return pow2_slopes(n)
            cp2 = 2 ** math.floor(math.log2(n))
            return pow2_slopes(cp2) + _alibi_slopes(2 * cp2)[0::2][:n - cp2]
        NUM_HEADS = 16
        B, S, H = hidden_states.shape
        nh = NUM_HEADS
        hd = H // nh
        scale = 1.0 / hd
        qkv = hidden_states @ w_qkv + b_qkv
        q, k, v = jnp.split(qkv, 3, axis=-1)
        q = q.reshape(B, S, nh, hd)
        k = k.reshape(B, S, nh, hd)
        v = v.reshape(B, S, nh, hd)
        scores = jnp.einsum('bqhd,bkhd->bhqk', q, k) * scale
        slopes = jnp.asarray(_alibi_slopes(nh), dtype=scores.dtype)
        pos = jnp.arange(S)
        rel = (pos[None, :] - pos[:, None]).astype(scores.dtype)
        bias = slopes[:, None, None] * rel[None, :, :]
        causal = pos[None, :] <= pos[:, None]
        scores = jnp.where(causal[None, None], scores + bias[None], jnp.finfo(scores.dtype).min)
        attn = jax.nn.softmax(scores, axis=-1)
        out = jnp.einsum('bhqk,bkhd->bqhd', attn, v).reshape(B, S, H)
        return out @ w_proj + b_proj

    def _L1_ffn_ref(x, gate_w, w1, w2, w3, sw1, sw2, sw3):
        import jax, jax.numpy as jnp
        import numpy as np
        TOPK = 2

        def _mlp(x, w1, w2, w3):
            a = jnp.dot(x, w1.T).astype(jnp.float32)
            b = jnp.dot(x, w3.T).astype(jnp.float32)
            h = (jax.nn.silu(a) * b).astype(x.dtype)
            return jnp.dot(h, w2.T)
        B, S, D = x.shape
        E = gate_w.shape[0]
        xf = x.reshape(-1, D)
        T = xf.shape[0]
        scores = jax.nn.sigmoid(jnp.dot(xf.astype(jnp.float32), gate_w.T))
        topv, topi = jax.lax.top_k(scores, TOPK)
        topv = topv / topv.sum(axis=-1, keepdims=True)
        dw = jnp.zeros((T, E), jnp.float32).at[jnp.arange(T)[:, None], topi].add(topv)
        y0 = _mlp(xf, sw1, sw2, sw3).astype(jnp.float32)

        def step(y, ws):
            e1, e2, e3, we = ws
            out = _mlp(xf, e1, e2, e3).astype(jnp.float32)
            return (y + out * we[:, None], None)
        y, _ = jax.lax.scan(step, y0, (w1, w2, w3, dw.T))
        return y.astype(x.dtype).reshape(B, S, D)
    x = L0_attn_x
    xn = _layernorm(x, axis=-1)
    s = _L0_attn_ref(xn, L0_attn_Wq, L0_attn_bq, L0_attn_Wk, L0_attn_bk, L0_attn_Wv, L0_attn_bv, L0_attn_Wo, L0_attn_bo)
    g = _silu(_L0_ffn_ref(xn, L0_ffn_router_weight, L0_ffn_gate_up_proj, L0_ffn_down_proj, L0_ffn_sh_gate_w, L0_ffn_sh_up_w, L0_ffn_sh_down_w, L0_ffn_shared_gate_w))
    x = x + s * g
    xn = _layernorm(x, axis=-1)
    s = _L1_attn_ref(xn, L1_attn_w_qkv, L1_attn_b_qkv, L1_attn_w_proj, L1_attn_b_proj)
    g = _silu(_L1_ffn_ref(xn, L1_ffn_gate_w, L1_ffn_w1, L1_ffn_w2, L1_ffn_w3, L1_ffn_sw1, L1_ffn_sw2, L1_ffn_sw3))
    x = x + s * g
    return x

_drawn_inputs = setup_inputs


def setup_inputs(seed=0):
    import zlib

    import numpy as np

    out = dict(_drawn_inputs(seed))
    spreads = {'L0_attn_bq': (0.0, 0.8),
     'L0_attn_bk': (0.0, 0.8),
     'L0_attn_bv': (0.0, 0.8),
     'L0_attn_bo': (0.0, 0.8)}
    factors = {'L0_attn_Wq': 8.0,
     'L0_attn_Wk': 8.0,
     'L0_attn_Wv': 8.0,
     'L0_attn_Wo': 8.0,
     'L0_ffn_router_weight': 8.0,
     'L0_ffn_gate_up_proj': 8.0,
     'L0_ffn_down_proj': 8.0,
     'L0_ffn_sh_gate_w': 8.0,
     'L0_ffn_sh_up_w': 8.0,
     'L0_ffn_sh_down_w': 8.0,
     'L0_ffn_shared_gate_w': 8.0,
     'L1_attn_w_qkv': 8.0,
     'L1_attn_b_qkv': 8.0,
     'L1_attn_w_proj': 8.0,
     'L1_attn_b_proj': 173.563,
     'L1_ffn_gate_w': 8.0,
     'L1_ffn_w1': 8.0,
     'L1_ffn_w2': 8.0,
     'L1_ffn_w3': 8.0,
     'L1_ffn_sw1': 8.0,
     'L1_ffn_sw2': 8.0,
     'L1_ffn_sw3': 8.0}
    for name, (base, spread) in spreads.items():
        noise = np.random.default_rng([zlib.crc32(name.encode()), seed]).standard_normal(out[name].shape)
        drawn = base * np.exp(spread * noise) if base else spread * noise
        out[name] = jnp.asarray(drawn.astype(out[name].dtype))
    for name, factor in factors.items():
        out[name] = (out[name] * factor).astype(out[name].dtype)
    return out
```

```python
from contextlib import ExitStack

import concourse.bass as bass
from concourse import mybir

F32 = mybir.dt.float32
F32R = mybir.dt.float32r
BF16 = mybir.dt.bfloat16
F16 = mybir.dt.float16
U32 = mybir.dt.uint32
ALU = mybir.AluOpType
ACT = mybir.ActivationFunctionType
AX = mybir.AxisListType
ds = bass.ds

P = 128
D = 256
KT = D // P
SEQ = 256
CH = 512
TPC = CH // P
H, HD = 16, 16
EPS_LN, EPS_Z = 1e-5, 1e-6
E0, E1 = 8, 16
G0, G1 = E0 + 1, E1 + 1
PARTS = 3
RING = 4
OPEN = 4
WCOLS = 2 * KT * P + D

C_ID = 0
C_DCOL = C_ID + P
C_DROW = C_DCOL + SEQ // P
C_BD = C_DROW + SEQ
C_IOTA = C_BD + P
C_QC = C_IOTA + E1
C_KC = C_QC + SEQ
C_ROWS = C_KC + 4 * SEQ
C_EPS = C_ROWS + 4
N_CF = C_EPS + 1


def after(n):
    return n + 1


def prime(eng, sems):
    for s in sems:
        eng.sem_inc(s, 1)


def n_tiles(rows):
    return -(-rows // P)


def two_block_kernel(nc, x_in, cf_in, cb_in, a0_in, c0_in, r0_in, w0_in, a1_in, c1_in, r1_in, w1_in, out):
    NCH = x_in.shape[0] // CH
    NTOK = x_in.shape[0] // P
    NT = {0: w0_in.shape[0], 1: w1_in.shape[0]}
    HALVES = 2
    CPH = NCH // HALVES
    GR = {0: G0, 1: G1}
    NE = {0: E0, 1: E1}
    SEL0 = 3 * P
    SEL1 = SEL0 + NT[0] * P
    SELM = SEL1 + NT[1] * P
    N_CB = SELM + H * P + P

    with ExitStack() as ctx:
        def sb(name, shape, dt):
            return ctx.enter_context(nc.sbuf_tensor(name, shape, dt))

        def sem(name):
            return ctx.enter_context(nc.semaphore(name))

        PS = [ctx.enter_context(nc.psum_tensor(f"bank{b}", [P, 512], F32)) for b in range(8)]

        x = sb("x", [P, NTOK, D], F32)
        cf = sb("cf", [P, N_CF], F32)
        cb = sb("cb", [P, N_CB], BF16)
        a1 = sb("a1", [P, a1_in.shape[1]], F32)
        c1 = sb("c1", [P, 10], F32)
        r1 = sb("r1", [P, 256], F32)
        sT = sb("sT", [P, KT, NCH * CH], F32)
        gT = sb("gT", [P, KT, NCH * CH], F32)
        dT = sb("dT", [P, NCH * CH], BF16)

        ident = cf[:, C_ID:C_ID + P]
        identb = cb[:, 0:P]
        mask_q = cb[:, P:2 * P]
        mask_k = cb[:, 2 * P:3 * P]

        s_x = sem("x_landed")
        s_cst = sem("constants_landed")
        s_a1 = sem("block1_weights_landed")
        s_zero = sem("dT_cleared")
        ones_set = sem("ones_set")

        xn = sb("xn", [P, TPC, D], F32)
        xt = sb("xt", [P, KT, CH], F32)
        stats = sb("stats", [P, TPC, 6], F32)
        mv = sb("mv", [P, TPC, 2], F32)
        sd = sb("sd", [P, TPC], F32)
        rs = sb("rs", [P, TPC], F32)
        lg = sb("lg", [P, TPC, G1], F32)
        lmax = sb("lmax", [P, TPC, 1], F32)
        lsub = sb("lsub", [P, TPC, G1], F32)
        ex = sb("ex", [P, TPC, G1], F32)
        exs = sb("exs", [P, TPC, 1], F32)
        pr = sb("pr", [P, TPC, G1], F32)
        top = sb("top", [P, TPC, 8], F32)
        topi = sb("topi", [P, TPC, 8], U32)
        topf = sb("topf", [P, TPC, 2], F32)
        wsum = sb("wsum", [P, TPC, 1], F32)
        wtop = sb("wtop", [P, TPC, 2], F32)
        hot = sb("hot", [P, 2, TPC, E1], F32)
        dw = sb("dw", [P, TPC, G1], F32)
        dres = sb("dres", [P, TPC, G1], F32)
        dp = sb("dp", [P, TPC, 96], BF16)
        scratch = sb("scratch", [P, 1], F32)

        qf = sb("qf", [P, 2, CH], F32)
        mneg = sb("mneg", [P, 2, H], F32)
        m2 = sb("m2", [P, 2, 2 * H], BF16)
        mT = sb("mT", [2 * H, SEQ], BF16)
        mres = sb("mres", [P, 2, H], F32)
        orc = sb("orc", [P, 2, H, 1], F32)
        ring0 = sb("ring", [P, RING, WCOLS], F32)
        ring1 = ring0[:, :, 0:WCOLS // 2].bitcast(BF16)

        def moe_buffers(L, tb):
            return dict(
                wh=tb(f"wh{L}", [P, RING, WCOLS if L == 0 else D], F32R),
                wl=tb(f"wl{L}", [P, RING, WCOLS], F32R) if L == 0 else None,
                sg=tb(f"sg{L}", [P, 2, CH], F32),
                hf=tb(f"hf{L}", [P, 2, CH], F32),
                hh=tb(f"hh{L}", [P, 4, CH], F32R),
                hl=tb(f"hl{L}", [P, 4, CH], F32R))

        def scope(outer):
            inner = ExitStack()
            return inner, lambda name, shape, dt: inner.enter_context(nc.sbuf_tensor(name, shape, dt))[:]

        MB = {}
        block0, tb = scope(ctx)
        xh32 = tb("xh32", [P, KT, NCH * CH], F32R)
        xl32 = tb("xl32", [P, KT, NCH * CH], F32R)
        inner, tb = scope(block0)
        a0 = tb("a0", [P, a0_in.shape[1]], F32)
        c0 = tb("c0", [P, 4], F32)
        r0 = tb("r0", [P, 512], F32)
        qr = tb("qr", [P, 2, CH], F32)
        qT = tb("qT", [P, 2, CH], F32)
        kb = tb("kb", [P, TPC, D], F32)
        kn = tb("kn", [P, TPC, D], F32)
        vo = tb("vo", [P, TPC, 2, 2 * P], F32)
        kvm = tb("kvm", [P, 2, 2, 2 * P], F32)
        den = tb("den", [P, CH], F32)
        rden = tb("rden", [P, CH], F32)
        aT = tb("aT", [P, 2, CH], F32)
        inner.close()
        inner, tb = scope(block0)
        MB[0] = moe_buffers(0, tb)
        inner.close()
        block0.close()
        block1, tb = scope(ctx)
        xh16 = tb("xh16", [P, KT, NCH * CH], F16)
        xl16 = tb("xl16", [P, KT, NCH * CH], F16)
        gs = tb("gs", [P, 2, CH], F32)
        inner, tb = scope(block1)
        qz = tb("qz", [P, 4, 4, CH], F32)
        kk = tb("kk", [P, 4, CH], F32)
        v1 = tb("v1", [P, TPC, H, 2 * HD], F32)
        pe_ = tb("expscores", [P, 2, 2, 4, SEQ], F32)
        ot = xn
        ao = tb("ao", [P, 2, D], F32)
        aoT = tb("aoT", [P, 2, CH], F32)
        inner.close()
        inner, tb = scope(block1)
        MB[1] = moe_buffers(1, tb)
        inner.close()
        block1.close()
        if True:
            S = {}
            for L in (0, 1):
                for n in ("mv", "sd", "xn", "xt_ps", "xt_sb", "xlo", "lg_ps", "lg_read", "lsub", "ex",
                          "dp", "dt_ps", "dt_sb", "s_ps", "s_sb", "chunk_vec",
                          "wh_ready", "wl_ready", "g_ps", "u_ps", "r_ps", "silu",
                          "us", "h", "hh", "hl", "down", "y_ps", "y_read"):
                    S[n, L] = sem(f"{n}_{L}")
            landed = {L: [sem(f"tile_landed_{L}_{n}") for n in range(RING)] for L in (0, 1)}

            def wait_landed(eng, L, h, turn, t):
                slot = t % RING
                loads = NT[L] // RING + (slot < NT[L] % RING)
                eng.wait_ge(landed[L][slot], (h * loads + turn + t // RING + 1) * 16)

            q_ps, qr_sb, qT_ready = sem("q_ps"), sem("qr_sb"), sem("qT_ready")
            kv_ps, kv_sb, k_ready = sem("kv_ps"), sem("kv_sb"), sem("k_ready")
            kvm_ps, kvm_ready, nd_ps, aT_ready = sem("kvm_ps"), sem("kvm_ready"), sem("nd_ps"), sem("aT_ready")
            gs_ready, cb_ps = sem("gs_ready"), sem("cb_ps")
            qk_ps, qk_sb, qz_ready = sem("qk_ps"), sem("qk_sb"), sem("qz_ready")
            v_ps, v_sb = sem("v_ps"), sem("v_sb")
            sm_ps, sm_read, m2_ready = sem("scores_ps"), sem("scores_maxed"), sem("max_parts_ready")
            mt_ps, mt_sb, st_ps, exd = sem("maxT_ps"), sem("maxT_sb"), sem("scoresT_ps"), sem("exp_done")
            pv_ps, ot_sb, on_ps, ao_ready = sem("pv_ps"), sem("ot_sb"), sem("on_ps"), sem("ao_ready")
            at_ps, at_sb = sem("at_ps"), sem("at_sb")
            fgs, fcb, fx, s_out = sem("final_gs"), sem("final_ps"), sem("final_x"), sem("out_stored")

            block = ctx.enter_context(nc.Block())

            @block.sync
            def _(sp):
                sp.dma_start(cf[:], cf_in).then_inc(s_cst, 16)
                xv = x_in.rearrange("(t p) d -> p t d", p=P)
                for c in range(NCH):
                    sp.dma_start(x[:, c * TPC:(c + 1) * TPC, :], xv[:, c * TPC:(c + 1) * TPC, :]).then_inc(s_x, 16)
                    if c == 0:
                        sp.dma_start(a0, a0_in).then_inc(s_cst, 16)
                        sp.dma_start(c0, c0_in).then_inc(s_cst, 16)
                        sp.dma_start(r0, r0_in.partition_broadcast(P)).then_inc(s_cst, 16)
                        sp.dma_start(cb[:], cb_in).then_inc(s_cst, 16)
                sp.dma_start(a1[:], a1_in).then_inc(s_a1, 16)
                sp.dma_start(c1[:], c1_in).then_inc(s_a1, 16)
                sp.dma_start(r1[:], r1_in.partition_broadcast(P)).then_inc(s_a1, 16)

                def stream(L, w_in, ring, freed):
                    with sp.Fori(0, HALVES) as h:
                        for n in range(RING):
                            freed(h, 0)
                            sp.dma_start(ring[:, n, :], w_in[n]).then_inc(landed[L][n], 16)
                        with sp.Fori(0, NT[L] // RING - 1) as p:
                            for j in range(RING):
                                tile = sp.snap(p * RING + RING + j)
                                freed(h, p * RING + j + 1)
                                sp.dma_start(ring[:, j, :], w_in[ds(tile, 1)].rearrange("a p n -> (a p) n"))\
                                  .then_inc(landed[L][j], 16)
                        freed(h, NT[L] - RING)
                        sp.dma_start(ring[:, 0, :], w_in[NT[L] - 1]).then_inc(landed[L][0], 16)

                def freed0(h, m):
                    sp.wait_ge(S["wh_ready", 0], after(h * NT[0] + m))
                    sp.wait_ge(S["wl_ready", 0], after(h * NT[0] + m))

                def freed1(h, m):
                    sp.wait_ge(S["down", 1], after(h * (NT[1] * CPH + OPEN) + m * CPH + OPEN * (not isinstance(m, int) or m > 0)))

                stream(0, w0_in, ring0, freed0)
                sp.wait_ge(S["y_ps", 0], after(HALVES))
                stream(1, w1_in, ring1, freed1)
                with sp.Fori(0, NCH) as i:
                    token, tile = sp.snap(i * CH), sp.snap(i * TPC)
                    sp.wait_ge(fx, after(i * 2 + 2))
                    sp.dma_start(out[ds(token, CH), :].rearrange("(t p) d -> p t d", p=P),
                                 x[:, ds(tile, TPC), :]).then_inc(s_out, 16)
                sp.wait_ge(s_out, 16 * NCH)

            @block.gpsimd
            def _(pool):
                pool.memset(dT[:], 0.0).then_inc(s_zero, 1)
                pool.memset(dp[:], 0.0).then_inc(s_zero, 1)
                pool.memset(vo[:, :, :, P:2 * P], 1.0).then_inc(ones_set, 1)

            @block.tensor
            def _(pe):
                prime(pe, [S[n, L] for L in (0, 1) for n in
                           ("xt_ps", "lg_ps", "dt_ps", "s_ps", "g_ps", "u_ps", "r_ps", "down", "y_ps")]
                      + [q_ps, kv_ps, kvm_ps, nd_ps, cb_ps, qk_ps, v_ps, sm_ps, mt_ps, st_ps, pv_ps, on_ps,
                         at_ps, fcb])
                pe.wait_ge(s_cst, 80)

                def front(L, i, a, rcol):
                    pe.wait_ge(S["s_sb", L], after(2 * i))
                    pe.wait_ge(S["xn", L], after(4 * i + 4))
                    for k in range(KT):
                        for t in range(TPC):
                            mm = pe.transpose(PS[k][:, t * P:(t + 1) * P], xn[:, t, k * P:(k + 1) * P], ident)
                        mm.then_inc(S["xt_ps", L], 1)
                    pe.wait_ge(S["xt_sb", L], after(2 * i + 2))
                    pe.wait_ge(S["lg_read", L], after(i))
                    n = GR[0] if L == 0 else NE[1]
                    for t in range(TPC):
                        for k in range(KT):
                            mm = pe.matmul(PS[2][:, t * 32:t * 32 + n], xt[:, k, t * P:(t + 1) * P],
                                           a[:, rcol + k * n:rcol + (k + 1) * n],
                                           start=(t == 0 and k == 0), stop=(k == 1), skip_group_check=True)
                    mm.then_inc(S["lg_ps", L], 1)

                def routing_transposes(L, i):
                    pe.wait_ge(S["dp", L], after(i + 1))
                    if L == 0:
                        pe.wait_ge(S["dt_sb", L], after(i))
                    n = PARTS * GR[L]
                    dst = PS[3][:].bitcast(BF16)
                    if L == 1:
                        n = 96
                    for t in range(TPC):
                        mm = pe.transpose(dst[0:n, t * P:(t + 1) * P], dp[:, t, 0:n], identb)
                    mm.then_inc(S["dt_ps", L], 1)

                def moe(L):
                    n_items = NT[L] * CPH
                    xs = (xh32, xl32) if L == 0 else (xh16, xl16)
                    wh, wl, hh, hl = (MB[L][n] for n in ("wh", "wl", "hh", "hl"))
                    down0 = 2 * KT * P if L == 0 else 0

                    def gates(h, base, k, turn):
                        slot, c = (k // CPH) % RING, k % CPH
                        g, u, r = (PS[(3 * k + n) % 4] for n in range(3))
                        tok = ds(h * (CPH * CH) + c * CH, CH)
                        tile_reg = turn * RING + k // CPH
                        if c == 0:
                            if L == 0:
                                pe.wait_ge(S["wh_ready", L], after(h * NT[L] + tile_reg + 1))
                                pe.wait_ge(S["wl_ready", L], after(h * NT[L] + tile_reg + 1))
                            else:
                                wait_landed(pe, L, h, turn, k // CPH)
                        for out_, col, ready in ((g, 0, S["g_ps", L]), (u, KT * P, S["u_ps", L])):
                            if out_ is g:
                                if k >= 2:
                                    pe.wait_ge(S["h", L], after(h * n_items + base + k - 1))
                            elif k >= 1:
                                pe.wait_ge(S["silu", L], after(h * n_items + base + k))
                            first = True
                            for kt in range(KT):
                                cols = slice(col + kt * P, col + (kt + 1) * P)
                                if L == 0:
                                    terms = ((wh[:, slot, cols], xs[0]), (wh[:, slot, cols], xs[1]),
                                             (wl[:, slot, cols], xs[0]))
                                else:
                                    terms = ((ring1[:, slot, cols], xs[0]), (ring1[:, slot, cols], xs[1]))
                                for n, (w, xx) in enumerate(terms):
                                    mm = pe.matmul(out_[:], w, xx[:, kt, tok], start=first,
                                                   stop=(kt == KT - 1 and n == len(terms) - 1))
                                    first = False
                            mm.then_inc(ready, 1)
                        if k >= 1:
                            pe.wait_ge(S["us", L], after(h * n_items + base + k))
                        s0 = SEL0 if L == 0 else SEL1
                        pe.matmul(r[:], cb[:, ds(s0 + tile_reg * P, P)], dT[:, tok], start=True,
                                  stop=True).then_inc(S["r_ps", L], 1)

                    def down(h, base, tile, k):
                        slot, c = (k // CPH) % RING, k % CPH
                        pe.wait_ge(S["hl", L], after(h * n_items + base + k + 1))
                        if L == 1:
                            pe.wait_ge(S["wh_ready", L], after(h * NT[L] + tile + k // CPH + 1))
                        for d in range(D // P):
                            cols = slice(down0 + d * P, down0 + (d + 1) * P)
                            terms = [(wh, hh), (wh, hl)] + ([(wl, hh)] if L == 0 else [])
                            for w, a in terms:
                                mm = pe.matmul(PS[4 + 2 * c + d][:], w[:, slot, cols], a[:, k % 4, :],
                                               start=False, stop=False, skip_group_check=True)
                        mm.then_inc(S["down", L], 1)
                        return mm

                    body = RING * CPH
                    with pe.Fori(0, HALVES) as h:
                        pe.wait_ge(S["y_read", L], after(h * 4))
                        for b in range(4):
                            pe.matmul(PS[4 + b][:], zcol, dT[:, 0:CH], start=True, stop=False,
                                      skip_group_check=True).then_inc(S["down", L], 1)
                        pe.wait_ge(S["h", L], after(h * n_items))
                        gates(h, 0, 0, 0)
                        gates(h, 0, 1, 0)
                        with pe.Fori(0, NT[L] // RING) as p:
                            for k in range(body):
                                gates(h, p * body, k + 2, p)
                                down(h, p * body, p * RING, k)
                        for k in range(NT[L] // RING * body, n_items):
                            mm = down(h, 0, 0, k)
                        pe.matmul(PS[7][:], zcol, dT[:, 0:CH], start=False, stop=True,
                                  skip_group_check=True).then_inc(S["y_ps", L], 1)

                pe.wait_ge(s_zero, 2)
                zcol = cb[:, SELM + H * P:SELM + H * P + P]

                with pe.Fori(0, NCH) as i:
                    front(0, i, a0, 2048)
                    for m in range(2):
                        for k in range(KT):
                            mm = pe.matmul(PS[4 + m][:], a0[:, k * D + m * P:k * D + (m + 1) * P], xt[:, k, :],
                                           start=(k == 0), stop=(k == 1))
                        mm.then_inc(q_ps, 1)
                    for t in range(TPC):
                        if t >= 2:
                            pe.wait_ge(kv_sb, after(i * TPC + t - 1))
                        for k in range(KT):
                            mm = pe.matmul(PS[6 + t % 2][:], xt[:, k, t * P:(t + 1) * P],
                                           a0[:, 512 + k * 512:512 + (k + 1) * 512], start=(k == 0), stop=(k == 1))
                        mm.then_inc(kv_ps, 1)
                    pe.wait_ge(ones_set, 1)
                    for b in range(2):
                        pe.wait_ge(k_ready, after(i * TPC + 2 * b + 2))
                        pe.wait_ge(kv_sb, after(i * TPC + 2 * b + 2))
                        for m in range(2):
                            for t in range(2):
                                mm = pe.matmul(PS[b][:, m * 256:(m + 1) * 256], kn[:, 2 * b + t, m * P:(m + 1) * P],
                                               vo[:, 2 * b + t, m, :], start=(m == 0 and t == 0), stop=(t == 1),
                                               skip_group_check=True)
                        mm.then_inc(kvm_ps, 1)
                    pe.wait_ge(kvm_ready, after(2 * i + 2))
                    pe.wait_ge(qT_ready, after(2 * i + 2))
                    for m in range(2):
                        for n in range(2):
                            for b in range(2):
                                mm = pe.matmul(PS[4 + 2 * m + n][:, b * SEQ:(b + 1) * SEQ],
                                               kvm[:, b, m, n * P:(n + 1) * P], qT[:, m, b * SEQ:(b + 1) * SEQ],
                                               start=(b == 0), stop=True, skip_group_check=True)
                        mm.then_inc(nd_ps, 1)
                    routing_transposes(0, i)
                    pe.wait_ge(aT_ready, after(2 * i + 2))
                    for d in range(2):
                        for m in range(2):
                            mm = pe.matmul(PS[d][:], a0[:, 1536 + m * D + d * P:1536 + m * D + (d + 1) * P],
                                           aT[:, m, :], start=(m == 0), stop=(m == 1))
                        mm.then_inc(S["s_ps", 0], 1)
                pe.wait_ge(S["s_sb", 0], after(2 * NCH))
                pe.wait_ge(S["dt_sb", 0], after(NCH))
                pe.wait_ge(S["xlo", 0], after(NCH))
                moe(0)

                pe.wait_ge(s_a1, 48)
                pe.wait_ge(S["y_read", 0], after(4 * HALVES))
                with pe.Fori(0, NCH) as i:
                    pe.wait_ge(gs_ready, after(i + 1))
                    pe.wait_ge(ot_sb, after(4 * i))
                    for t in range(TPC):
                        for d in range(2):
                            mm = pe.transpose(PS[4 + t // 2][:, (t % 2) * D + d * P:(t % 2) * D + (d + 1) * P],
                                              gs[:, d, t * P:(t + 1) * P], ident)
                        if t % 2:
                            mm.then_inc(cb_ps, 1)
                    front(1, i, a1, 3072)
                    for mt in range(8):
                        if mt >= 2:
                            pe.wait_ge(qk_sb, after(8 * i + mt - 1))
                        for k in range(KT):
                            w0_ = (mt // 4) * 1024 + k * 512 + (mt % 4) * P
                            mm = pe.matmul(PS[6 + mt % 2][:], a1[:, w0_:w0_ + P], xt[:, k, :],
                                           start=(k == 0), stop=(k == 1))
                        mm.then_inc(qk_ps, 1)
                    for t in range(TPC):
                        for k in range(KT):
                            mm = pe.matmul(PS[4 + t // 2][:, (t % 2) * D:(t % 2 + 1) * D], xt[:, k, t * P:(t + 1) * P],
                                           a1[:, 2048 + k * D:2048 + (k + 1) * D],
                                           start=(k == 0 and t % 2 == 0), stop=(k == 1), skip_group_check=True)
                        if t % 2:
                            mm.then_inc(v_ps, 1)
                    routing_transposes(1, i)
                    pe.wait_ge(qz_ready, after(4 * i + 4))
                    pe.wait_ge(qk_sb, after(8 * i + 8))
                    pe.wait_ge(S["dt_sb", 1], after(i + 1))
                    pe.wait_ge(ones_set, 2)
                    for b in range(2):
                        bb = 2 * i + b
                        if b == 1:
                            pe.wait_ge(exd, after(8 * bb))
                        for U in range(8):
                            qt, g = U // 4, U % 4
                            if U >= 2:
                                pe.wait_ge(sm_read, after(8 * bb + U - 1))
                            nk = (qt + 1) * P
                            for j in range(4):
                                bank = PS[2 * (U % 2) + j // 2]
                                pe.matmul(bank[:, (j % 2) * 256:(j % 2) * 256 + nk],
                                          qz[:, g, j, b * SEQ + qt * P:b * SEQ + (qt + 1) * P],
                                          kk[:, g, b * SEQ:b * SEQ + nk], start=(j % 2 == 0), stop=False,
                                          skip_group_check=True)
                                if j % 2:
                                    mm = pe.matmul(bank[:].rearrange("p (j n) -> p j n", j=2)[:, :, qt * P:(qt + 1) * P],
                                                   identb, mask_q.unsqueeze(1).to_broadcast([P, 2, P]),
                                                   start=False, stop=True, skip_group_check=True)
                            mm.then_inc(sm_ps, 1)
                        pe.wait_ge(m2_ready, after(bb + 1))
                        mb_ = PS[6][:].bitcast(BF16)
                        if b == 1:
                            pe.wait_ge(ao_ready, after(2 * bb))
                        for qt in range(2):
                            mm = pe.transpose(mb_[0:2 * H, qt * P:(qt + 1) * P], m2[:, qt, :], identb)
                        mm.then_inc(mt_ps, 1)
                        pe.wait_ge(mt_sb, after(bb + 1))

                        def weighted_values(g):
                            pe.wait_ge(exd, after(8 * bb + 2 * g + 2))
                            pe.wait_ge(v_sb, after(2 * i + 2))
                            if b == 1 and g == 0:
                                pe.wait_ge(at_sb, after(bb))
                            for j in range(4):
                                o_ = PS[4 + g // 2][32 * j:32 * j + 32, (g % 2) * 256:(g % 2) * 256 + 256]
                                pe.matmul(o_, v1[:, 2 * b, 4 * g + j, :], pe_[:, g % 2, 0, j, :],
                                          start=(g % 2 == 0), stop=False, skip_group_check=True)
                                mm = pe.matmul(o_[:, P:2 * P], v1[:, 2 * b + 1, 4 * g + j, :],
                                               pe_[:, g % 2, 1, j, P:2 * P], start=False, stop=True,
                                               skip_group_check=True)
                            mm.then_inc(pv_ps, 1)

                        for V in range(8):
                            g, kt = V // 2, V % 2
                            if V >= 2:
                                pe.wait_ge(exd, after(8 * bb + V - 1))
                            q0 = kt * P
                            for j in range(4):
                                bank = PS[2 * (V % 2) + j // 2]
                                o_ = bank[:, (j % 2) * 256 + q0:(j % 2) * 256 + 256]
                                pe.matmul(o_, kk[:, g, b * SEQ + kt * P:b * SEQ + (kt + 1) * P],
                                          qz[:, g, j, b * SEQ + q0:(b + 1) * SEQ], start=(j % 2 == 0), stop=False,
                                          skip_group_check=True)
                                sm0 = SELM + (4 * g + j) * P
                                pe.matmul(o_, cb[0:2 * H, sm0:sm0 + P], mT[:, q0:SEQ], start=False, stop=False,
                                          skip_group_check=True)
                                if j % 2:
                                    mm = pe.matmul(bank[:].rearrange("p (j n) -> p j n", j=2)[:, :, q0:q0 + P],
                                                   identb, mask_k.unsqueeze(1).to_broadcast([P, 2, P]),
                                                   start=False, stop=True, skip_group_check=True)
                            mm.then_inc(st_ps, 1)
                            if V % 2 and g >= 1:
                                weighted_values(g - 1)
                        weighted_values(3)
                        pe.wait_ge(ot_sb, after(2 * bb + 2))
                        for qt in range(2):
                            for g in range(4):
                                mm = pe.transpose(PS[6 + qt][:, g * P:(g + 1) * P], ot[:, g, qt * P:(qt + 1) * P], ident)
                            mm.then_inc(on_ps, 1)
                        pe.wait_ge(ao_ready, after(2 * bb + 2))
                        for qt in range(2):
                            for m in range(2):
                                mm = pe.transpose(PS[4][:, (m * 2 + qt) * P:(m * 2 + qt + 1) * P],
                                                  ao[:, qt, m * P:(m + 1) * P], ident)
                        mm.then_inc(at_ps, 1)
                    pe.wait_ge(at_sb, after(2 * i + 2))
                    for d in range(2):
                        for m in range(2):
                            mm = pe.matmul(PS[d][:], a1[:, 2560 + m * D + d * P:2560 + m * D + (d + 1) * P],
                                           aoT[:, m, :], start=(m == 0), stop=(m == 1))
                        mm.then_inc(S["s_ps", 1], 1)
                pe.wait_ge(S["s_sb", 1], after(2 * NCH))
                pe.wait_ge(S["xlo", 1], after(NCH))
                moe(1)
                pe.wait_ge(S["y_read", 1], after(4 * HALVES))
                with pe.Fori(0, NCH) as i:
                    pe.wait_ge(fgs, after(i + 1))
                    pe.wait_ge(fx, after(2 * i))
                    for t in range(TPC):
                        for d in range(2):
                            mm = pe.transpose(PS[4 + t // 2][:, (t % 2) * D + d * P:(t % 2) * D + (d + 1) * P],
                                              gs[:, d, t * P:(t + 1) * P], ident)
                        if t % 2:
                            mm.then_inc(fcb, 1)

            @block.scalar
            def _(act):
                prime(act, [S[n, L] for L in (0, 1) for n in
                            ("sd", "xt_sb", "ex", "s_sb", "wh_ready", "silu", "hh", "y_read")]
                      + [qr_sb, k_ready, exd, ot_sb, at_sb])
                act.wait_ge(s_cst, 80)
                eps_ln = cf[:, C_EPS:C_EPS + 1]

                def front(L, i):
                    act.wait_ge(S["mv", L], after(i + 1))
                    act.activation(sd[:], mv[:, :, 1], ACT.Sqrt, bias=eps_ln).then_inc(S["sd", L], 1)
                    act.wait_ge(S["xlo", L], after(i))
                    if L == 0:
                        act.wait_ge(kv_ps, after(TPC * i))
                    else:
                        act.wait_ge(v_ps, after(2 * i))
                    for k in range(KT):
                        act.wait_ge(S["xt_ps", L], after(2 * i + k + 1))
                        act.activation(xt[:, k, :], PS[k][:], ACT.Copy).then_inc(S["xt_sb", L], 1)
                    act.wait_ge(S["lsub", L], after(i + 1))
                    if L == 0:
                        act.activation(ex[:, :, 0:E0], lsub[:, :, 0:E0], ACT.Exp)
                        act.activation(ex[:, :, E0:G0], lg[:, :, E0:G0], ACT.Exp, scale=-1.0).then_inc(S["ex", L], 1)
                    else:
                        act.activation(ex[:, :, 0:E1], lg[:, :, 0:E1], ACT.Exp, scale=-1.0).then_inc(S["ex", L], 1)

                def moe(L):
                    n_items = NT[L] * CPH
                    w0c = 0 if L == 0 else 2 * KT * P
                    wh, sg, hf, hh = (MB[L][n] for n in ("wh", "sg", "hf", "hh"))

                    def split(h, turn, n):
                        slot = n % RING
                        wait_landed(act, L, h, turn, n)
                        src = ring0 if L == 0 else ring1
                        act.activation(wh[:, slot, :], src[:, slot, w0c:WCOLS], ACT.Copy).then_inc(S["wh_ready", L], 1)

                    def silu(h, base, k):
                        act.wait_ge(S["g_ps", L], after(h * n_items + base + k + 1))
                        act.activation(sg[:, k % 2, :], PS[(3 * k) % 4][:], ACT.Silu).then_inc(S["silu", L], 1)

                    def high_part(h, base, k):
                        act.wait_ge(S["h", L], after(h * n_items + base + k + 1))
                        act.wait_ge(S["down", L], after(h * (n_items + OPEN) + OPEN + base + k - 3))
                        act.activation(hh[:, k % 4, :], hf[:, k % 2, :], ACT.Copy).then_inc(S["hh", L], 1)

                    body = RING * CPH
                    with act.Fori(0, HALVES) as h:
                        act.wait_ge(S["down", L], after(h * (n_items + OPEN)))
                        split(h, 0, 0)
                        silu(h, 0, 0)
                        with act.Fori(0, NT[L] // RING) as p:
                            for j in range(RING):
                                act.wait_ge(S["down", L], after(h * (n_items + OPEN) + OPEN + p * body + (j - 2) * CPH))
                                split(h, p, j + 1)
                                for k in range(j * CPH, (j + 1) * CPH):
                                    silu(h, p * body, k + 1)
                                    high_part(h, p * body, k)
                        for k in range(NT[L] // RING * body, n_items):
                            if k + 1 < n_items:
                                silu(h, 0, k + 1)
                            high_part(h, 0, k)
                        act.wait_ge(S["y_ps", L], after(h + 1))
                        for c in range(CPH):
                            for d in range(2):
                                act.activation(gT[:, d, ds(h * (CPH * CH) + c * CH, CH)], PS[4 + 2 * c + d][:],
                                               ACT.Silu).then_inc(S["y_read", L], 1)

                with act.Fori(0, NCH) as i:
                    front(0, i)
                    for m in range(2):
                        act.wait_ge(q_ps, after(2 * i + m + 1))
                        act.wait_ge(qT_ready, after(2 * i))
                        act.activation(qr[:, m, :], PS[4 + m][:], ACT.Relu, bias=c0[:, m:m + 1]).then_inc(qr_sb, 1)
                    act.wait_ge(kvm_ps, after(2 * i))
                    for t in range(TPC):
                        act.wait_ge(kv_sb, after(TPC * i + t + 1))
                        act.activation(kn[:, t, :], kb[:, t, :], ACT.Relu,
                                       scale=cf[:, C_DCOL + t % 2:C_DCOL + t % 2 + 1]).then_inc(k_ready, 1)
                    for d in range(2):
                        act.wait_ge(S["s_ps", 0], after(2 * i + d + 1))
                        act.activation(sT[:, d, ds(i * CH, CH)], PS[d][:], ACT.Identity,
                                       bias=c0[:, 2 + d:3 + d]).then_inc(S["s_sb", 0], 1)
                act.wait_ge(nd_ps, after(2 * NCH))
                act.wait_ge(aT_ready, after(2 * NCH))
                moe(0)

                act.wait_ge(s_a1, 48)
                with act.Fori(0, NCH) as i:
                    front(1, i)
                    for b in range(2):
                        bb = 2 * i + b
                        for V in range(8):
                            g, kt = V // 2, V % 2
                            q0 = kt * P
                            act.wait_ge(st_ps, after(8 * bb + V + 1))
                            if g >= 2:
                                act.wait_ge(pv_ps, after(4 * bb + g - 1))
                            else:
                                act.wait_ge(pv_ps, after(4 * bb))
                            for n in range(2):
                                ins = act.activation(pe_[:, g % 2, kt, 2 * n:2 * n + 2, q0:SEQ],
                                                     PS[2 * (V % 2) + n][:].rearrange("p (j n) -> p j n", j=2)[:, :, q0:SEQ],
                                                     ACT.Exp, scale=1.0 / HD)
                            ins.then_inc(exd, 1)
                        for n in range(2):
                            act.wait_ge(pv_ps, after(4 * bb + 2 * n + 2))
                            if n == 0:
                                act.wait_ge(on_ps, after(2 * bb))
                            act.activation(ot[:, 2 * n:2 * n + 2, :], PS[4 + n][:].rearrange("p (g n) -> p g n", g=2),
                                           ACT.Copy).then_inc(ot_sb, 1)
                        act.wait_ge(at_ps, after(bb + 1))
                        if b == 0:
                            act.wait_ge(S["s_ps", 1], after(2 * i))
                        act.activation(aoT[:, :, b * SEQ:(b + 1) * SEQ], PS[4][:].rearrange("p (m n) -> p m n", m=2),
                                       ACT.Copy).then_inc(at_sb, 1)
                    for d in range(2):
                        act.wait_ge(S["s_ps", 1], after(2 * i + d + 1))
                        act.wait_ge(gs_ready, after(i + 1))
                        act.activation(sT[:, d, ds(i * CH, CH)], PS[d][:], ACT.Identity,
                                       bias=c1[:, 8 + d:9 + d]).then_inc(S["s_sb", 1], 1)
                moe(1)

            @block.vector
            def _(dve):
                prime(dve, [S[n, L] for L in (0, 1) for n in
                            ("mv", "xn", "xlo", "lg_read", "lsub", "dp", "dt_sb", "chunk_vec", "wl_ready",
                             "us", "h", "hl")]
                      + [qT_ready, kv_sb, kvm_ready, aT_ready, gs_ready, qk_sb, qz_ready, v_sb, sm_read,
                         m2_ready, mt_sb, ao_ready, fgs, fx])
                dve.wait_ge(s_cst, 80)
                dve.wait_ge(s_zero, 2)

                def hold():
                    dve.memset(scratch[:], 0.0)

                class Steps:

                    def __init__(self, sem_, base):
                        self.sem, self.base, self.n = sem_, base, 0

                    def __call__(self, ins):
                        self.n += 1
                        ins.then_inc(self.sem, 1)
                        dve.wait_ge(self.sem, after(self.base + self.n))

                STEPS = {0: 19 + 0, 1: 0}

                def front(L, i, step):
                    hold()
                    for t in range(TPC):
                        ins = dve.bn_stats(stats[:, t, :], x[:, ds(i * TPC + t, 1), :].rearrange("p a d -> p (a d)"))
                    step(ins)
                    dve.wait_ge(S["sd", L], after(i))
                    hold()
                    for t in range(TPC):
                        ins = dve.bn_aggr(mv[:, t, :], stats[:, t, :])
                    ins.then_inc(S["mv", L], 1)
                    dve.wait_ge(S["sd", L], after(i + 1))
                    step(dve.reciprocal(rs[:], sd[:]))
                    dve.wait_ge(S["xt_ps", L], after(2 * i))
                    for t in range(TPC):
                        dve.tensor_scalar(xn[:, t, :], x[:, ds(i * TPC + t, 1), :].rearrange("p a d -> p (a d)"),
                                          mv[:, t, 0:1], rs[:, t:t + 1], ALU.subtract, ALU.mult).then_inc(S["xn", L], 1)
                    hi, lo = (xh32, xl32) if L == 0 else (xh16, xl16)
                    dve.wait_ge(S["xt_sb", L], after(2 * i + 2))
                    step(dve.tensor_copy(hi[:, :, ds(i * CH, CH)], xt[:]))
                    hv = hi[:, :, ds(i * CH, CH)]
                    if L == 0:
                        hv = xh32f[:, :, ds(i * CH, CH)]
                    dve.tensor_tensor(lo[:, :, ds(i * CH, CH)], xt[:], hv, ALU.subtract).then_inc(S["xlo", L], 1)
                    n = G0 if L == 0 else E1
                    dve.wait_ge(S["lg_ps", L], after(i + 1))
                    dve.wait_ge(S["ex", L], after(i))
                    dve.tensor_copy(lg[:, :, 0:n], PS[2][:, 0:TPC * 32].rearrange("p (t n) -> p t n", t=TPC)[:, :, 0:n])\
                       .then_inc(S["lg_read", L], 1)
                    dve.wait_ge(S["lg_read", L], after(i + 1))
                    if L == 0:
                        step(dve.tensor_reduce(lmax[:, :, 0], lg[:, :, 0:E0], AX.X, ALU.max))
                        dve.tensor_tensor(lsub[:, :, 0:E0], lg[:, :, 0:E0], lmax[:].to_broadcast([P, TPC, E0]),
                                          ALU.subtract).then_inc(S["lsub", L], 1)
                    else:
                        dve.tensor_copy(lsub[:, 0, 0:1], lg[:, 0, 0:1]).then_inc(S["lsub", L], 1)

                def routing(L, i, step):
                    e, n = NE[L], GR[L]
                    dve.wait_ge(S["ex", L], after(i + 1))
                    if L == 0:
                        step(dve.tensor_reduce(exs[:, :, 0], ex[:, :, 0:E0], AX.X, ALU.add))
                        step(dve.reciprocal(wsum[:], exs[:]))
                        step(dve.tensor_tensor(pr[:, :, 0:E0], ex[:, :, 0:E0], wsum[:].to_broadcast([P, TPC, E0]), ALU.mult))
                        step(dve.tensor_scalar(ex[:, :, E0:G0], ex[:, :, E0:G0], 1.0, None, ALU.add))
                        step(dve.reciprocal(dw[:, :, E0:G0], ex[:, :, E0:G0]))
                    else:
                        step(dve.tensor_scalar(ex[:, :, 0:E1], ex[:, :, 0:E1], 1.0, None, ALU.add))
                        step(dve.reciprocal(pr[:, :, 0:E1], ex[:, :, 0:E1]))
                    hold()
                    for t in range(TPC):
                        ins = dve.max(top[:, t, :], pr[:, t, 0:e])
                    step(ins)
                    hold()
                    for t in range(TPC):
                        ins = dve.max_index(topi[:, t, :], top[:, t, :], pr[:, t, 0:e])
                    step(ins)
                    step(dve.tensor_copy(topf[:], topi[:, :, 0:2]))
                    step(dve.tensor_tensor(exs[:], top[:, :, 0:1], top[:, :, 1:2], ALU.add))
                    step(dve.reciprocal(wsum[:], exs[:]))
                    step(dve.tensor_tensor(wtop[:], top[:, :, 0:2], wsum[:].to_broadcast([P, TPC, 2]), ALU.mult))
                    for r in range(2):
                        for t in range(TPC):
                            ins = dve.tensor_scalar(hot[:, r, t, 0:e], cf[:, C_IOTA:C_IOTA + e], topf[:, t, r:r + 1],
                                                    wtop[:, t, r:r + 1], ALU.is_equal, ALU.mult)
                    step(ins)
                    step(dve.tensor_tensor(dw[:, :, 0:e], hot[:, 0, :, 0:e], hot[:, 1, :, 0:e], ALU.add))
                    if L == 1:
                        step(dve.memset(dw[:, :, e:n], 1.0))
                    dve.wait_ge(S["dt_ps", L], after(i))
                    step(dve.tensor_copy(dp[:, :, 0:n], dw[:, :, 0:n]))
                    step(dve.tensor_tensor(dres[:, :, 0:n], dw[:, :, 0:n], dp[:, :, 0:n], ALU.subtract))
                    step(dve.tensor_copy(dp[:, :, n:2 * n], dres[:, :, 0:n]))
                    dve.tensor_tensor(dp[:, :, 2 * n:3 * n], dres[:, :, 0:n], dp[:, :, n:2 * n], ALU.subtract)\
                       .then_inc(S["dp", L], 1)

                def routing_out(L, i):
                    dve.wait_ge(S["dt_ps", L], after(i + 1))
                    n = PARTS * GR[L]
                    dve.tensor_copy(dT[0:n, ds(i * CH, CH)], PS[3][:].bitcast(BF16)[0:n, 0:CH]).then_inc(S["dt_sb", L], 1)

                def moe(L):
                    n_items = NT[L] * CPH
                    wl, sg, hf, hl = (MB[L][n] for n in ("wl", "sg", "hf", "hl"))
                    whf, hhf = MB[L]["wh"].bitcast(F32), MB[L]["hh"].bitcast(F32)

                    def split(h, turn, n):
                        slot = n % RING
                        wait_landed(dve, L, h, turn, n)
                        dve.wait_ge(S["wh_ready", L], after(h * NT[L] + turn * RING + n + 1))
                        dve.tensor_tensor(wl[:, slot, :], ring0[:, slot, :], whf[:, slot, :], ALU.subtract)\
                           .then_inc(S["wl_ready", L], 1)

                    def product(h, base, k):
                        it = h * n_items + base + k
                        dve.wait_ge(S["hl", L], after(it - 1) if k else after(h * n_items))
                        dve.wait_ge(S["silu", L], after(it + 1))
                        dve.wait_ge(S["u_ps", L], after(it + 1))
                        dve.tensor_tensor(hf[:, k % 2, :], PS[(3 * k + 1) % 4][:], sg[:, k % 2, :], ALU.mult)\
                           .then_inc(S["us", L], 1)
                        dve.wait_ge(S["us", L], after(it + 1))
                        dve.wait_ge(S["r_ps", L], after(it + 1))
                        dve.tensor_tensor(hf[:, k % 2, :], PS[(3 * k + 2) % 4][:], hf[:, k % 2, :], ALU.mult)\
                           .then_inc(S["h", L], 1)

                    def low_part(h, base, k):
                        it = h * n_items + base + k
                        dve.wait_ge(S["down", L], after(h * (n_items + OPEN) + OPEN + base + k - 3))
                        dve.wait_ge(S["hh", L], after(it + 1))
                        dve.tensor_tensor(hl[:, k % 4, :], hf[:, k % 2, :], hhf[:, k % 4, :], ALU.subtract)\
                           .then_inc(S["hl", L], 1)

                    body = RING * CPH
                    with dve.Fori(0, HALVES) as h:
                        if L == 0:
                            dve.wait_ge(S["down", L], after(h * (n_items + OPEN)))
                            split(h, 0, 0)
                        product(h, 0, 0)
                        with dve.Fori(0, NT[L] // RING) as p:
                            for j in range(RING):
                                if L == 0:
                                    split(h, p, j + 1)
                                for k in range(j * CPH, (j + 1) * CPH):
                                    product(h, p * body, k + 1)
                                    low_part(h, p * body, k)
                        for k in range(NT[L] // RING * body, n_items):
                            if k + 1 < n_items:
                                product(h, 0, k + 1)
                            low_part(h, 0, k)

                xh32f = xh32.bitcast(F32)

                dve.wait_ge(s_x, 16 * NCH)
                with dve.Fori(0, NCH) as i:
                    step = Steps(S["chunk_vec", 0], i * N_STEPS[0])
                    front(0, i, step)
                    dve.wait_ge(k_ready, after(TPC * i))
                    dve.wait_ge(kvm_ps, after(2 * i))
                    dve.wait_ge(nd_ps, after(2 * i))
                    for m in range(2):
                        dve.wait_ge(qr_sb, after(2 * i + m + 1))
                        dve.tensor_tensor(qT[:, m, :].rearrange("p (b n) -> p b n", b=2),
                                          qr[:, m, :].rearrange("p (b n) -> p b n", b=2),
                                          cf[:, C_DROW:C_DROW + SEQ].unsqueeze(1).to_broadcast([P, 2, SEQ]),
                                          ALU.mult).then_inc(qT_ready, 1)
                    for t in range(TPC):
                        dve.wait_ge(kv_ps, after(TPC * i + t + 1))
                        dve.tensor_tensor(kb[:, t, :], PS[6 + t % 2][:, 0:D], r0[:, 0:D], ALU.add)
                        dve.tensor_tensor(vo[:, t, :, 0:P], PS[6 + t % 2][:, D:2 * D].rearrange("p (m n) -> p m n", m=2),
                                          r0[:, D:2 * D].rearrange("p (m n) -> p m n", m=2), ALU.add).then_inc(kv_sb, 1)
                    routing(0, i, step)
                    bd = cf[:, C_BD:C_BD + P].unsqueeze(1).to_broadcast([P, 4, P])
                    for b in range(2):
                        dve.wait_ge(kvm_ps, after(2 * i + b + 1))
                        dve.tensor_tensor(kvm[:, b, :, :].rearrange("p m (s n) -> p (m s) n", s=2),
                                          PS[b][:].rearrange("p (s n) -> p s n", s=4), bd, ALU.mult).then_inc(kvm_ready, 1)
                    dve.wait_ge(S["s_ps", 0], after(2 * i))
                    for m in range(2):
                        dve.wait_ge(nd_ps, after(2 * i + m + 1))
                        step(dve.tensor_scalar(den[:], PS[5 + 2 * m][:], EPS_Z, None, ALU.add))
                        step(dve.reciprocal(rden[:], den[:]))
                        dve.tensor_tensor(aT[:, m, :], PS[4 + 2 * m][:], rden[:], ALU.mult).then_inc(aT_ready, 1)
                    routing_out(0, i)
                    assert step.n == N_STEPS[0], step.n
                dve.wait_ge(S["s_ps", 0], after(2 * NCH))
                moe(0)

                dve.wait_ge(s_a1, 48)
                dve.wait_ge(S["y_ps", 0], after(HALVES))
                dve.memset(v1[:, :, :, HD:2 * HD], 1.0).then_inc(ones_set, 1)
                with dve.Fori(0, NCH) as i:
                    step = Steps(S["chunk_vec", 1], i * N_STEPS[1])
                    dve.wait_ge(S["y_read", 0], after(4 * HALVES))
                    dve.wait_ge(cb_ps, after(2 * i))
                    dve.tensor_tensor(gs[:], sT[:, :, ds(i * CH, CH)], gT[:, :, ds(i * CH, CH)], ALU.mult).then_inc(gs_ready, 1)
                    for n in range(2):
                        dve.wait_ge(cb_ps, after(2 * i + n + 1))
                        xx = x[:, ds(i * TPC + 2 * n, 2), :]
                        ins = dve.tensor_tensor(xx, xx, PS[4 + n][:].rearrange("p (t d) -> p t d", t=2), ALU.add)
                        step(ins)
                    front(1, i, step)
                    for mt in range(8):
                        dve.wait_ge(qk_ps, after(8 * i + mt + 1))
                        src = PS[6 + mt % 2][:].rearrange("p (b n) -> p b n", b=2)
                        if mt < 4:
                            c_ = cf[:, C_QC:C_QC + SEQ].unsqueeze(1).to_broadcast([P, 2, SEQ])
                            dst = qf[:, mt % 2, :]
                            dve.scalar_tensor_tensor(out=dst.rearrange("p (b n) -> p b n", b=2), in0=src,
                                                     scalar=c1[:, mt:mt + 1], in1=c_, op0=ALU.add,
                                                     op1=ALU.add).then_inc(qk_sb, 1)
                            dve.wait_ge(qk_sb, after(8 * i + mt + 1))
                            if mt == 0:
                                dve.wait_ge(st_ps, after(16 * i))
                            for j in range(4):
                                ins = dve.tensor_scalar(qz[:, mt, j, :], dst, cf[:, C_ROWS + j:C_ROWS + j + 1], None, ALU.mult)
                            ins.then_inc(qz_ready, 1)
                        else:
                            g = mt - 4
                            c_ = cf[:, C_KC + g * SEQ:C_KC + (g + 1) * SEQ].unsqueeze(1).to_broadcast([P, 2, SEQ])
                            dve.scalar_tensor_tensor(out=kk[:, g, :].rearrange("p (b n) -> p b n", b=2), in0=src,
                                                     scalar=c1[:, mt:mt + 1], in1=c_, op0=ALU.add,
                                                     op1=ALU.add).then_inc(qk_sb, 1)
                    dve.wait_ge(pv_ps, after(8 * i))
                    for n in range(2):
                        dve.wait_ge(v_ps, after(2 * i + n + 1))
                        for t in range(2):
                            ins = dve.tensor_tensor(v1[:, 2 * n + t, :, 0:HD],
                                                    PS[4 + n][:, t * D:(t + 1) * D].rearrange("p (h e) -> p h e", h=H),
                                                    r1[:].rearrange("p (h e) -> p h e", h=H), ALU.add)
                        ins.then_inc(v_sb, 1)
                    routing(1, i, step)
                    routing_out(1, i)
                    for b in range(2):
                        bb = 2 * i + b
                        for U in range(8):
                            qt, g = U // 4, U % 4
                            dve.wait_ge(sm_ps, after(8 * bb + U + 1))
                            for n in range(2):
                                src = PS[2 * (U % 2) + n][:].rearrange("p (j n) -> p j n", j=2)[:, :, 0:(qt + 1) * P]
                                ins = dve.tensor_reduce(mneg[:, qt, 4 * g + 2 * n:4 * g + 2 * n + 2], src, AX.X, ALU.max,
                                                        negate=True)
                            ins.then_inc(sm_read, 1)
                        dve.wait_ge(sm_read, after(8 * bb + 8))
                        dve.wait_ge(mt_ps, after(bb))
                        step(dve.tensor_copy(m2[:, :, 0:H], mneg[:]))
                        step(dve.tensor_tensor(mres[:], mneg[:], m2[:, :, 0:H], ALU.subtract))
                        dve.tensor_copy(m2[:, :, H:2 * H], mres[:]).then_inc(m2_ready, 1)
                        dve.wait_ge(mt_ps, after(bb + 1))
                        dve.wait_ge(st_ps, after(8 * bb))
                        dve.tensor_copy(mT[:], PS[6][:].bitcast(BF16)[0:2 * H, 0:SEQ]).then_inc(mt_sb, 1)
                        for qt in range(2):
                            dve.wait_ge(on_ps, after(2 * bb + qt + 1))
                            src = PS[6 + qt][:].rearrange("p (h e) -> p h e", h=H)
                            step(dve.reciprocal(orc[:, qt, :, :], src[:, :, HD:HD + 1]))
                            if qt == 0:
                                dve.wait_ge(at_ps, after(bb))
                            dve.tensor_tensor(ao[:, qt, :].rearrange("p (h e) -> p h e", h=H), src[:, :, 0:HD],
                                              orc[:, qt, :, :].to_broadcast([P, H, HD]), ALU.mult).then_inc(ao_ready, 1)
                    assert step.n == N_STEPS[1], step.n
                moe(1)
                with dve.Fori(0, NCH) as i:
                    dve.wait_ge(S["y_read", 1], after(4 * HALVES))
                    dve.wait_ge(fcb, after(2 * i))
                    dve.tensor_tensor(gs[:], sT[:, :, ds(i * CH, CH)], gT[:, :, ds(i * CH, CH)], ALU.mult).then_inc(fgs, 1)
                    for n in range(2):
                        dve.wait_ge(fcb, after(2 * i + n + 1))
                        xx = x[:, ds(i * TPC + 2 * n, 2), :]
                        dve.tensor_tensor(xx, xx, PS[4 + n][:].rearrange("p (t d) -> p t d", t=2), ALU.add).then_inc(fx, 1)


N_STEPS = {0: 24, 1: 27}


def kernel(**inp):
    import numpy as np
    import ml_dtypes
    import concourse.bacc as _bacc
    from concourse import mybir as _mybir
    from concourse.bass_utils import run_bass_kernel_spmd as _run

    a = {k: np.asarray(v) for k, v in inp.items()}
    f32, bf16 = np.float32, ml_dtypes.bfloat16

    def kxm(w):
        return w.reshape(2, 128, -1).transpose(1, 0, 2).reshape(128, -1)

    def heads_apart(w):
        o = np.zeros(w.shape[:-1] + (16, 32), w.dtype)
        o[..., 0:16] = w.reshape(w.shape[:-1] + (16, 16))
        return o.reshape(w.shape[:-1] + (512,))

    def cols(v):
        return v.reshape(-1, 128).T

    x = a["L0_attn_x"].reshape(-1, 256)
    kv = np.concatenate([a["L0_attn_Wk"].T, a["L0_attn_Wv"].T], 1)
    router0 = np.concatenate([a["L0_ffn_router_weight"].T, a["L0_ffn_shared_gate_w"].T], 1)
    a0 = np.concatenate([kxm(a["L0_attn_Wq"].T), kxm(kv), kxm(a["L0_attn_Wo"].T), kxm(router0)], 1)
    c0 = np.concatenate([cols(a["L0_attn_bq"]), cols(a["L0_attn_bo"])], 1)
    r0 = np.concatenate([a["L0_attn_bk"], a["L0_attn_bv"]])
    wqkv, bqkv = a["L1_attn_w_qkv"], a["L1_attn_b_qkv"]
    a1 = np.concatenate([kxm(heads_apart(wqkv[:, 0:256])), kxm(heads_apart(wqkv[:, 256:512])), kxm(wqkv[:, 512:768]),
                         kxm(a["L1_attn_w_proj"]), kxm(a["L1_ffn_gate_w"].T)], 1)
    c1 = np.concatenate([cols(heads_apart(bqkv[0:256])), cols(heads_apart(bqkv[256:512])), cols(a["L1_attn_b_proj"])], 1)
    r1 = bqkv[512:768]

    def tiles(gate, up, down):
        n = n_tiles(gate.shape[0])

        def pad(w):
            o = np.zeros((n * 128, 256), w.dtype)
            o[0:w.shape[0]] = w
            return o.reshape(n, 128, 256)
        t = [pad(w).reshape(n, 128, 2, 128).transpose(0, 3, 2, 1).reshape(n, 128, 256) for w in (gate, up)]
        return np.ascontiguousarray(np.concatenate(t + [pad(down)], 2))

    gu, dn = a["L0_ffn_gate_up_proj"], a["L0_ffn_down_proj"]
    inner0 = gu.shape[1] // 2
    w0 = tiles(np.concatenate([gu[:, :inner0].reshape(-1, 256), a["L0_ffn_sh_gate_w"]]),
               np.concatenate([gu[:, inner0:].reshape(-1, 256), a["L0_ffn_sh_up_w"]]),
               np.concatenate([dn.transpose(0, 2, 1).reshape(-1, 256), a["L0_ffn_sh_down_w"].T]))
    inner1 = a["L1_ffn_w1"].shape[1]
    w1 = tiles(np.concatenate([a["L1_ffn_w1"].reshape(-1, 256), a["L1_ffn_sw1"]]),
               np.concatenate([a["L1_ffn_w3"].reshape(-1, 256), a["L1_ffn_sw3"]]),
               np.concatenate([a["L1_ffn_w2"].transpose(0, 2, 1).reshape(-1, 256), a["L1_ffn_sw2"].T]))

    def selector(inner, experts, shared):
        owner = np.concatenate([np.repeat(np.arange(experts), inner), np.full(shared, experts)])
        o = np.zeros((128, n_tiles(len(owner)) * 128), bf16)
        for part in range(PARTS):
            o[part * (experts + 1) + owner, np.arange(len(owner))] = 1
        return o

    cf = np.zeros((128, N_CF), f32)
    pos = np.arange(SEQ, dtype=f32)
    decay = np.exp(-pos / SEQ).astype(f32)
    p = np.arange(128)
    cf[:, C_ID:C_ID + 128] = np.eye(128)
    cf[:, C_DCOL:C_DCOL + 2] = decay.reshape(2, 128).T
    cf[:, C_DROW:C_DROW + SEQ] = decay
    cf[:, C_BD:C_BD + 128] = (p[:, None] // HD == p[None, :] // HD)
    cf[:, C_IOTA:C_IOTA + E1] = np.arange(E1)
    slopes = 2.0 ** (-0.5 * np.arange(1, H + 1))
    for j in range(4):
        cf[32 * j:32 * j + 32, C_ROWS + j] = 1
        cf[32 * j + 16, C_QC:C_QC + SEQ] = 1
        cf[32 * j + 17, C_QC:C_QC + SEQ] = -pos
        for g in range(4):
            cf[32 * j + 16, C_KC + g * SEQ:C_KC + (g + 1) * SEQ] = HD * slopes[4 * g + j] * pos
            cf[32 * j + 17, C_KC + g * SEQ:C_KC + (g + 1) * SEQ] = HD * slopes[4 * g + j]
    cf[:, C_EPS] = EPS_LN
    cbs = [np.eye(128), np.where(p[None, :] > p[:, None], -1e30, 0), np.where(p[None, :] < p[:, None], -1e30, 0),
           selector(inner0, E0, a["L0_ffn_sh_gate_w"].shape[0]), selector(inner1, E1, a["L1_ffn_sw1"].shape[0])]
    selm = np.zeros((128, H, 128))
    for h in range(H):
        selm[h, h] = selm[H + h, h] = 1
    cbs += [selm.reshape(128, -1), np.zeros((128, 128))]
    cb = np.concatenate([c.astype(bf16) for c in cbs], 1)

    nc = _bacc.Bacc("TRN2", target_bir_lowering=False, num_devices=1)
    arrays, args = {}, []
    for name, v in (("x", x), ("cf", cf), ("cb", cb), ("a0", a0), ("c0", c0), ("r0", r0), ("w0", w0), ("a1", a1),
                    ("c1", c1), ("r1", r1), ("w1", w1)):
        v = np.ascontiguousarray(v)
        arrays[f"in_{name}"] = v
        args.append(nc.dram_tensor(f"in_{name}", v.shape, _mybir.dt.from_np(v.dtype), kind="ExternalInput").ap())
    out = nc.dram_tensor("out_0", x.shape, _mybir.dt.float32, kind="ExternalOutput").ap()
    two_block_kernel(nc, *args, out)
    r = _run(nc, [arrays], core_ids=[0])
    return r.results[0]["out_0"].reshape(a["L0_attn_x"].shape)
```

```python
from contextlib import ExitStack

import concourse.bass as bass
from concourse import mybir

F32 = mybir.dt.float32
F32R = mybir.dt.float32r
BF16 = mybir.dt.bfloat16
F16 = mybir.dt.float16
U32 = mybir.dt.uint32
ALU = mybir.AluOpType
ACT = mybir.ActivationFunctionType
AX = mybir.AxisListType
ds = bass.ds

P = 128
D = 256
KT = D // P
SEQ = 256
CH = 512
TPC = CH // P
H, HD = 16, 16
VO = P + H // 2
EPS_LN, EPS_Z = 1e-5, 1e-6
E0, E1 = 8, 16
G0, G1 = E0 + 1, E1 + 1
PARTS = 3
RING = 4
OPEN = 4
WCOLS = 2 * KT * P + D

C_ID = 0
C_DCOL = C_ID + P
C_DROW = C_DCOL + SEQ // P
C_BD = C_DROW + SEQ
C_IOTA = C_BD + P
C_POSQ = C_IOTA + E1
C_POSK = C_POSQ + SEQ
C_SLQ = C_POSK + SEQ
C_SLK = C_SLQ + H // 2
C_EPS = C_SLK + H // 2
N_CF = C_EPS + 1


SCORE_BANKS = ((2, 0), (6, 6))
DT_BANK = (0, 3)
SUM_BANK = (6, 0)
OUT_BANK = (6, 2)


def after(n):
    return n + 1


def prime(eng, sems):
    for s in sems:
        eng.sem_inc(s, 1)


def n_tiles(rows):
    return -(-rows // P)


def two_block_kernel(nc, x_in, cf_in, cb_in, a0_in, c0_in, r0_in, w0_in, a1_in, c1_in, r1_in, w1_in, spread_in, out):
    NCH = x_in.shape[0] // CH
    NTOK = x_in.shape[0] // P
    NT = {0: w0_in.shape[0], 1: w1_in.shape[0]}
    HALVES = 2
    CPH = NCH // HALVES
    GR = {0: G0, 1: G1}
    NE = {0: E0, 1: E1}
    SEL0 = 3 * P
    SEL1 = SEL0 + NT[0] * P
    SELM = SEL1 + NT[1] * P
    ZERO = SELM + H * P
    N_CB = ZERO + P

    with ExitStack() as ctx:
        def sb(name, shape, dt):
            return ctx.enter_context(nc.sbuf_tensor(name, shape, dt))

        def sem(name):
            return ctx.enter_context(nc.semaphore(name))

        PS = [ctx.enter_context(nc.psum_tensor(f"bank{b}", [P, 512], F32)) for b in range(8)]

        x = sb("x", [P, NTOK, D], F32)
        cf = sb("cf", [P, N_CF], F32)
        cb = sb("cb", [P, N_CB], BF16)
        a1 = sb("a1", [P, a1_in.shape[1]], F32)
        c1 = sb("c1", [P, 6], F32)
        r1 = sb("r1", [P, 256], F32)
        sT = sb("sT", [P, KT, NCH * CH], F32)
        gT = sb("gT", [P, KT, NCH * CH], F32)
        dT = sb("dT", [P, NCH * CH], BF16)

        ident = cf[:, C_ID:C_ID + P]
        identb = cb[:, 0:P]
        mask_q = cb[:, P:2 * P]
        mask_k = cb[:, 2 * P:3 * P]

        s_x0 = sem("first_x_landed")
        s_x = sem("other_x_landed")
        s_cf = sem("float_constants_landed")
        s_a0 = sem("block0_weights_landed")
        s_cb = sem("bfloat_constants_landed")
        s_a1 = sem("block1_weights_landed")
        s_zero = sem("dT_cleared")
        ones_set = sem("ones_set")

        xn = sb("xn", [P, TPC, D], F32)
        xt = sb("xt", [P, KT, CH], F32)
        stats = sb("stats", [P, TPC, 6], F32)
        mv = sb("mv", [P, TPC, 2], F32)
        sd = sb("sd", [P, TPC], F32)
        rs = sb("rs", [P, TPC], F32)
        lg = sb("lg", [P, TPC, G1], F32)
        lmax = sb("lmax", [P, TPC, 1], F32)
        lsub = sb("lsub", [P, TPC, G1], F32)
        ex = sb("ex", [P, TPC, G1], F32)
        exs = sb("exs", [P, TPC, 1], F32)
        pr = sb("pr", [P, TPC, G1], F32)
        top = sb("top", [P, TPC, 8], F32)
        topi = sb("topi", [P, TPC, 8], U32)
        topf = sb("topf", [P, TPC, 2], F32)
        wsum = sb("wsum", [P, TPC, 1], F32)
        wtop = sb("wtop", [P, TPC, 2], F32)
        hot = sb("hot", [P, 2, TPC, E1], F32)
        dw = sb("dw", [P, TPC, G1], F32)
        dres = sb("dres", [P, TPC, G1], F32)
        dp = sb("dp", [P, TPC, 96], BF16)
        scratch = sb("scratch", [P, 1], F32)

        mneg = sb("mneg", [P, 2, H], F32)
        m2 = sb("m2", [P, 2, 2 * H], BF16)
        mT = sb("mT", [P, SEQ], BF16)
        mres = sb("mres", [P, 2, H], F32)
        orc = sb("orc", [P, 2, H, 1], F32)
        ring0 = sb("ring", [P, RING, WCOLS], F32)
        ring1 = ring0[:, :, 0:WCOLS // 2].bitcast(BF16)

        def moe_buffers(L, tb):
            return dict(
                wh=tb(f"wh{L}", [P, RING, WCOLS if L == 0 else D], F32R),
                wl=tb(f"wl{L}", [P, RING, WCOLS], F32R) if L == 0 else None,
                sg=tb(f"sg{L}", [P, 2, CH], F32),
                hf=tb(f"hf{L}", [P, 2, CH], F32),
                hh=tb(f"hh{L}", [P, 4, CH], F32R),
                hl=tb(f"hl{L}", [P, 4, CH], F32R))

        def scope(outer):
            inner = ExitStack()
            return inner, lambda name, shape, dt: inner.enter_context(nc.sbuf_tensor(name, shape, dt))[:]

        MB = {}
        block0, tb = scope(ctx)
        xh32 = tb("xh32", [P, KT, NCH * CH], F32R)
        xl32 = tb("xl32", [P, KT, NCH * CH], F32R)
        inner, tb = scope(block0)
        a0 = tb("a0", [P, a0_in.shape[1]], F32)
        c0 = tb("c0", [P, 4], F32)
        r0 = tb("r0", [P, 512], F32)
        qT = tb("qT", [P, 2, CH], F32)
        kb = tb("kb", [P, TPC, D], F32)
        kn = tb("kn", [P, TPC, D], F32)
        vo = tb("vo", [P, TPC, 2, VO], F32)
        kvm = tb("kvm", [P, 2, 2, VO], F32)
        den = tb("den", [P, TPC, H, 1], F32)
        rden = tb("rden", [P, TPC, H, 1], F32)
        an = tb("an", [P, TPC, D], F32)
        aT = tb("aT", [P, 2, CH], F32)
        inner.close()
        inner, tb = scope(block0)
        MB[0] = moe_buffers(0, tb)
        inner.close()
        block0.close()
        block1, tb = scope(ctx)
        xh16 = tb("xh16", [P, KT, NCH * CH], F16)
        xl16 = tb("xl16", [P, KT, NCH * CH], F16)
        gs = tb("gs", [P, 2, CH], F32)
        inner, tb = scope(block1)
        spread = tb("spread", [P, 4, 4, P], F32R)
        part_h = tb("part_h", [P, 2, CH], F32R)
        part_l = tb("part_l", [P, 2, CH], F32R)
        QS = tb("QS", [P, H // 2, CH], F32R)
        KS = tb("KS", [P, H // 2, CH], F32R)
        v1 = tb("v1", [P, TPC, H, 2 * HD], F32)
        pe_ = tb("expscores", [P, 2, 2, 4, SEQ], F32)
        spread_stage = pe_[:, 0, 0, :, :].rearrange("p j n -> p (j n)").bitcast(BF16)
        ot = tb("ot", [P, 4, SEQ], F32)
        ao = tb("ao", [P, 2, D], F32)
        aoT = tb("aoT", [P, 2, CH], F32)
        inner.close()
        inner, tb = scope(block1)
        MB[1] = moe_buffers(1, tb)
        inner.close()
        block1.close()
        if True:
            S = {}
            for L in (0, 1):
                for n in ("mv", "sd", "xn", "xt_ps", "xt_sb", "xlo", "lg_ps", "lg_read", "lsub", "ex",
                          "dp", "dt_ps", "dt_sb", "s_ps", "s_sb", "chunk_vec",
                          "wh_ready", "wl_ready", "g_ps", "u_ps", "r_ps", "silu",
                          "us", "h", "hh", "hl", "down", "y_ps", "y_read"):
                    S[n, L] = sem(f"{n}_{L}")
            landed = {L: [sem(f"tile_landed_{L}_{n}") for n in range(RING)] for L in (0, 1)}

            def wait_landed(eng, L, h, turn, t):
                slot = t % RING
                loads = NT[L] // RING + (slot < NT[L] % RING)
                eng.wait_ge(landed[L][slot], (h * loads + turn + t // RING + 1) * 16)

            q_ps, qr_sb, qT_ready = sem("q_ps"), sem("qr_sb"), sem("qT_ready")
            kv_ps, kv_sb, k_ready = sem("kv_ps"), sem("kv_sb"), sem("k_ready")
            kvm_ps, kvm_ready, nd_ps, an_ready = sem("kvm_ps"), sem("kvm_ready"), sem("nd_ps"), sem("an_ready")
            aT_ps, aT_sb = sem("aT_ps"), sem("aT_sb")
            gs_ready, cb_ps = sem("gs_ready"), sem("cb_ps")
            proj_ps, high_ready, low_ready = sem("proj_ps"), sem("high_ready"), sem("low_ready")
            spread_ps, stacked = sem("spread_ps"), sem("stacked")
            spread_landed, spread_set, front_vec = sem("spread_landed"), sem("spread_set"), sem("front_vec")
            ln_vec = sem("ln_vec")
            v_ps, v_sb = sem("v_ps"), sem("v_sb")
            sm_ps, sm_read, m2_ready = sem("scores_ps"), sem("scores_maxed"), sem("max_parts_ready")
            mt_ps, mt_sb, st_ps, exd = sem("maxT_ps"), sem("maxT_sb"), sem("scoresT_ps"), sem("exp_done")
            pv_ps, ot_sb, on_ps, ao_ready = sem("pv_ps"), sem("ot_sb"), sem("on_ps"), sem("ao_ready")
            at_ps, at_sb = sem("at_ps"), sem("at_sb")
            fgs, fcb, fx, s_out = sem("final_gs"), sem("final_ps"), sem("final_x"), sem("out_stored")

            block = ctx.enter_context(nc.Block())

            @block.sync
            def _(sp):
                xv = x_in.rearrange("(t p) d -> p t d", p=P)
                sp.dma_start(x[:, 0:TPC, :], xv[:, 0:TPC, :]).then_inc(s_x0, 16)
                sp.dma_start(a0, a0_in).then_inc(s_a0, 16)
                sp.dma_start(c0, c0_in).then_inc(s_a0, 16)
                sp.dma_start(r0, r0_in.partition_broadcast(P)).then_inc(s_a0, 16)
                for c in range(1, NCH):
                    sp.dma_start(x[:, c * TPC:(c + 1) * TPC, :], xv[:, c * TPC:(c + 1) * TPC, :]).then_inc(s_x, 16)
                sp.dma_start(cb[:], cb_in).then_inc(s_cb, 16)
                sp.dma_start(a1[:], a1_in).then_inc(s_a1, 16)
                sp.dma_start(c1[:], c1_in).then_inc(s_a1, 16)
                sp.dma_start(r1[:], r1_in.partition_broadcast(P)).then_inc(s_a1, 16)

                def stream(L, w_in, ring, freed):
                    with sp.Fori(0, HALVES) as h:
                        for n in range(RING):
                            freed(h, 0)
                            sp.dma_start(ring[:, n, :], w_in[n]).then_inc(landed[L][n], 16)
                        with sp.Fori(0, NT[L] // RING - 1) as p:
                            for j in range(RING):
                                tile = sp.snap(p * RING + RING + j)
                                freed(h, p * RING + j + 1)
                                sp.dma_start(ring[:, j, :], w_in[ds(tile, 1)].rearrange("a p n -> (a p) n"))\
                                  .then_inc(landed[L][j], 16)
                        freed(h, NT[L] - RING)
                        sp.dma_start(ring[:, 0, :], w_in[NT[L] - 1]).then_inc(landed[L][0], 16)

                def freed0(h, m):
                    sp.wait_ge(S["wh_ready", 0], after(h * NT[0] + m))
                    sp.wait_ge(S["wl_ready", 0], after(h * NT[0] + m))

                def freed1(h, m):
                    sp.wait_ge(S["down", 1], after(h * (NT[1] * CPH + OPEN) + m * CPH + OPEN * (not isinstance(m, int) or m > 0)))

                stream(0, w0_in, ring0, freed0)
                sp.wait_ge(S["y_ps", 0], after(HALVES))
                sp.dma_start(spread_stage, spread_in).then_inc(spread_landed, 16)
                stream(1, w1_in, ring1, freed1)
                with sp.Fori(0, NCH) as i:
                    token, tile = sp.snap(i * CH), sp.snap(i * TPC)
                    sp.wait_ge(fx, after(i * 2 + 2))
                    sp.dma_start(out[ds(token, CH), :].rearrange("(t p) d -> p t d", p=P),
                                 x[:, ds(tile, TPC), :]).then_inc(s_out, 16)
                sp.wait_ge(s_out, 16 * NCH)

            @block.gpsimd
            def _(pool):
                pool.dma_start(cf[:], cf_in).then_inc(s_cf, 16)
                pool.memset(dT[:], 0.0).then_inc(s_zero, 1)
                pool.memset(mT[:], 0.0).then_inc(s_zero, 1)
                pool.memset(dp[:], 0.0).then_inc(s_zero, 1)
                pool.memset(vo[:, :, :, P:VO], 1.0).then_inc(ones_set, 1)

            @block.tensor
            def _(pe):
                prime(pe, [S[n, L] for L in (0, 1) for n in
                           ("xt_ps", "lg_ps", "dt_ps", "s_ps", "g_ps", "u_ps", "r_ps", "down", "y_ps")]
                      + [q_ps, kv_ps, kvm_ps, nd_ps, aT_ps, cb_ps, proj_ps, spread_ps, v_ps, sm_ps, mt_ps, st_ps, pv_ps, on_ps,
                         at_ps, fcb])
                pe.wait_ge(s_cf, 16)

                def x_transposes(L, i, banks):
                    pe.wait_ge(S["xn", L], after(4 * i + 4))
                    for k in range(KT):
                        for t in range(TPC):
                            mm = pe.transpose(PS[banks[k]][:, t * P:(t + 1) * P], xn[:, t, k * P:(k + 1) * P], ident)
                        mm.then_inc(S["xt_ps", L], 1)

                def logits(L, bank, a, rcol):
                    n = GR[0] if L == 0 else NE[1]
                    for t in range(TPC):
                        for k in range(KT):
                            mm = pe.matmul(PS[bank][:, t * 32:t * 32 + n], xt[:, k, t * P:(t + 1) * P],
                                           a[:, rcol + k * n:rcol + (k + 1) * n],
                                           start=(t == 0 and k == 0), stop=(k == 1), skip_group_check=True)
                    mm.then_inc(S["lg_ps", L], 1)

                def routing_transposes(L, i):
                    pe.wait_ge(S["dp", L], after(i + 1))
                    n = PARTS * GR[L]
                    dst = PS[DT_BANK[L]][:].bitcast(BF16)
                    if L == 1:
                        n = 96
                    for t in range(TPC):
                        mm = pe.transpose(dst[0:n, t * P:(t + 1) * P], dp[:, t, 0:n], identb)
                    mm.then_inc(S["dt_ps", L], 1)

                def moe(L):
                    n_items = NT[L] * CPH
                    xs = (xh32, xl32) if L == 0 else (xh16, xl16)
                    wh, wl, hh, hl = (MB[L][n] for n in ("wh", "wl", "hh", "hl"))
                    down0 = 2 * KT * P if L == 0 else 0

                    def gates(h, base, k, turn):
                        slot, c = (k // CPH) % RING, k % CPH
                        g, u, r = (PS[(3 * k + n) % 4] for n in range(3))
                        tok = ds(h * (CPH * CH) + c * CH, CH)
                        tile_reg = turn * RING + k // CPH
                        if c == 0:
                            if L == 0:
                                pe.wait_ge(S["wh_ready", L], after(h * NT[L] + tile_reg + 1))
                                pe.wait_ge(S["wl_ready", L], after(h * NT[L] + tile_reg + 1))
                            else:
                                wait_landed(pe, L, h, turn, k // CPH)
                        for out_, col, ready in ((g, 0, S["g_ps", L]), (u, KT * P, S["u_ps", L])):
                            if out_ is g:
                                if k >= 2:
                                    pe.wait_ge(S["h", L], after(h * n_items + base + k - 1))
                            elif k >= 1:
                                pe.wait_ge(S["silu", L], after(h * n_items + base + k))
                            first = True
                            for kt in range(KT):
                                cols = slice(col + kt * P, col + (kt + 1) * P)
                                if L == 0:
                                    terms = ((wh[:, slot, cols], xs[0]), (wh[:, slot, cols], xs[1]),
                                             (wl[:, slot, cols], xs[0]))
                                else:
                                    terms = ((ring1[:, slot, cols], xs[0]), (ring1[:, slot, cols], xs[1]))
                                for n, (w, xx) in enumerate(terms):
                                    mm = pe.matmul(out_[:], w, xx[:, kt, tok], start=first,
                                                   stop=(kt == KT - 1 and n == len(terms) - 1))
                                    first = False
                            mm.then_inc(ready, 1)
                        if k >= 1:
                            pe.wait_ge(S["us", L], after(h * n_items + base + k))
                        s0 = SEL0 if L == 0 else SEL1
                        pe.matmul(r[:], cb[:, ds(s0 + tile_reg * P, P)], dT[:, tok], start=True,
                                  stop=True).then_inc(S["r_ps", L], 1)

                    def down(h, base, tile, k):
                        slot, c = (k // CPH) % RING, k % CPH
                        pe.wait_ge(S["hl", L], after(h * n_items + base + k + 1))
                        if L == 1:
                            pe.wait_ge(S["wh_ready", L], after(h * NT[L] + tile + k // CPH + 1))
                        for d in range(D // P):
                            cols = slice(down0 + d * P, down0 + (d + 1) * P)
                            terms = [(wh, hh), (wh, hl)] + ([(wl, hh)] if L == 0 else [])
                            for w, a in terms:
                                mm = pe.matmul(PS[4 + 2 * c + d][:], w[:, slot, cols], a[:, k % 4, :],
                                               start=False, stop=False, skip_group_check=True)
                        mm.then_inc(S["down", L], 1)
                        return mm

                    body = RING * CPH
                    with pe.Fori(0, HALVES) as h:
                        pe.wait_ge(S["y_read", L], after(h * 4))
                        for b in range(4):
                            pe.matmul(PS[4 + b][:], zcol, dT[:, 0:CH], start=True, stop=False,
                                      skip_group_check=True).then_inc(S["down", L], 1)
                        pe.wait_ge(S["h", L], after(h * n_items))
                        gates(h, 0, 0, 0)
                        gates(h, 0, 1, 0)
                        with pe.Fori(0, NT[L] // RING) as p:
                            for k in range(body):
                                gates(h, p * body, k + 2, p)
                                down(h, p * body, p * RING, k)
                        for k in range(NT[L] // RING * body, n_items):
                            mm = down(h, 0, 0, k)
                        pe.matmul(PS[7][:], zcol, dT[:, 0:CH], start=False, stop=True,
                                  skip_group_check=True).then_inc(S["y_ps", L], 1)

                zcol = cb[:, ZERO:ZERO + P]

                def linear_attention(i, more):
                    for m in range(2):
                        for k in range(KT):
                            mm = pe.matmul(PS[4 + m][:], a0[:, k * D + m * P:k * D + (m + 1) * P], xt[:, k, :],
                                           start=(k == 0), stop=(k == 1))
                        mm.then_inc(q_ps, 1)
                    for t in range(TPC):
                        if t >= 2:
                            pe.wait_ge(kv_sb, after(i * TPC + t - 1))
                        for k in range(KT):
                            mm = pe.matmul(PS[6 + t % 2][:], xt[:, k, t * P:(t + 1) * P],
                                           a0[:, 512 + k * 512:512 + (k + 1) * 512], start=(k == 0), stop=(k == 1))
                        mm.then_inc(kv_ps, 1)
                    pe.wait_ge(S["s_sb", 0], after(2 * i))
                    logits(0, 2, a0, 2048)
                    pe.wait_ge(S["dt_sb", 0], after(i))
                    for b in range(2):
                        pe.wait_ge(k_ready, after(i * TPC + 2 * b + 2))
                        pe.wait_ge(kv_sb, after(i * TPC + 2 * b + 2))
                        for m in range(2):
                            for t in range(2):
                                mm = pe.matmul(PS[b][:, m * 256:m * 256 + VO], kn[:, 2 * b + t, m * P:(m + 1) * P],
                                               vo[:, 2 * b + t, m, :], start=(m == 0 and t == 0), stop=(t == 1),
                                               skip_group_check=True)
                        mm.then_inc(kvm_ps, 1)
                    if more:
                        pe.wait_ge(S["lg_read", 0], after(i + 1))
                        x_transposes(0, i + 1, (3, 2))
                    pe.wait_ge(qT_ready, after(2 * i + 2))
                    for t in range(TPC):
                        pe.wait_ge(kvm_ready, after(2 * i + t // 2 + 1))
                        for m in range(2):
                            mm = pe.matmul(PS[4 + t][:, m * 256:m * 256 + VO], qT[:, m, t * P:(t + 1) * P],
                                           kvm[:, t // 2, m, :], start=(m == 0), stop=True, skip_group_check=True)
                        mm.then_inc(nd_ps, 1)
                    for t in range(TPC):
                        pe.wait_ge(an_ready, after(TPC * i + t + 1))
                        for m in range(2):
                            mm = pe.transpose(PS[m][:, t * P:(t + 1) * P], an[:, t, m * P:(m + 1) * P], ident)
                    mm.then_inc(aT_ps, 1)
                    if more:
                        pe.wait_ge(S["xt_sb", 0], after(2 * i + 4))
                    else:
                        pe.wait_ge(S["lg_read", 0], after(i + 1))
                    pe.wait_ge(aT_sb, after(2 * i + 2))
                    for d in range(2):
                        for m in range(2):
                            mm = pe.matmul(PS[2 + d][:], a0[:, 1536 + m * D + d * P:1536 + m * D + (d + 1) * P],
                                           aT[:, m, :], start=(m == 0), stop=(m == 1))
                        mm.then_inc(S["s_ps", 0], 1)
                    routing_transposes(0, i)

                x_transposes(0, 0, (3, 2))
                pe.wait_ge(s_a0, 48)
                pe.wait_ge(s_cb, 16)
                pe.wait_ge(s_zero, 3)
                pe.wait_ge(ones_set, 1)
                pe.wait_ge(S["xt_sb", 0], after(2))
                with pe.Fori(0, NCH - 1) as i:
                    linear_attention(i, True)
                linear_attention(NCH - 1, False)
                pe.wait_ge(S["s_sb", 0], after(2 * NCH))
                pe.wait_ge(S["dt_sb", 0], after(NCH))
                pe.wait_ge(S["xlo", 0], after(NCH))
                moe(0)

                pe.wait_ge(s_a1, 48)
                pe.wait_ge(ones_set, 2)
                pe.wait_ge(S["y_read", 0], after(4 * HALVES))

                def result_transposes(c):
                    pe.wait_ge(gs_ready, after(c + 1))
                    for t in range(TPC):
                        for d in range(2):
                            mm = pe.transpose(PS[6 + t // 2][:, (t % 2) * D + d * P:(t % 2) * D + (d + 1) * P],
                                              gs[:, d, t * P:(t + 1) * P], ident)
                        if t % 2:
                            mm.then_inc(cb_ps, 1)

                def project(i, n):
                    kind, a = n % 2, n // 2
                    if n >= 2:
                        pe.wait_ge(low_ready, after(4 * i + n - 1))
                    for k in range(KT):
                        w0_ = kind * 512 + k * D + a * P
                        mm = pe.matmul(PS[6 + n % 2][:], a1[:, w0_:w0_ + P], xt[:, k, :], start=(k == 0), stop=(k == 1))
                    mm.then_inc(proj_ps, 1)

                def spread_pairs(i, n):
                    kind = n % 2
                    pe.wait_ge(high_ready, after(4 * i + n + 1))
                    pe.wait_ge(low_ready, after(4 * i + n + 1))
                    for j in range(4):
                        if n:
                            pe.wait_ge(stacked, after(16 * i + 4 * n + j - 3))
                        pe.matmul(PS[2 + j][:], spread[:, 2 * kind, j, :], part_h[:, n % 2, :], start=True, stop=False)
                        pe.matmul(PS[2 + j][:], spread[:, 2 * kind + 1, j, :], part_l[:, n % 2, :],
                                  start=False, stop=True).then_inc(spread_ps, 1)

                def project_values(n):
                    for t in range(2):
                        for k in range(KT):
                            mm = pe.matmul(PS[n][:, t * D:(t + 1) * D], xt[:, k, (2 * n + t) * P:(2 * n + t + 1) * P],
                                           a1[:, 1024 + k * D:1024 + (k + 1) * D],
                                           start=(k == 0 and t == 0), stop=(k == 1), skip_group_check=True)
                    mm.then_inc(v_ps, 1)

                def scores(i, b, U):
                    bb, g, qt = 2 * i + b, U // 2, U % 2
                    bank0 = SCORE_BANKS[b][U % 2]
                    if b == 1 or U >= 2:
                        pe.wait_ge(sm_read, after(8 * bb + U - (b == 0)))
                    for r in range(2):
                        rows = slice(64 * r, 64 * r + 64)
                        bank = PS[bank0 + r]
                        for p in range(2):
                            q0 = b * SEQ + qt * P
                            pe.matmul(bank[:, p * SEQ:(p + 1) * SEQ], QS[rows, 2 * g + p, q0:q0 + P],
                                      KS[rows, 2 * g + p, b * SEQ:(b + 1) * SEQ], start=(p == 0), stop=False,
                                      skip_group_check=True)
                    for r in range(2):
                        mm = pe.matmul(PS[bank0 + r][:].rearrange("p (j n) -> p j n", j=2)[:, :, qt * P:(qt + 1) * P],
                                       identb, mask_q.unsqueeze(1).to_broadcast([P, 2, P]),
                                       start=False, stop=True, skip_group_check=True)
                    mm.then_inc(sm_ps, 1)

                def max_transposes(i, b):
                    bb = 2 * i + b
                    if b == 1:
                        pe.wait_ge(exd, after(8 * bb))
                    pe.wait_ge(m2_ready, after(bb + 1))
                    mb_ = PS[0][:].bitcast(BF16)
                    for qt in range(2):
                        mm = pe.transpose(mb_[0:2 * H, qt * P:(qt + 1) * P], m2[:, qt, :], identb)
                    mm.then_inc(mt_ps, 1)

                def scores_T(i, b, V):
                    bb, g, kt = 2 * i + b, V // 2, V % 2
                    if V == 0:
                        pe.wait_ge(mt_sb, after(bb + 1))
                    if V >= 2:
                        pe.wait_ge(exd, after(8 * bb + V - 1))
                    q0 = kt * P
                    for r in range(2):
                        rows = slice(64 * r, 64 * r + 64)
                        bank = PS[2 * (V % 2) + r]
                        for p in range(2):
                            k0 = b * SEQ + kt * P
                            pe.matmul(bank[:, p * SEQ:(p + 1) * SEQ], KS[rows, 2 * g + p, k0:k0 + P],
                                      QS[rows, 2 * g + p, b * SEQ:(b + 1) * SEQ], start=(p == 0), stop=False,
                                      skip_group_check=True)
                    for r in range(2):
                        bank = PS[2 * (V % 2) + r]
                        for p in range(2):
                            sm0 = SELM + (4 * g + 2 * p + r) * P
                            pe.matmul(bank[:, p * SEQ + q0:(p + 1) * SEQ], cb[:, sm0:sm0 + P], mT[:, q0:SEQ],
                                      start=False, stop=False, skip_group_check=True)
                        mm = pe.matmul(bank[:].rearrange("p (j n) -> p j n", j=2)[:, :, q0:q0 + P],
                                       identb, mask_k.unsqueeze(1).to_broadcast([P, 2, P]),
                                       start=False, stop=True, skip_group_check=True)
                    mm.then_inc(st_ps, 1)

                def weighted_values(i, b, g):
                    bb = 2 * i + b
                    pe.wait_ge(exd, after(8 * bb + 2 * g + 2))
                    if g == 0:
                        if b == 0:
                            pe.wait_ge(v_sb, after(2 * i + 2))
                            pe.wait_ge(S["lg_read", 1], after(i + 1))
                        else:
                            pe.wait_ge(ot_sb, after(2 * bb))
                    for r in range(2):
                        for p in range(2):
                            j = 2 * p + r
                            o_ = PS[4 + g // 2][32 * j:32 * j + 32, (g % 2) * 256:(g % 2) * 256 + 256]
                            pe.matmul(o_, v1[:, 2 * b, 4 * g + j, :], pe_[:, g % 2, 0, 2 * r + p, :],
                                      start=(g % 2 == 0), stop=False, skip_group_check=True)
                            mm = pe.matmul(o_[:, P:2 * P], v1[:, 2 * b + 1, 4 * g + j, :],
                                           pe_[:, g % 2, 1, 2 * r + p, P:2 * P], start=False, stop=True,
                                           skip_group_check=True)
                    mm.then_inc(pv_ps, 1)

                def heads_transposes(i, b):
                    bb = 2 * i + b
                    pe.wait_ge(ot_sb, after(2 * bb + 2))
                    for qt in range(2):
                        for g in range(4):
                            mm = pe.transpose(PS[SUM_BANK[b] + qt][:, g * P:(g + 1) * P], ot[:, g, qt * P:(qt + 1) * P], ident)
                        mm.then_inc(on_ps, 1)

                def outputs_transposes(i, b):
                    bb = 2 * i + b
                    pe.wait_ge(ao_ready, after(2 * bb + 2))
                    for qt in range(2):
                        for m in range(2):
                            mm = pe.transpose(PS[OUT_BANK[b]][:, (m * 2 + qt) * P:(m * 2 + qt + 1) * P],
                                              ao[:, qt, m * P:(m + 1) * P], ident)
                    mm.then_inc(at_ps, 1)

                def attention(i, more):
                    pe.wait_ge(S["dt_sb", 1], after(i))
                    project(i, 0)
                    project(i, 1)
                    spread_pairs(i, 0)
                    project(i, 2)
                    spread_pairs(i, 1)
                    project(i, 3)
                    spread_pairs(i, 2)
                    pe.wait_ge(S["s_sb", 1], after(2 * i))
                    project_values(0)
                    spread_pairs(i, 3)
                    project_values(1)
                    pe.wait_ge(stacked, after(16 * i + 16))
                    scores(i, 0, 0)
                    pe.wait_ge(v_sb, after(2 * i + 2))
                    for U in range(1, 8):
                        scores(i, 0, U)
                    logits(1, 4, a1, 2048)
                    max_transposes(i, 0)
                    if more:
                        pe.wait_ge(low_ready, after(4 * i + 4))
                        result_transposes(i + 1)
                    for g in range(4):
                        scores_T(i, 0, 2 * g)
                        if g == 0:
                            if more:
                                pe.wait_ge(front_vec, after((i + 1) * N_FRONT + 2))
                            else:
                                pe.wait_ge(low_ready, after(4 * i + 4))
                        scores(i, 1, 2 * g)
                        scores_T(i, 0, 2 * g + 1)
                        if g:
                            weighted_values(i, 0, g - 1)
                        scores(i, 1, 2 * g + 1)
                    weighted_values(i, 0, 3)
                    max_transposes(i, 1)
                    for g in range(4):
                        scores_T(i, 1, 2 * g)
                        scores_T(i, 1, 2 * g + 1)
                        if g == 0:
                            heads_transposes(i, 0)
                        if g == 2:
                            outputs_transposes(i, 0)
                        if g == 3 and more:
                            pe.wait_ge(at_sb, after(2 * i + 1))
                            x_transposes(1, i + 1, (7, 6))
                        if g:
                            weighted_values(i, 1, g - 1)
                    weighted_values(i, 1, 3)
                    routing_transposes(1, i)
                    heads_transposes(i, 1)
                    outputs_transposes(i, 1)
                    pe.wait_ge(at_sb, after(2 * i + 2))
                    for d in range(2):
                        for m in range(2):
                            mm = pe.matmul(PS[d][:], a1[:, 1536 + m * D + d * P:1536 + m * D + (d + 1) * P],
                                           aoT[:, m, :], start=(m == 0), stop=(m == 1))
                        mm.then_inc(S["s_ps", 1], 1)
                    if more:
                        pe.wait_ge(S["xt_sb", 1], after(2 * i + 4))

                result_transposes(0)
                pe.wait_ge(front_vec, after(2))
                x_transposes(1, 0, (7, 6))
                pe.wait_ge(S["xt_sb", 1], after(2))
                pe.wait_ge(spread_set, 1)
                with pe.Fori(0, NCH - 1) as i:
                    attention(i, True)
                attention(NCH - 1, False)
                pe.wait_ge(S["s_sb", 1], after(2 * NCH))
                pe.wait_ge(S["dt_sb", 1], after(NCH))
                pe.wait_ge(S["xlo", 1], after(NCH))
                moe(1)
                pe.wait_ge(S["y_read", 1], after(4 * HALVES))
                with pe.Fori(0, NCH) as i:
                    pe.wait_ge(fgs, after(i + 1))
                    pe.wait_ge(fx, after(2 * i))
                    for t in range(TPC):
                        for d in range(2):
                            mm = pe.transpose(PS[4 + t // 2][:, (t % 2) * D + d * P:(t % 2) * D + (d + 1) * P],
                                              gs[:, d, t * P:(t + 1) * P], ident)
                        if t % 2:
                            mm.then_inc(fcb, 1)

            @block.scalar
            def _(act):
                prime(act, [S[n, L] for L in (0, 1) for n in
                            ("sd", "xt_sb", "ex", "s_sb", "wh_ready", "silu", "hh", "y_read")]
                      + [qr_sb, k_ready, aT_sb, high_ready, exd, ot_sb, at_sb])
                act.wait_ge(s_cf, 16)
                eps_ln = cf[:, C_EPS:C_EPS + 1]

                def deviation(L, i):
                    act.wait_ge(S["mv", L], after(i + 1))
                    act.activation(sd[:], mv[:, :, 1], ACT.Sqrt, bias=eps_ln).then_inc(S["sd", L], 1)

                def x_copies(L, i, banks):
                    act.wait_ge(S["xlo", L], after(i))
                    if L == 0:
                        act.wait_ge(kv_ps, after(TPC * i))
                    act.wait_ge(S["lg_ps", L], after(i))
                    for k in range(KT):
                        act.wait_ge(S["xt_ps", L], after(2 * i + k + 1))
                        act.activation(xt[:, k, :], PS[banks[k]][:], ACT.Copy).then_inc(S["xt_sb", L], 1)

                def moe(L):
                    n_items = NT[L] * CPH
                    w0c = 0 if L == 0 else 2 * KT * P
                    wh, sg, hf, hh = (MB[L][n] for n in ("wh", "sg", "hf", "hh"))

                    def split(h, turn, n):
                        slot = n % RING
                        wait_landed(act, L, h, turn, n)
                        src = ring0 if L == 0 else ring1
                        act.activation(wh[:, slot, :], src[:, slot, w0c:WCOLS], ACT.Copy).then_inc(S["wh_ready", L], 1)

                    def silu(h, base, k):
                        act.wait_ge(S["g_ps", L], after(h * n_items + base + k + 1))
                        act.activation(sg[:, k % 2, :], PS[(3 * k) % 4][:], ACT.Silu).then_inc(S["silu", L], 1)

                    def high_part(h, base, k):
                        act.wait_ge(S["h", L], after(h * n_items + base + k + 1))
                        act.wait_ge(S["down", L], after(h * (n_items + OPEN) + OPEN + base + k - 3))
                        act.activation(hh[:, k % 4, :], hf[:, k % 2, :], ACT.Copy).then_inc(S["hh", L], 1)

                    body = RING * CPH
                    with act.Fori(0, HALVES) as h:
                        act.wait_ge(S["down", L], after(h * (n_items + OPEN)))
                        split(h, 0, 0)
                        silu(h, 0, 0)
                        with act.Fori(0, NT[L] // RING) as p:
                            for j in range(RING):
                                act.wait_ge(S["down", L], after(h * (n_items + OPEN) + OPEN + p * body + (j - 2) * CPH))
                                split(h, p, j + 1)
                                for k in range(j * CPH, (j + 1) * CPH):
                                    silu(h, p * body, k + 1)
                                    high_part(h, p * body, k)
                        for k in range(NT[L] // RING * body, n_items):
                            if k + 1 < n_items:
                                silu(h, 0, k + 1)
                            high_part(h, 0, k)
                        act.wait_ge(S["y_ps", L], after(h + 1))
                        for c in range(CPH):
                            for d in range(2):
                                act.activation(gT[:, d, ds(h * (CPH * CH) + c * CH, CH)], PS[4 + 2 * c + d][:],
                                               ACT.Silu).then_inc(S["y_read", L], 1)

                def linear_attention(i, more):
                    act.wait_ge(qT_ready, after(2 * i))
                    act.wait_ge(nd_ps, after(TPC * i))
                    for m in range(2):
                        act.wait_ge(q_ps, after(2 * i + m + 1))
                        act.activation(qT[:, m, :], PS[4 + m][:], ACT.Relu, bias=c0[:, m:m + 1]).then_inc(qr_sb, 1)
                    if more:
                        deviation(0, i + 1)
                    act.wait_ge(kvm_ps, after(2 * i))
                    for t in range(TPC):
                        act.wait_ge(kv_sb, after(TPC * i + t + 1))
                        act.activation(kn[:, t, :], kb[:, t, :], ACT.Relu,
                                       scale=cf[:, C_DCOL + t % 2:C_DCOL + t % 2 + 1]).then_inc(k_ready, 1)
                    act.wait_ge(S["lsub", 0], after(i + 1))
                    act.activation(ex[:, :, 0:E0], lsub[:, :, 0:E0], ACT.Exp)
                    act.activation(ex[:, :, E0:G0], lg[:, :, E0:G0], ACT.Exp, scale=-1.0).then_inc(S["ex", 0], 1)
                    if more:
                        x_copies(0, i + 1, (3, 2))
                    act.wait_ge(aT_ps, after(i + 1))
                    act.wait_ge(S["s_ps", 0], after(2 * i))
                    for m in range(2):
                        act.activation(aT[:, m, :], PS[m][:], ACT.Copy).then_inc(aT_sb, 1)
                    for d in range(2):
                        act.wait_ge(S["s_ps", 0], after(2 * i + d + 1))
                        act.activation(sT[:, d, ds(i * CH, CH)], PS[2 + d][:], ACT.Identity,
                                       bias=c0[:, 2 + d:3 + d]).then_inc(S["s_sb", 0], 1)

                deviation(0, 0)
                x_copies(0, 0, (3, 2))
                act.wait_ge(s_a0, 48)
                with act.Fori(0, NCH - 1) as i:
                    linear_attention(i, True)
                linear_attention(NCH - 1, False)
                moe(0)

                act.wait_ge(s_a1, 48)

                def exp_scores(i, b, V):
                    bb, g, kt = 2 * i + b, V // 2, V % 2
                    q0 = kt * P
                    act.wait_ge(st_ps, after(8 * bb + V + 1))
                    act.wait_ge(pv_ps, after(4 * bb + max(g - 1, 0)))
                    for r in range(2):
                        ins = act.activation(pe_[:, g % 2, kt, 2 * r:2 * r + 2, q0:SEQ],
                                             PS[2 * (V % 2) + r][:].rearrange("p (j n) -> p j n", j=2)[:, :, q0:SEQ],
                                             ACT.Exp, scale=1.0 / HD)
                    ins.then_inc(exd, 1)

                def sums_copies(i, b):
                    bb = 2 * i + b
                    for n in range(2):
                        act.wait_ge(pv_ps, after(4 * bb + 2 * n + 2))
                        if n == 0:
                            act.wait_ge(on_ps, after(2 * bb))
                        act.activation(ot[:, 2 * n:2 * n + 2, :], PS[4 + n][:].rearrange("p (g n) -> p g n", g=2),
                                       ACT.Copy).then_inc(ot_sb, 1)

                def outputs_copy(i, b):
                    act.wait_ge(at_ps, after(2 * i + b + 1))
                    if b == 0:
                        act.wait_ge(S["s_ps", 1], after(2 * i))
                    act.activation(aoT[:, :, b * SEQ:(b + 1) * SEQ],
                                   PS[OUT_BANK[b]][:].rearrange("p (m n) -> p m n", m=2), ACT.Copy).then_inc(at_sb, 1)

                def attention(i, more):
                    act.wait_ge(spread_ps, after(16 * i))
                    for n in range(4):
                        act.wait_ge(proj_ps, after(4 * i + n + 1))
                        if n >= 2:
                            act.wait_ge(spread_ps, after(16 * i + 4 * (n - 1)))
                        bias = 2 * (n % 2) + n // 2
                        act.activation(part_h[:, n % 2, :], PS[6 + n % 2][:], ACT.Identity,
                                       bias=c1[:, bias:bias + 1]).then_inc(high_ready, 1)
                    act.wait_ge(S["lg_read", 1], after(i + 1))
                    act.activation(ex[:, :, 0:E1], lg[:, :, 0:E1], ACT.Exp, scale=-1.0).then_inc(S["ex", 1], 1)
                    for V in range(8):
                        exp_scores(i, 0, V)
                        if V == 3 and more:
                            deviation(1, i + 1)
                    sums_copies(i, 0)
                    for V in range(8):
                        exp_scores(i, 1, V)
                        if V == 5:
                            outputs_copy(i, 0)
                    if more:
                        x_copies(1, i + 1, (7, 6))
                    sums_copies(i, 1)
                    outputs_copy(i, 1)
                    for d in range(2):
                        act.wait_ge(S["s_ps", 1], after(2 * i + d + 1))
                        act.wait_ge(gs_ready, after(i + 1))
                        act.activation(sT[:, d, ds(i * CH, CH)], PS[d][:], ACT.Identity,
                                       bias=c1[:, 4 + d:5 + d]).then_inc(S["s_sb", 1], 1)

                deviation(1, 0)
                x_copies(1, 0, (7, 6))
                act.wait_ge(spread_set, 1)
                with act.Fori(0, NCH - 1) as i:
                    attention(i, True)
                attention(NCH - 1, False)
                moe(1)

            @block.vector
            def _(dve):
                prime(dve, [S[n, L] for L in (0, 1) for n in
                            ("mv", "xn", "xlo", "lg_read", "lsub", "dp", "dt_sb", "chunk_vec", "wl_ready",
                             "us", "h", "hl")]
                      + [qT_ready, kv_sb, kvm_ready, an_ready, gs_ready, low_ready, stacked, front_vec, ln_vec, v_sb, sm_read,
                         m2_ready, mt_sb, ao_ready, fgs, fx])
                dve.wait_ge(s_cf, 16)

                def hold():
                    dve.memset(scratch[:], 0.0)

                class Steps:

                    def __init__(self, sem_, base):
                        self.sem, self.base, self.n = sem_, base, 0

                    def __call__(self, ins):
                        self.n += 1
                        ins.then_inc(self.sem, 1)
                        dve.wait_ge(self.sem, after(self.base + self.n))

                def statistics(L, i, step):
                    hold()
                    for t in range(TPC):
                        ins = dve.bn_stats(stats[:, t, :], x[:, ds(i * TPC + t, 1), :].rearrange("p a d -> p (a d)"))
                    step(ins)
                    dve.wait_ge(S["sd", L], after(i))
                    hold()
                    for t in range(TPC):
                        ins = dve.bn_aggr(mv[:, t, :], stats[:, t, :])
                    ins.then_inc(S["mv", L], 1)

                def normalise(L, i, step):
                    dve.wait_ge(S["sd", L], after(i + 1))
                    step(dve.reciprocal(rs[:], sd[:]))
                    dve.wait_ge(S["xt_ps", L], after(2 * i))
                    for t in range(TPC):
                        dve.tensor_scalar(xn[:, t, :], x[:, ds(i * TPC + t, 1), :].rearrange("p a d -> p (a d)"),
                                          mv[:, t, 0:1], rs[:, t:t + 1], ALU.subtract, ALU.mult).then_inc(S["xn", L], 1)

                def split_x(L, i, step):
                    hi, lo = (xh32, xl32) if L == 0 else (xh16, xl16)
                    dve.wait_ge(S["xt_sb", L], after(2 * i + 2))
                    step(dve.tensor_copy(hi[:, :, ds(i * CH, CH)], xt[:]))
                    hv = hi[:, :, ds(i * CH, CH)]
                    if L == 0:
                        hv = xh32f[:, :, ds(i * CH, CH)]
                    dve.tensor_tensor(lo[:, :, ds(i * CH, CH)], xt[:], hv, ALU.subtract).then_inc(S["xlo", L], 1)

                def read_logits(L, i, bank):
                    n = G0 if L == 0 else E1
                    dve.wait_ge(S["lg_ps", L], after(i + 1))
                    dve.wait_ge(S["ex", L], after(i))
                    dve.tensor_copy(lg[:, :, 0:n], PS[bank][:, 0:TPC * 32].rearrange("p (t n) -> p t n", t=TPC)[:, :, 0:n])\
                       .then_inc(S["lg_read", L], 1)

                def routing(L, i, step):
                    e, n = NE[L], GR[L]
                    dve.wait_ge(S["ex", L], after(i + 1))
                    if L == 0:
                        step(dve.tensor_reduce(exs[:, :, 0], ex[:, :, 0:E0], AX.X, ALU.add))
                        step(dve.reciprocal(wsum[:], exs[:]))
                        step(dve.tensor_tensor(pr[:, :, 0:E0], ex[:, :, 0:E0], wsum[:].to_broadcast([P, TPC, E0]), ALU.mult))
                        step(dve.tensor_scalar(ex[:, :, E0:G0], ex[:, :, E0:G0], 1.0, None, ALU.add))
                        step(dve.reciprocal(dw[:, :, E0:G0], ex[:, :, E0:G0]))
                    else:
                        step(dve.tensor_scalar(ex[:, :, 0:E1], ex[:, :, 0:E1], 1.0, None, ALU.add))
                        step(dve.reciprocal(pr[:, :, 0:E1], ex[:, :, 0:E1]))
                    hold()
                    for t in range(TPC):
                        ins = dve.max(top[:, t, :], pr[:, t, 0:e])
                    step(ins)
                    hold()
                    for t in range(TPC):
                        ins = dve.max_index(topi[:, t, :], top[:, t, :], pr[:, t, 0:e])
                    step(ins)
                    step(dve.tensor_copy(topf[:], topi[:, :, 0:2]))
                    step(dve.tensor_tensor(exs[:], top[:, :, 0:1], top[:, :, 1:2], ALU.add))
                    step(dve.reciprocal(wsum[:], exs[:]))
                    step(dve.tensor_tensor(wtop[:], top[:, :, 0:2], wsum[:].to_broadcast([P, TPC, 2]), ALU.mult))
                    for r in range(2):
                        for t in range(TPC):
                            ins = dve.tensor_scalar(hot[:, r, t, 0:e], cf[:, C_IOTA:C_IOTA + e], topf[:, t, r:r + 1],
                                                    wtop[:, t, r:r + 1], ALU.is_equal, ALU.mult)
                    step(ins)
                    step(dve.tensor_tensor(dw[:, :, 0:e], hot[:, 0, :, 0:e], hot[:, 1, :, 0:e], ALU.add))
                    if L == 1:
                        step(dve.memset(dw[:, :, e:n], 1.0))
                    dve.wait_ge(S["dt_ps", L], after(i))
                    step(dve.tensor_copy(dp[:, :, 0:n], dw[:, :, 0:n]))
                    step(dve.tensor_tensor(dres[:, :, 0:n], dw[:, :, 0:n], dp[:, :, 0:n], ALU.subtract))
                    step(dve.tensor_copy(dp[:, :, n:2 * n], dres[:, :, 0:n]))
                    dve.tensor_tensor(dp[:, :, 2 * n:3 * n], dres[:, :, 0:n], dp[:, :, n:2 * n], ALU.subtract)\
                       .then_inc(S["dp", L], 1)

                def routing_out(L, i):
                    dve.wait_ge(S["dt_ps", L], after(i + 1))
                    n = PARTS * GR[L]
                    dve.tensor_copy(dT[0:n, ds(i * CH, CH)], PS[DT_BANK[L]][:].bitcast(BF16)[0:n, 0:CH]).then_inc(S["dt_sb", L], 1)

                def moe(L):
                    n_items = NT[L] * CPH
                    wl, sg, hf, hl = (MB[L][n] for n in ("wl", "sg", "hf", "hl"))
                    whf, hhf = MB[L]["wh"].bitcast(F32), MB[L]["hh"].bitcast(F32)

                    def split(h, turn, n):
                        slot = n % RING
                        wait_landed(dve, L, h, turn, n)
                        dve.wait_ge(S["wh_ready", L], after(h * NT[L] + turn * RING + n + 1))
                        dve.tensor_tensor(wl[:, slot, :], ring0[:, slot, :], whf[:, slot, :], ALU.subtract)\
                           .then_inc(S["wl_ready", L], 1)

                    def product(h, base, k):
                        it = h * n_items + base + k
                        dve.wait_ge(S["hl", L], after(it - 1) if k else after(h * n_items))
                        dve.wait_ge(S["silu", L], after(it + 1))
                        dve.wait_ge(S["u_ps", L], after(it + 1))
                        dve.tensor_tensor(hf[:, k % 2, :], PS[(3 * k + 1) % 4][:], sg[:, k % 2, :], ALU.mult)\
                           .then_inc(S["us", L], 1)
                        dve.wait_ge(S["us", L], after(it + 1))
                        dve.wait_ge(S["r_ps", L], after(it + 1))
                        dve.tensor_tensor(hf[:, k % 2, :], PS[(3 * k + 2) % 4][:], hf[:, k % 2, :], ALU.mult)\
                           .then_inc(S["h", L], 1)

                    def low_part(h, base, k):
                        it = h * n_items + base + k
                        dve.wait_ge(S["down", L], after(h * (n_items + OPEN) + OPEN + base + k - 3))
                        dve.wait_ge(S["hh", L], after(it + 1))
                        dve.tensor_tensor(hl[:, k % 4, :], hf[:, k % 2, :], hhf[:, k % 4, :], ALU.subtract)\
                           .then_inc(S["hl", L], 1)

                    body = RING * CPH
                    with dve.Fori(0, HALVES) as h:
                        if L == 0:
                            dve.wait_ge(S["down", L], after(h * (n_items + OPEN)))
                            split(h, 0, 0)
                        product(h, 0, 0)
                        with dve.Fori(0, NT[L] // RING) as p:
                            for j in range(RING):
                                if L == 0:
                                    split(h, p, j + 1)
                                for k in range(j * CPH, (j + 1) * CPH):
                                    product(h, p * body, k + 1)
                                    low_part(h, p * body, k)
                        for k in range(NT[L] // RING * body, n_items):
                            if k + 1 < n_items:
                                product(h, 0, k + 1)
                            low_part(h, 0, k)

                xh32f = xh32.bitcast(F32)

                def linear_attention(i, more):
                    step = Steps(S["chunk_vec", 0], i * N_STEPS[0])
                    ahead = Steps(ln_vec, (i + 1) * N_LN)
                    if more:
                        statistics(0, i + 1, ahead)
                    for m in range(2):
                        dve.wait_ge(qr_sb, after(2 * i + m + 1))
                        qq = qT[:, m, :].rearrange("p (b n) -> p b n", b=2)
                        dve.tensor_tensor(qq, qq, cf[:, C_DROW:C_DROW + SEQ].unsqueeze(1).to_broadcast([P, 2, SEQ]),
                                          ALU.mult).then_inc(qT_ready, 1)
                    dve.wait_ge(k_ready, after(TPC * i))
                    dve.wait_ge(kvm_ps, after(2 * i))
                    for t in range(TPC):
                        dve.wait_ge(kv_ps, after(TPC * i + t + 1))
                        dve.tensor_tensor(kb[:, t, :], PS[6 + t % 2][:, 0:D], r0[:, 0:D], ALU.add)
                        dve.tensor_tensor(vo[:, t, :, 0:P], PS[6 + t % 2][:, D:2 * D].rearrange("p (m n) -> p m n", m=2),
                                          r0[:, D:2 * D].rearrange("p (m n) -> p m n", m=2), ALU.add).then_inc(kv_sb, 1)
                    if more:
                        normalise(0, i + 1, ahead)
                    read_logits(0, i, 2)
                    dve.wait_ge(S["lg_read", 0], after(i + 1))
                    step(dve.tensor_reduce(lmax[:, :, 0], lg[:, :, 0:E0], AX.X, ALU.max))
                    dve.tensor_tensor(lsub[:, :, 0:E0], lg[:, :, 0:E0], lmax[:].to_broadcast([P, TPC, E0]),
                                      ALU.subtract).then_inc(S["lsub", 0], 1)
                    dve.wait_ge(nd_ps, after(TPC * i))
                    for b in range(2):
                        dve.wait_ge(kvm_ps, after(2 * i + b + 1))
                        src = PS[b][:].rearrange("p (m n) -> p m n", m=2)
                        dve.tensor_tensor(kvm[:, b, :, 0:P], src[:, :, 0:P],
                                          cf[:, C_BD:C_BD + P].unsqueeze(1).to_broadcast([P, 2, P]), ALU.mult)
                        dve.tensor_tensor(kvm[:, b, :, P:VO], src[:, :, P:VO],
                                          cf[:, C_BD:C_BD + P:HD].unsqueeze(1).to_broadcast([P, 2, H // 2]),
                                          ALU.mult).then_inc(kvm_ready, 1)
                    for t in range(TPC):
                        dve.wait_ge(nd_ps, after(TPC * i + t + 1))
                        ins = dve.tensor_scalar(den[:, t, :, 0].rearrange("p (m n) -> p m n", m=2),
                                                PS[4 + t][:].rearrange("p (m n) -> p m n", m=2)[:, :, P:VO],
                                                EPS_Z, None, ALU.add)
                    step(ins)
                    step(dve.reciprocal(rden[:], den[:]))
                    dve.wait_ge(aT_ps, after(i))
                    for t in range(TPC):
                        for m in range(2):
                            hs = slice(m * (H // 2), (m + 1) * (H // 2))
                            ins = dve.tensor_tensor(an[:, t, m * P:(m + 1) * P].rearrange("p (h e) -> p h e", e=HD),
                                                    PS[4 + t][:, m * 256:m * 256 + P].rearrange("p (h e) -> p h e", e=HD),
                                                    rden[:, t, hs, :].to_broadcast([P, H // 2, HD]), ALU.mult)
                        ins.then_inc(an_ready, 1)
                    routing(0, i, step)
                    if more:
                        split_x(0, i + 1, ahead)
                        assert ahead.n == N_LN, ahead.n
                    routing_out(0, i)
                    assert step.n == N_STEPS[0], step.n

                ahead = Steps(ln_vec, 0)
                dve.wait_ge(s_x0, 16)
                statistics(0, 0, ahead)
                normalise(0, 0, ahead)
                split_x(0, 0, ahead)
                dve.wait_ge(s_a0, 48)
                dve.wait_ge(s_x, 16 * (NCH - 1))
                dve.wait_ge(s_zero, 3)
                with dve.Fori(0, NCH - 1) as i:
                    linear_attention(i, True)
                linear_attention(NCH - 1, False)
                dve.wait_ge(S["s_ps", 0], after(2 * NCH))
                moe(0)

                dve.wait_ge(s_a1, 48)
                dve.wait_ge(S["y_ps", 0], after(HALVES))
                dve.memset(v1[:, :, :, HD:2 * HD], 1.0).then_inc(ones_set, 1)
                dve.wait_ge(S["y_read", 0], after(4 * HALVES))
                part_hf = part_h.bitcast(F32)

                def gate(c):
                    dve.wait_ge(cb_ps, after(2 * c))
                    dve.tensor_tensor(gs[:], sT[:, :, ds(c * CH, CH)], gT[:, :, ds(c * CH, CH)], ALU.mult)\
                       .then_inc(gs_ready, 1)

                def add_result(c, step):
                    for n in range(2):
                        dve.wait_ge(cb_ps, after(2 * c + n + 1))
                        xx = x[:, ds(c * TPC + 2 * n, 2), :]
                        step(dve.tensor_tensor(xx, xx, PS[6 + n][:].rearrange("p (t d) -> p t d", t=2), ALU.add))

                def low_part_of(i, n):
                    bias = 2 * (n % 2) + n // 2
                    dve.wait_ge(high_ready, after(4 * i + n + 1))
                    if n < 2:
                        dve.wait_ge(spread_ps, after(16 * i))
                    else:
                        dve.wait_ge(spread_ps, after(16 * i + 4 * (n - 1)))
                    dve.scalar_tensor_tensor(out=part_l[:, n % 2, :], in0=PS[6 + n % 2][:], scalar=c1[:, bias:bias + 1],
                                             in1=part_hf[:, n % 2, :], op0=ALU.add, op1=ALU.subtract).then_inc(low_ready, 1)

                def stack(i, n):
                    kind, a = n % 2, n // 2
                    dst, pos, sl = ((QS, C_POSQ, C_SLQ), (KS, C_POSK, C_SLK))[kind]
                    if n == 0:
                        dve.wait_ge(st_ps, after(16 * i))
                    for j in range(4):
                        t = 4 * a + j
                        dve.wait_ge(spread_ps, after(16 * i + 4 * n + j + 1))
                        dve.scalar_tensor_tensor(out=dst[:, t, :].rearrange("p (b n) -> p b n", b=2),
                                                 in0=PS[2 + j][:].rearrange("p (b n) -> p b n", b=2),
                                                 scalar=cf[:, sl + t:sl + t + 1],
                                                 in1=cf[:, pos:pos + SEQ].unsqueeze(1).to_broadcast([P, 2, SEQ]),
                                                 op0=ALU.add, op1=ALU.add).then_inc(stacked, 1)

                def maxima(i, b, U):
                    bb, g, qt = 2 * i + b, U // 2, U % 2
                    bank0 = SCORE_BANKS[b][U % 2]
                    dve.wait_ge(sm_ps, after(8 * bb + U + 1))
                    for r in range(2):
                        src = PS[bank0 + r][:].rearrange("p (j n) -> p j n", j=2)[:, :, 0:(qt + 1) * P]
                        ins = dve.tensor_reduce(mneg[:, qt, 4 * g + r:4 * g + 4:2], src, AX.X, ALU.max, negate=True)
                    ins.then_inc(sm_read, 1)

                def max_parts(i, b, step):
                    bb = 2 * i + b
                    dve.wait_ge(sm_read, after(8 * bb + 8))
                    dve.wait_ge(mt_ps, after(bb))
                    step(dve.tensor_copy(m2[:, :, 0:H], mneg[:]))
                    step(dve.tensor_tensor(mres[:], mneg[:], m2[:, :, 0:H], ALU.subtract))
                    dve.tensor_copy(m2[:, :, H:2 * H], mres[:]).then_inc(m2_ready, 1)

                def read_max(i, b):
                    bb = 2 * i + b
                    dve.wait_ge(mt_ps, after(bb + 1))
                    dve.wait_ge(st_ps, after(8 * bb))
                    dve.tensor_copy(mT[0:2 * H, :], PS[0][:].bitcast(BF16)[0:2 * H, 0:SEQ]).then_inc(mt_sb, 1)

                def divide(i, b, step):
                    bb = 2 * i + b
                    dve.wait_ge(at_ps, after(bb))
                    for qt in range(2):
                        dve.wait_ge(on_ps, after(2 * bb + qt + 1))
                        src = PS[SUM_BANK[b] + qt][:].rearrange("p (h e) -> p h e", h=H)
                        step(dve.reciprocal(orc[:, qt, :, :], src[:, :, HD:HD + 1]))
                        dve.tensor_tensor(ao[:, qt, :].rearrange("p (h e) -> p h e", h=H), src[:, :, 0:HD],
                                          orc[:, qt, :, :].to_broadcast([P, H, HD]), ALU.mult).then_inc(ao_ready, 1)

                def attention(i, more):
                    step = Steps(S["chunk_vec", 1], i * N_STEPS[1])
                    ahead = Steps(front_vec, (i + 1) * N_FRONT)
                    if more:
                        gate(i + 1)
                    low_part_of(i, 0)
                    low_part_of(i, 1)
                    stack(i, 0)
                    low_part_of(i, 2)
                    stack(i, 1)
                    low_part_of(i, 3)
                    stack(i, 2)
                    stack(i, 3)
                    dve.wait_ge(pv_ps, after(8 * i))
                    for n in range(2):
                        dve.wait_ge(v_ps, after(2 * i + n + 1))
                        for t in range(2):
                            ins = dve.tensor_tensor(v1[:, 2 * n + t, :, 0:HD],
                                                    PS[n][:, t * D:(t + 1) * D].rearrange("p (h e) -> p h e", h=H),
                                                    r1[:].rearrange("p (h e) -> p h e", h=H), ALU.add)
                        ins.then_inc(v_sb, 1)
                    for U in range(8):
                        maxima(i, 0, U)
                    max_parts(i, 0, step)
                    read_logits(1, i, 4)
                    read_max(i, 0)
                    if more:
                        add_result(i + 1, ahead)
                    for U in range(8):
                        maxima(i, 1, U)
                        if U == 1 and more:
                            statistics(1, i + 1, ahead)
                        if U == 5 and more:
                            normalise(1, i + 1, ahead)
                    max_parts(i, 1, step)
                    read_max(i, 1)
                    routing(1, i, step)
                    divide(i, 0, step)
                    divide(i, 1, step)
                    routing_out(1, i)
                    if more:
                        split_x(1, i + 1, ahead)
                        assert ahead.n == N_FRONT, ahead.n
                    assert step.n == N_STEPS[1], step.n

                ahead = Steps(front_vec, 0)
                gate(0)
                add_result(0, ahead)
                statistics(1, 0, ahead)
                normalise(1, 0, ahead)
                dve.wait_ge(spread_landed, 16)
                dve.tensor_copy(spread.rearrange("p a b n -> p (a b n)"), spread_stage).then_inc(spread_set, 1)
                split_x(1, 0, ahead)
                with dve.Fori(0, NCH - 1) as i:
                    attention(i, True)
                attention(NCH - 1, False)
                moe(1)
                with dve.Fori(0, NCH) as i:
                    dve.wait_ge(S["y_read", 1], after(4 * HALVES))
                    dve.wait_ge(fcb, after(2 * i))
                    dve.tensor_tensor(gs[:], sT[:, :, ds(i * CH, CH)], gT[:, :, ds(i * CH, CH)], ALU.mult).then_inc(fgs, 1)
                    for n in range(2):
                        dve.wait_ge(fcb, after(2 * i + n + 1))
                        xx = x[:, ds(i * TPC + 2 * n, 2), :]
                        dve.tensor_tensor(xx, xx, PS[4 + n][:].rearrange("p (t d) -> p t d", t=2), ALU.add).then_inc(fx, 1)


N_STEPS = {0: 19, 1: 22}
N_LN = 3
N_FRONT = 5


def kernel(**inp):
    import numpy as np
    import ml_dtypes
    import concourse.bacc as _bacc
    from concourse import mybir as _mybir
    from concourse.bass_utils import run_bass_kernel_spmd as _run

    a = {k: np.asarray(v) for k, v in inp.items()}
    f32, bf16 = np.float32, ml_dtypes.bfloat16

    def kxm(w):
        return w.reshape(2, 128, -1).transpose(1, 0, 2).reshape(128, -1)

    def cols(v):
        return v.reshape(-1, 128).T

    x = a["L0_attn_x"].reshape(-1, 256)
    kv = np.concatenate([a["L0_attn_Wk"].T, a["L0_attn_Wv"].T], 1)
    router0 = np.concatenate([a["L0_ffn_router_weight"].T, a["L0_ffn_shared_gate_w"].T], 1)
    a0 = np.concatenate([kxm(a["L0_attn_Wq"].T), kxm(kv), kxm(a["L0_attn_Wo"].T), kxm(router0)], 1)
    c0 = np.concatenate([cols(a["L0_attn_bq"]), cols(a["L0_attn_bo"])], 1)
    r0 = np.concatenate([a["L0_attn_bk"], a["L0_attn_bv"]])
    wqkv, bqkv = a["L1_attn_w_qkv"], a["L1_attn_b_qkv"]
    a1 = np.concatenate([kxm(wqkv[:, 0:256]), kxm(wqkv[:, 256:512]), kxm(wqkv[:, 512:768]),
                         kxm(a["L1_attn_w_proj"]), kxm(a["L1_ffn_gate_w"].T)], 1)
    c1 = np.concatenate([cols(bqkv[0:512]), cols(a["L1_attn_b_proj"])], 1)
    r1 = bqkv[512:768]

    def tiles(gate, up, down):
        n = n_tiles(gate.shape[0])

        def pad(w):
            o = np.zeros((n * 128, 256), w.dtype)
            o[0:w.shape[0]] = w
            return o.reshape(n, 128, 256)
        t = [pad(w).reshape(n, 128, 2, 128).transpose(0, 3, 2, 1).reshape(n, 128, 256) for w in (gate, up)]
        return np.ascontiguousarray(np.concatenate(t + [pad(down)], 2))

    gu, dn = a["L0_ffn_gate_up_proj"], a["L0_ffn_down_proj"]
    inner0 = gu.shape[1] // 2
    w0 = tiles(np.concatenate([gu[:, :inner0].reshape(-1, 256), a["L0_ffn_sh_gate_w"]]),
               np.concatenate([gu[:, inner0:].reshape(-1, 256), a["L0_ffn_sh_up_w"]]),
               np.concatenate([dn.transpose(0, 2, 1).reshape(-1, 256), a["L0_ffn_sh_down_w"].T]))
    inner1 = a["L1_ffn_w1"].shape[1]
    w1 = tiles(np.concatenate([a["L1_ffn_w1"].reshape(-1, 256), a["L1_ffn_sw1"]]),
               np.concatenate([a["L1_ffn_w3"].reshape(-1, 256), a["L1_ffn_sw3"]]),
               np.concatenate([a["L1_ffn_w2"].transpose(0, 2, 1).reshape(-1, 256), a["L1_ffn_sw2"].T]))

    def selector(inner, experts, shared):
        owner = np.concatenate([np.repeat(np.arange(experts), inner), np.full(shared, experts)])
        o = np.zeros((128, n_tiles(len(owner)) * 128), bf16)
        for part in range(PARTS):
            o[part * (experts + 1) + owner, np.arange(len(owner))] = 1
        return o

    cf = np.zeros((128, N_CF), f32)
    pos = np.arange(SEQ, dtype=f32)
    decay = np.exp(-pos / SEQ).astype(f32)
    p = np.arange(128)
    cf[:, C_ID:C_ID + 128] = np.eye(128)
    cf[:, C_DCOL:C_DCOL + 2] = decay.reshape(2, 128).T
    cf[:, C_DROW:C_DROW + SEQ] = decay
    cf[:, C_BD:C_BD + 128] = (p[:, None] // HD == p[None, :] // HD)
    cf[:, C_IOTA:C_IOTA + E1] = np.arange(E1)
    slope = (HD * np.float32(2.0 ** (-0.5 * np.arange(1, H + 1)))).astype(f32)
    slope_h = np.array([np.float32(np.round(v * 2.0 ** (12 - np.frexp(v)[1])) * 2.0 ** (np.frexp(v)[1] - 12))
                        for v in slope.astype(np.float64)])
    for r in range(2):
        row = 64 * r + 3 * HD
        cf[row + 2:row + 4, C_POSQ:C_POSQ + SEQ] = -pos
        cf[row:row + 2, C_POSK:C_POSK + SEQ] = pos
        for j, part in enumerate((slope_h, slope - slope_h)):
            cf[row + j, C_SLQ:C_SLQ + H // 2] = part[r::2]
            cf[row + 2 + j, C_SLK:C_SLK + H // 2] = part[r::2]
    cf[:, C_EPS] = EPS_LN
    cbs = [np.eye(128), np.where(p[None, :] > p[:, None], -1e30, 0), np.where(p[None, :] < p[:, None], -1e30, 0),
           selector(inner0, E0, a["L0_ffn_sh_gate_w"].shape[0]), selector(inner1, E1, a["L1_ffn_sw1"].shape[0])]
    selm = np.zeros((128, H, 128))
    for h in range(H):
        selm[h, h] = selm[H + h, h] = 1
    spread = np.zeros((128, 4, 4, 128))
    for m, places in enumerate(((0, 2), (1,), (0, 1), (2,))):
        for row in range(128):
            for place in places:
                spread[row, m, row // 32, 64 * (row % 32 // HD) + place * HD + row % HD] = 1
    cbs += [selm.reshape(128, -1), np.zeros((128, 128))]
    cb = np.concatenate([c.astype(bf16) for c in cbs], 1)

    nc = _bacc.Bacc("TRN2", target_bir_lowering=False, num_devices=1)
    arrays, args = {}, []
    for name, v in (("x", x), ("cf", cf), ("cb", cb), ("a0", a0), ("c0", c0), ("r0", r0), ("w0", w0), ("a1", a1),
                    ("c1", c1), ("r1", r1), ("w1", w1), ("spread", spread.reshape(128, -1).astype(bf16))):
        v = np.ascontiguousarray(v)
        arrays[f"in_{name}"] = v
        args.append(nc.dram_tensor(f"in_{name}", v.shape, _mybir.dt.from_np(v.dtype), kind="ExternalInput").ap())
    out = nc.dram_tensor("out_0", x.shape, _mybir.dt.float32, kind="ExternalOutput").ap()
    two_block_kernel(nc, *args, out)
    r = _run(nc, [arrays], core_ids=[0])
    return r.results[0]["out_0"].reshape(a["L0_attn_x"].shape)
```

```python
from contextlib import ExitStack

import concourse.bass as bass
from concourse import mybir

F32 = mybir.dt.float32
F32R = mybir.dt.float32r
BF16 = mybir.dt.bfloat16
F16 = mybir.dt.float16
U32 = mybir.dt.uint32
ALU = mybir.AluOpType
ACT = mybir.ActivationFunctionType
AX = mybir.AxisListType
ds = bass.ds

P = 128
D = 256
KT = D // P
SEQ = 256
CH = 512
TPC = CH // P
H, HD = 16, 16
VO = P + H // 2
EPS_LN, EPS_Z = 1e-5, 1e-6
E0, E1 = 8, 16
G0, G1 = E0 + 1, E1 + 1
PARTS = 3
RING = 4
OPEN = 4
WCOLS = 2 * KT * P + D

C_ID = 0
C_DCOL = C_ID + P
C_DROW = C_DCOL + SEQ // P
C_BD = C_DROW + SEQ
C_IOTA = C_BD + P
C_POS = C_IOTA + E1
C_SLOPE = C_POS + SEQ
C_EPS = C_SLOPE + H // 2
N_CF = C_EPS + 1

MAX_BANK = (2, 6)
DT_BANK = (0, 3)
KV_BANK = (6, 2)
V_BANK = (6, 7, 6, 7)
SUM_BANK = (6, 0)
OUT_BANK = (6, 2)


def score_bank(b, U):
    return 6 if b else 2 if U in (3, 5, 7) else 0


def after(n):
    return n + 1


def prime(eng, sems):
    for s in sems:
        eng.sem_inc(s, 1)


def n_tiles(rows):
    return -(-rows // P)


def two_block_kernel(nc, x_in, cf_in, cb_in, a0_in, c0_in, r0_in, w0_in, a1_in, c1_in, r1_in, w1_in, spread_in, out):
    NCH = x_in.shape[0] // CH
    NTOK = x_in.shape[0] // P
    NT = {0: w0_in.shape[0], 1: w1_in.shape[0]}
    HALVES = 2
    CPH = NCH // HALVES
    GR = {0: G0, 1: G1}
    NE = {0: E0, 1: E1}
    SEL0 = 3 * P
    SEL1 = SEL0 + NT[0] * P
    SELM = SEL1 + NT[1] * P
    ZERO = SELM + H * P
    N_CB = ZERO + P

    with ExitStack() as ctx:
        def sb(name, shape, dt):
            return ctx.enter_context(nc.sbuf_tensor(name, shape, dt))

        def sem(name):
            return ctx.enter_context(nc.semaphore(name))

        PS = [ctx.enter_context(nc.psum_tensor(f"bank{b}", [P, 512], F32)) for b in range(8)]

        x = sb("x", [P, NTOK, D], F32)
        cf = sb("cf", [P, N_CF], F32)
        cb = sb("cb", [P, N_CB], BF16)
        a1 = sb("a1", [P, a1_in.shape[1]], F32)
        c1 = sb("c1", [P, 6], F32)
        r1 = sb("r1", [P, 256], F32)
        s_ = sb("s", [P, NTOK, D], F32)
        g_ = sb("g", [P, NTOK, D], F32)
        gated = sb("gated", [P, TPC, D], F32)
        dT = sb("dT", [P, NCH * CH], BF16)

        ident = cf[:, C_ID:C_ID + P]
        identb = cb[:, 0:P]
        mask_q = cb[:, P:2 * P]
        mask_k = cb[:, 2 * P:3 * P]

        s_x0 = sem("first_x_landed")
        s_x = sem("other_x_landed")
        s_cf = sem("float_constants_landed")
        s_a0 = sem("block0_weights_landed")
        s_cb = sem("bfloat_constants_landed")
        s_a1 = sem("block1_weights_landed")
        s_zero = sem("tables_cleared")
        ones_set = sem("ones_set")

        xn = sb("xn", [P, TPC, D], F32)
        xt = sb("xt", [P, KT, CH], F32)
        stats = sb("stats", [P, TPC, 6], F32)
        mv = sb("mv", [P, TPC, 2], F32)
        sd = sb("sd", [P, TPC], F32)
        rs = sb("rs", [P, TPC], F32)
        lg = sb("lg", [P, TPC, G0], F32)
        lmax = sb("lmax", [P, TPC, 1], F32)
        lsub = sb("lsub", [P, TPC, E0], F32)
        ex = sb("ex", [P, TPC, G1], F32)
        exs = sb("exs", [P, TPC, 1], F32)
        pr = sb("pr", [P, TPC, E1], F32)
        top = sb("top", [P, TPC, 8], F32)
        topi = sb("topi", [P, TPC, 8], U32)
        topf = sb("topf", [P, TPC, 2], F32)
        wsum = sb("wsum", [P, TPC, 1], F32)
        wtop = sb("wtop", [P, TPC, 2], F32)
        hot = sb("hot", [P, 2, TPC, E1], F32)
        dw = sb("dw", [P, TPC, G1], F32)
        dres = sb("dres", [P, TPC, G1], F32)
        dp = sb("dp", [P, TPC, 96], BF16)

        mneg = sb("mneg", [P, 2, H], F32)
        m2 = sb("m2", [P, 2, 2 * H], BF16)
        mT = sb("mT", [P, SEQ], BF16)
        mres = sb("mres", [P, 2, H], F32)
        orc = sb("orc", [P, 2, H, 1], F32)
        ring0 = sb("ring", [P, RING, WCOLS], F32)
        ring1 = ring0[:, :, 0:WCOLS // 2].bitcast(BF16)
        unused_act = sb("unused_act", [P, 1], F32)
        unused_vec = sb("unused_vec", [P, 1], F32)

        def moe_buffers(L, tb):
            return dict(
                wh=tb(f"wh{L}", [P, RING, WCOLS if L == 0 else D], F32R),
                wl=tb(f"wl{L}", [P, RING, WCOLS], F32R) if L == 0 else None,
                sg=tb(f"sg{L}", [P, 2, CH], F32),
                hf=tb(f"hf{L}", [P, 2, CH], F32),
                hh=tb(f"hh{L}", [P, 4, CH], F32R),
                hl=tb(f"hl{L}", [P, 4, CH], F32R))

        def scope(outer):
            inner = ExitStack()
            return inner, lambda name, shape, dt: inner.enter_context(nc.sbuf_tensor(name, shape, dt))[:]

        MB = {}
        block0, tb = scope(ctx)
        xh32 = tb("xh32", [P, KT, NCH * CH], F32R)
        xl32 = tb("xl32", [P, KT, NCH * CH], F32R)
        inner, tb = scope(block0)
        a0 = tb("a0", [P, a0_in.shape[1]], F32)
        c0 = tb("c0", [P, 2], F32)
        r0 = tb("r0", [P, 3 * D], F32)
        qT = tb("qT", [P, 2, CH], F32)
        kb = tb("kb", [P, TPC, D], F32)
        kn = tb("kn", [P, TPC, D], F32)
        vo = tb("vo", [P, TPC, 2, VO], F32)
        kvm = tb("kvm", [P, 2, 2, VO], F32)
        den = tb("den", [P, TPC, H, 1], F32)
        rden = tb("rden", [P, TPC, H, 1], F32)
        an = tb("an", [P, TPC, D], F32)
        aT = tb("aT", [P, 2, CH], F32)
        inner.close()
        inner, tb = scope(block0)
        MB[0] = moe_buffers(0, tb)
        inner.close()
        block0.close()
        block1, tb = scope(ctx)
        xh16 = tb("xh16", [P, KT, NCH * CH], F16)
        xl16 = tb("xl16", [P, KT, NCH * CH], F16)
        inner, tb = scope(block1)
        spread = tb("spread", [P, 4, 4, P], F32R)
        part_h = tb("part_h", [P, 2, CH], F32R)
        part_l = tb("part_l", [P, 2, CH], F32R)
        QS = tb("QS", [P, H // 2, CH], F32R)
        KS = tb("KS", [P, H // 2, CH], F32R)
        v1 = tb("v1", [P, TPC, H, 2 * HD], F32)
        pe_ = tb("expscores", [P, 2, 2, 4, SEQ], F32)
        spread_stage = pe_[:, 0, 0, :, :].rearrange("p j n -> p (j n)").bitcast(BF16)
        ot = tb("ot", [P, 4, SEQ], F32)
        ao = tb("ao", [P, 2, D], F32)
        aoT = tb("aoT", [P, 2, CH], F32)
        inner.close()
        inner, tb = scope(block1)
        MB[1] = moe_buffers(1, tb)
        inner.close()
        block1.close()
        S = {}
        for L in (0, 1):
            for n in ("mv", "sd", "xn", "xt_ps", "xt_sb", "xlo",
                      "ex", "dp", "dt_ps", "dt_sb",
                      "s_ps", "s_sb", "chunk_vec",
                      "wh_ready", "g_ps", "u_ps", "r_ps",
                      "silu", "us", "h", "hh", "hl", "down",
                      "y_ps", "y_read"):
                S[n, L] = sem(f"{n}_{L}")
        for n in ("lg_read", "lsub", "wl_ready"):
            S[n, 0] = sem(f"{n}_0")
        landed = {L: [sem(f"tile_landed_{L}_{n}") for n in range(RING)] for L in (0, 1)}

        def wait_landed(eng, L, h, turn, t):
            slot = t % RING
            eng.wait_ge(landed[L][slot], (h * (NT[L] // RING) + turn + t // RING + 1) * 16)

        def splits(L, h, tile):
            return after(h * (NT[L] - 1) + tile + 1)

        q_ps, qr_sb, qT_ready = sem("q_ps"), sem("qr_sb"), sem("qT_ready")
        kv_ps, kv_sb, k_ready = sem("kv_ps"), sem("kv_sb"), sem("k_ready")
        kvm_ps, kvm_ready, nd_ps, an_ready = sem("kvm_ps"), sem("kvm_ready"), sem("nd_ps"), sem("an_ready")
        aT_ps, aT_sb = sem("aT_ps"), sem("aT_sb")
        vbias_ps, vbias_ready = sem("vbias_ps"), sem("vbias_ready")
        gate_done, x_updated = sem("gate_done"), sem("x_updated")
        proj_ps, high_ready, low_ready = sem("proj_ps"), sem("high_ready"), sem("low_ready")
        spread_ps, q_stacked, k_stacked = sem("spread_ps"), sem("q_stacked"), sem("k_stacked")
        spread_landed, spread_set, front_vec = sem("spread_landed"), sem("spread_set"), sem("front_vec")
        ln_vec = sem("ln_vec")
        v_ps, v_sb = sem("v_ps"), sem("v_sb")
        sm_ps, sm_read, m2_ready = sem("scores_ps"), sem("scores_maxed"), sem("max_parts_ready")
        mt_ps, mt_sb, st_ps, exd = sem("maxT_ps"), sem("maxT_sb"), sem("scoresT_ps"), sem("exp_done")
        pv_ps, ot_sb, on_ps, ao_ready = sem("pv_ps"), sem("ot_sb"), sem("on_ps"), sem("ao_ready")
        at_ps, at_sb = sem("at_ps"), sem("at_sb")
        last_gated, last_x, s_out = sem("last_gated"), sem("last_x"), sem("out_stored")

        block = ctx.enter_context(nc.Block())

        @block.sync
        def _(sp):
            xv = x_in.rearrange("(t p) d -> p t d", p=P)
            sp.dma_start(x[:, 0:TPC, :], xv[:, 0:TPC, :]).then_inc(s_x0, 16)
            sp.dma_start(c0, c0_in).then_inc(s_a0, 16)
            sp.dma_start(r0, r0_in.partition_broadcast(P)).then_inc(s_a0, 16)
            for c in range(1, NCH):
                sp.dma_start(x[:, c * TPC:(c + 1) * TPC, :], xv[:, c * TPC:(c + 1) * TPC, :]).then_inc(s_x, 16)
            sp.dma_start(cb[:], cb_in).then_inc(s_cb, 16)
            sp.dma_start(a1[:], a1_in).then_inc(s_a1, 16)
            sp.dma_start(c1[:], c1_in).then_inc(s_a1, 16)
            sp.dma_start(r1[:], r1_in.partition_broadcast(P)).then_inc(s_a1, 16)

            def stream(L, w_in, ring, freed, freed_before):
                def load(tile, slot):
                    sp.dma_start(ring[:, slot, :], w_in[ds(tile, 1)].rearrange("a p n -> (a p) n"))\
                      .then_inc(landed[L][slot], 16)

                sp.dma_start(ring[:, 0, :], w_in[0]).then_inc(landed[L][0], 16)
                with sp.Fori(0, HALVES) as h:
                    first = [sp.snap(h * -1 + n) for n in range(1, RING)]
                    last = sp.snap(h * -1 + (NT[L] - 1))
                    freed_before(h)
                    for n in range(1, RING):
                        load(first[n - 1], n)
                    with sp.Fori(0, NT[L] // RING - 1) as p:
                        for j in range(RING):
                            tile = sp.snap(p * RING + RING + j - h)
                            freed(h, p * RING + j)
                            load(tile, j)
                    freed(h, NT[L] - 1 - RING)
                    load(last, 0)

            def freed0(h, tile):
                sp.wait_ge(S["wh_ready", 0], splits(0, h, tile))
                sp.wait_ge(S["wl_ready", 0], splits(0, h, tile))

            def freed_before0(h):
                sp.wait_ge(S["wh_ready", 0], after(h * (NT[0] - 1)))
                sp.wait_ge(S["wl_ready", 0], after(h * (NT[0] - 1)))

            def freed1(h, tile):
                sp.wait_ge(S["down", 1], after(h * (NT[1] * CPH + OPEN) + OPEN + (tile + 1) * CPH))

            def freed_before1(h):
                sp.wait_ge(S["down", 1], after(h * (NT[1] * CPH + OPEN - CPH)))

            stream(0, w0_in, ring0, freed0, freed_before0)
            sp.wait_ge(S["y_ps", 0], after(HALVES))
            sp.dma_start(spread_stage, spread_in).then_inc(spread_landed, 16)
            stream(1, w1_in, ring1, freed1, freed_before1)
            ov = out.rearrange("(n t p) d -> n p t d", p=P, t=2)
            for c in range(CPH):
                sp.wait_ge(x_updated, after(NCH + c + 1))
                for n in range(2):
                    sp.dma_start(ov[2 * c + n], x[:, (2 * c + n) * 2:(2 * c + n) * 2 + 2, :]).then_inc(s_out, 16)
            for n in range(2 * CPH, 4 * CPH):
                sp.wait_ge(last_x, n - 2 * CPH + 1)
                sp.dma_start(ov[n], x[:, 2 * n:2 * n + 2, :]).then_inc(s_out, 16)
            sp.wait_ge(s_out, 16 * 2 * NCH)

        @block.gpsimd
        def _(pool):
            pool.dma_start(cf[:], cf_in).then_inc(s_cf, 16)
            pool.memset(dT[:], 0.0).then_inc(s_zero, 1)
            pool.memset(mT[:], 0.0).then_inc(s_zero, 1)
            pool.memset(dp[:], 0.0).then_inc(s_zero, 1)
            pool.memset(vo[:, :, :, P:VO], 1.0).then_inc(ones_set, 1)
            prime(pool, [gate_done, x_updated])

            def update(L, c):
                n = L * NCH + c
                tiles = ds(c * TPC, TPC)
                pool.tensor_tensor(gated[:], s_[:, tiles, :], g_[:, tiles, :], ALU.mult).then_inc(gate_done, 1)
                pool.wait_ge(gate_done, after(n + 1))
                pool.tensor_tensor(x[:, tiles, :], x[:, tiles, :], gated[:], ALU.add).then_inc(x_updated, 1)
                pool.wait_ge(x_updated, after(n + 1))

            with pool.Fori(0, HALVES) as h:
                pool.wait_ge(S["y_read", 0], after(h * 4 + 4))
                for c in range(CPH):
                    update(0, h * CPH + c)
            pool.wait_ge(S["y_read", 1], after(4))
            for c in range(CPH):
                update(1, c)

        @block.tensor
        def _(pe):
            prime(pe, [S[n, L] for L in (0, 1) for n in
                       ("xt_ps", "dt_ps", "s_ps", "g_ps", "u_ps", "r_ps", "down", "y_ps")]
                  + [q_ps, kv_ps, kvm_ps, nd_ps, aT_ps, proj_ps, spread_ps, v_ps, sm_ps, mt_ps, st_ps, pv_ps, on_ps,
                     at_ps])
            pe.wait_ge(s_cf, 16)

            def x_transposes(L, i, banks):
                pe.wait_ge(S["xn", L], after(4 * i + 4))
                for k in range(KT):
                    for t in range(TPC):
                        mm = pe.transpose(PS[banks[k]][:, t * P:(t + 1) * P], xn[:, t, k * P:(k + 1) * P], ident)
                    mm.then_inc(S["xt_ps", L], 1)

            def out_projection(L, a, w, acol, banks, ready):
                for n in range(2):
                    ready(n)
                    for t in range(2):
                        for m in range(2):
                            mm = pe.matmul(PS[banks + n][:, t * D:(t + 1) * D], a[:, m, (2 * n + t) * P:(2 * n + t + 1) * P],
                                           w[:, acol + m * D:acol + (m + 1) * D], start=(m == 0 and t == 0),
                                           stop=(m == 1), skip_group_check=True)
                    mm.then_inc(S["s_ps", L], 1)

            def routing_transposes(L, i):
                pe.wait_ge(S["dp", L], after(i + 1))
                n = PARTS * GR[L]
                dst = PS[DT_BANK[L]][:].bitcast(BF16)
                if L == 1:
                    n = 96
                for t in range(TPC):
                    mm = pe.transpose(dst[0:n, t * P:(t + 1) * P], dp[:, t, 0:n], identb)
                mm.then_inc(S["dt_ps", L], 1)

            def moe(L):
                n_items = NT[L] * CPH
                xs = (xh32, xl32) if L == 0 else (xh16, xl16)
                wh, wl, hh, hl = (MB[L][n] for n in ("wh", "wl", "hh", "hl"))
                down0 = 2 * KT * P if L == 0 else 0

                def gates(h, base, k, turn):
                    slot, c = (k // CPH) % RING, k % CPH
                    g, u, r = (PS[(3 * k + n) % 4] for n in range(3))
                    tok = ds(h * (CPH * CH) + c * CH, CH)
                    tile_reg = turn * RING + k // CPH
                    if c == 0:
                        if L == 0:
                            pe.wait_ge(S["wh_ready", L], splits(L, h, tile_reg))
                        else:
                            wait_landed(pe, L, h, turn, k // CPH)
                    for out_, col, ready in ((g, 0, S["g_ps", L]), (u, KT * P, S["u_ps", L])):
                        if out_ is g:
                            if k >= 2:
                                pe.wait_ge(S["h", L], after(h * n_items + base + k - 1))
                        elif k >= 1:
                            pe.wait_ge(S["silu", L], after(h * n_items + base + k))
                        src = wh if L == 0 else ring1
                        terms = [(src, xx, kt) for kt in range(KT) for xx in xs]
                        if L == 0:
                            terms += [(wl, xh32, kt) for kt in range(KT)]
                        for n, (w, xx, kt) in enumerate(terms):
                            if w is wl and n == 2 * KT and c == 0 and out_ is g:
                                pe.wait_ge(S["wl_ready", L], splits(L, h, tile_reg))
                            mm = pe.matmul(out_[:], w[:, slot, col + kt * P:col + (kt + 1) * P], xx[:, kt, tok],
                                           start=(n == 0), stop=(n == len(terms) - 1))
                        mm.then_inc(ready, 1)
                    if k >= 1:
                        pe.wait_ge(S["us", L], after(h * n_items + base + k))
                    s0 = SEL0 if L == 0 else SEL1
                    owner = tile_reg - h if k >= CPH else h * (NT[L] - 1)
                    pe.matmul(r[:], cb[:, ds(s0 + owner * P, P)], dT[:, tok], start=True,
                              stop=True).then_inc(S["r_ps", L], 1)

                def down(h, base, tile, k):
                    slot, c = (k // CPH) % RING, k % CPH
                    pe.wait_ge(S["hl", L], after(h * n_items + base + k + 1))
                    if L == 1:
                        pe.wait_ge(S["wh_ready", L], splits(L, h, tile + k // CPH))
                    for t in range(TPC):
                        out_ = PS[4 + 2 * c + t // 2][:, (t % 2) * D:(t % 2 + 1) * D]
                        for w, a in [(wh, hh)] + ([(wl, hh)] if L == 0 else []) + [(wh, hl)]:
                            mm = pe.matmul(out_, a[:, k % 4, t * P:(t + 1) * P], w[:, slot, down0:down0 + D],
                                           start=False, stop=False, skip_group_check=True)
                    mm.then_inc(S["down", L], 1)
                    return mm

                body = RING * CPH
                with pe.Fori(0, HALVES) as h:
                    pe.wait_ge(S["h", L], after(h * n_items))
                    gates(h, 0, 0, 0)
                    gates(h, 0, 1, 0)
                    pe.wait_ge(S["y_read", L], after(h * 4))
                    for b in range(4):
                        pe.matmul(PS[4 + b][:], zcol, dT[:, 0:CH], start=True, stop=False,
                                  skip_group_check=True).then_inc(S["down", L], 1)
                    with pe.Fori(0, NT[L] // RING) as p:
                        for k in range(body):
                            gates(h, p * body, k + 2, p)
                            down(h, p * body, p * RING, k)
                    for k in range(NT[L] // RING * body, n_items):
                        mm = down(h, 0, 0, k)
                    pe.matmul(PS[7][:], zcol, dT[:, 0:CH], start=False, stop=True,
                              skip_group_check=True).then_inc(S["y_ps", L], 1)

            zcol = cb[:, ZERO:ZERO + P]

            def linear_attention(i, more):
                for m in range(2):
                    for k in range(KT):
                        mm = pe.matmul(PS[4 + m][:], a0[:, k * D + m * P:k * D + (m + 1) * P], xt[:, k, :],
                                       start=(k == 0), stop=(k == 1))
                    mm.then_inc(q_ps, 1)
                for t in range(TPC):
                    if t == 1:
                        pe.wait_ge(S["s_sb", 0], after(2 * i))
                    if t >= 2:
                        pe.wait_ge(kv_sb, after(i * TPC + t - 1))
                    for bank, c, n in ((KV_BANK[t % 2], 0, D + G0), (KV_BANK[t % 2] + 1, D + G0, D)):
                        for k in range(KT):
                            w0_ = 512 + k * (2 * D + G0) + c
                            mm = pe.matmul(PS[bank][:, 0:n], xt[:, k, t * P:(t + 1) * P], a0[:, w0_:w0_ + n],
                                           start=(k == 0), stop=(k == 1))
                    mm.then_inc(kv_ps, 1)
                pe.wait_ge(S["dt_sb", 0], after(i))
                for b in range(2):
                    pe.wait_ge(k_ready, after(i * TPC + 2 * b + 2))
                    pe.wait_ge(kv_sb, after(i * TPC + 2 * b + 2))
                    for m in range(2):
                        for t in range(2):
                            mm = pe.matmul(PS[b][:, m * 256:m * 256 + VO], kn[:, 2 * b + t, m * P:(m + 1) * P],
                                           vo[:, 2 * b + t, m, :], start=(m == 0 and t == 0), stop=(t == 1),
                                           skip_group_check=True)
                    mm.then_inc(kvm_ps, 1)
                pe.wait_ge(qT_ready, after(2 * i + 2))
                for b in range(2):
                    pe.wait_ge(kvm_ready, after(2 * i + b + 1))
                    for t in (2 * b, 2 * b + 1):
                        for m in range(2):
                            mm = pe.matmul(PS[4 + t][:, m * 256:m * 256 + VO], qT[:, m, t * P:(t + 1) * P],
                                           kvm[:, b, m, :], start=(m == 0), stop=True, skip_group_check=True)
                    mm.then_inc(nd_ps, 1)
                    if b == 0 and more:
                        x_transposes(0, i + 1, (3, 2))
                for b in range(2):
                    pe.wait_ge(an_ready, after(2 * i + b + 1))
                    for t in range(2):
                        for m in range(2):
                            mm = pe.transpose(PS[b][:, m * SEQ + t * P:m * SEQ + (t + 1) * P],
                                              an[:, 2 * b + t, m * P:(m + 1) * P], ident)
                    mm.then_inc(aT_ps, 1)
                if more:
                    pe.wait_ge(S["xt_sb", 0], after(2 * i + 4))
                out_projection(0, aT, a0, 512 + KT * (2 * D + G0), 2,
                               lambda b: pe.wait_ge(aT_sb, after(2 * i + b + 1)))
                pe.wait_ge(s_cb, 16)
                routing_transposes(0, i)

            x_transposes(0, 0, (3, 2))
            pe.wait_ge(s_a0, 48)
            pe.wait_ge(s_zero, 3)
            pe.wait_ge(ones_set, 1)
            pe.wait_ge(S["xt_sb", 0], after(2))
            with pe.Fori(0, NCH - 1) as i:
                linear_attention(i, True)
            linear_attention(NCH - 1, False)
            pe.wait_ge(S["s_sb", 0], after(2 * NCH))
            pe.wait_ge(S["dt_sb", 0], after(NCH))
            pe.wait_ge(S["xlo", 0], after(NCH))
            moe(0)

            pe.wait_ge(s_a1, 48)
            pe.wait_ge(ones_set, 2)

            pe.wait_ge(S["y_read", 0], after(4 * HALVES))
            for m in range(2):
                w0_ = 1024 + KT * (D + E1) + m * D
                mm = pe.matmul(PS[0][:, 0:D], c1[:, 4 + m:5 + m].to_broadcast([P, P]), a1[:, w0_:w0_ + D],
                               start=(m == 0), stop=(m == 1))
            mm.then_inc(vbias_ps, 1)

            def project(i, n):
                kind, a = n % 2, n // 2
                if n >= 2:
                    pe.wait_ge(low_ready, after(4 * i + n - 1))
                for k in range(KT):
                    w0_ = kind * 512 + k * D + a * P
                    mm = pe.matmul(PS[6 + n % 2][:], a1[:, w0_:w0_ + P], xt[:, k, :], start=(k == 0), stop=(k == 1))
                mm.then_inc(proj_ps, 1)

            def spread_pairs(i, n):
                kind = n % 2
                pe.wait_ge(high_ready, after(4 * i + n + 1))
                pe.wait_ge(low_ready, after(4 * i + n + 1))
                for j in range(4):
                    if n:
                        pe.wait_ge((k_stacked, q_stacked)[kind], after(8 * i + 4 * ((n - 1) // 2) + j + 1))
                    pe.matmul(PS[2 + j][:], spread[:, 2 * kind, j, :], part_h[:, n % 2, :], start=True, stop=False)
                    pe.matmul(PS[2 + j][:], spread[:, 2 * kind + 1, j, :], part_l[:, n % 2, :],
                              start=False, stop=True).then_inc(spread_ps, 1)

            def project_values(i, t):
                for k in range(KT):
                    w0_ = 1024 + k * (D + E1)
                    mm = pe.matmul(PS[V_BANK[t]][:, 0:D + E1], xt[:, k, t * P:(t + 1) * P], a1[:, w0_:w0_ + D + E1],
                                   start=(k == 0), stop=(k == 1))
                mm.then_inc(v_ps, 1)

            def scores(i, b, U):
                bb, g, qt = 2 * i + b, U // 2, U % 2
                bank0 = score_bank(b, U)
                if U:
                    pe.wait_ge(sm_read, after(8 * bb + U - (b == 0 and U >= 3)))
                for r in range(2):
                    rows = slice(64 * r, 64 * r + 64)
                    bank = PS[bank0 + r]
                    for p in range(2):
                        q0 = b * SEQ + qt * P
                        pe.matmul(bank[:, p * SEQ:(p + 1) * SEQ], QS[rows, 2 * g + p, q0:q0 + P],
                                  KS[rows, 2 * g + p, b * SEQ:(b + 1) * SEQ], start=(p == 0), stop=False,
                                  skip_group_check=True)
                for r in range(2):
                    mm = pe.matmul(PS[bank0 + r][:].rearrange("p (j n) -> p j n", j=2)[:, :, qt * P:(qt + 1) * P],
                                   identb, mask_q.unsqueeze(1).to_broadcast([P, 2, P]),
                                   start=False, stop=True, skip_group_check=True)
                mm.then_inc(sm_ps, 1)

            def max_transposes(i, b):
                bb = 2 * i + b
                pe.wait_ge(m2_ready, after(bb + 1))
                mb_ = PS[MAX_BANK[b]][:].bitcast(BF16)
                for qt in range(2):
                    mm = pe.transpose(mb_[0:2 * H, qt * P:(qt + 1) * P], m2[:, qt, :], identb)
                mm.then_inc(mt_ps, 1)

            def scores_T(i, b, V):
                bb, g, kt = 2 * i + b, V // 2, V % 2
                if V >= 2 or b == 1:
                    pe.wait_ge(exd, after(8 * bb + V - 1))
                elif V == 1:
                    pe.wait_ge(mt_sb, after(bb + 1))
                q0 = kt * P
                for r in range(2):
                    rows = slice(64 * r, 64 * r + 64)
                    bank = PS[2 * (V % 2) + r]
                    for p in range(2):
                        k0 = b * SEQ + kt * P
                        pe.matmul(bank[:, p * SEQ:(p + 1) * SEQ], KS[rows, 2 * g + p, k0:k0 + P],
                                  QS[rows, 2 * g + p, b * SEQ:(b + 1) * SEQ], start=(p == 0), stop=False,
                                  skip_group_check=True)
                if V == 0:
                    pe.wait_ge(mt_sb, after(bb + 1))
                for r in range(2):
                    bank = PS[2 * (V % 2) + r]
                    for p in range(2):
                        sm0 = SELM + (4 * g + 2 * p + r) * P
                        pe.matmul(bank[:, p * SEQ + q0:(p + 1) * SEQ], cb[:, sm0:sm0 + P], mT[:, q0:SEQ],
                                  start=False, stop=False, skip_group_check=True)
                    mm = pe.matmul(bank[:].rearrange("p (j n) -> p j n", j=2)[:, :, q0:q0 + P],
                                   identb, mask_k.unsqueeze(1).to_broadcast([P, 2, P]),
                                   start=False, stop=True, skip_group_check=True)
                mm.then_inc(st_ps, 1)

            def weighted_values(i, b, g):
                bb = 2 * i + b
                pe.wait_ge(exd, after(8 * bb + 2 * g + 2))
                if g == 0:
                    if b == 0:
                        pe.wait_ge(v_sb, after(TPC * i + TPC))
                    else:
                        pe.wait_ge(ot_sb, after(2 * bb))
                for r in range(2):
                    for p in range(2):
                        j = 2 * p + r
                        o_ = PS[4 + g // 2][32 * j:32 * j + 32, (g % 2) * 256:(g % 2) * 256 + 256]
                        pe.matmul(o_, v1[:, 2 * b, 4 * g + j, :], pe_[:, g % 2, 0, 2 * r + p, :],
                                  start=(g % 2 == 0), stop=False, skip_group_check=True)
                        mm = pe.matmul(o_[:, P:2 * P], v1[:, 2 * b + 1, 4 * g + j, :],
                                       pe_[:, g % 2, 1, 2 * r + p, P:2 * P], start=False, stop=True,
                                       skip_group_check=True)
                mm.then_inc(pv_ps, 1)

            def heads_transposes(i, b):
                bb = 2 * i + b
                pe.wait_ge(ot_sb, after(2 * bb + 2))
                for qt in range(2):
                    for g in range(4):
                        mm = pe.transpose(PS[SUM_BANK[b] + qt][:, g * P:(g + 1) * P], ot[:, g, qt * P:(qt + 1) * P], ident)
                    mm.then_inc(on_ps, 1)

            def outputs_transposes(i, b):
                bb = 2 * i + b
                pe.wait_ge(ao_ready, after(2 * bb + 2))
                for qt in range(2):
                    for m in range(2):
                        mm = pe.transpose(PS[OUT_BANK[b]][:, (m * 2 + qt) * P:(m * 2 + qt + 1) * P],
                                          ao[:, qt, m * P:(m + 1) * P], ident)
                mm.then_inc(at_ps, 1)

            def attention(i, more):
                pe.wait_ge(S["dt_sb", 1], after(i))
                project(i, 0)
                project(i, 1)
                spread_pairs(i, 0)
                project(i, 2)
                spread_pairs(i, 1)
                project(i, 3)
                spread_pairs(i, 2)
                pe.wait_ge(S["s_sb", 1], after(2 * i))
                pe.wait_ge(q_stacked, after(8 * i + 4))
                pe.wait_ge(k_stacked, after(8 * i + 4))
                scores(i, 0, 0)
                pe.wait_ge(low_ready, after(4 * i + 4))
                project_values(i, 0)
                scores(i, 0, 1)
                spread_pairs(i, 3)
                scores(i, 0, 2)
                project_values(i, 1)
                pe.wait_ge(q_stacked, after(8 * i + 8))
                pe.wait_ge(k_stacked, after(8 * i + 8))
                for U in range(3, 8):
                    scores(i, 0, U)
                    if U in (5, 7):
                        t = 2 + U // 7
                        pe.wait_ge(v_sb, after(TPC * i + t - 1))
                        project_values(i, t)
                max_transposes(i, 0)
                scores_T(i, 0, 0)
                pe.wait_ge(v_sb, after(TPC * i + TPC))
                scores(i, 1, 0)
                scores_T(i, 0, 1)
                scores(i, 1, 1)
                for g in (1, 2):
                    scores_T(i, 0, 2 * g)
                    scores_T(i, 0, 2 * g + 1)
                    scores(i, 1, 2 * g)
                    weighted_values(i, 0, g - 1)
                    scores(i, 1, 2 * g + 1)
                scores_T(i, 0, 6)
                scores(i, 1, 6)
                scores_T(i, 0, 7)
                scores(i, 1, 7)
                weighted_values(i, 0, 2)
                weighted_values(i, 0, 3)
                max_transposes(i, 1)
                for g in range(4):
                    scores_T(i, 1, 2 * g)
                    scores_T(i, 1, 2 * g + 1)
                    if g == 0:
                        heads_transposes(i, 0)
                    if g == 2:
                        outputs_transposes(i, 0)
                    if g:
                        weighted_values(i, 1, g - 1)
                weighted_values(i, 1, 3)
                routing_transposes(1, i)
                heads_transposes(i, 1)
                if more:
                    pe.wait_ge(at_sb, after(2 * i + 1))
                    x_transposes(1, i + 1, (7, 6))
                outputs_transposes(i, 1)
                out_projection(1, aoT, a1, 1024 + KT * (D + E1), 0,
                               lambda b: pe.wait_ge(at_sb, after(2 * i + b + 1)))
                if more:
                    pe.wait_ge(S["xt_sb", 1], after(2 * i + 4))

            x_transposes(1, 0, (7, 6))
            pe.wait_ge(S["xt_sb", 1], after(2))
            pe.wait_ge(spread_set, 1)
            pe.wait_ge(vbias_ready, 1)
            with pe.Fori(0, NCH - 1) as i:
                attention(i, True)
            attention(NCH - 1, False)
            pe.wait_ge(S["s_sb", 1], after(2 * NCH))
            pe.wait_ge(S["dt_sb", 1], after(NCH))
            pe.wait_ge(S["xlo", 1], after(NCH))
            moe(1)
        @block.scalar
        def _(act):
            prime(act, [S[n, L] for L in (0, 1) for n in
                        ("sd", "xt_sb", "ex", "wh_ready", "silu", "hh", "y_read")]
                  + [qr_sb, k_ready, aT_sb, high_ready, q_stacked, v_sb, exd, ot_sb, at_sb])
            act.dma_start(a0, a0_in).then_inc(s_a0, 16)
            act.wait_ge(s_cf, 16)
            eps_ln = cf[:, C_EPS:C_EPS + 1]

            def deviation(L, i):
                act.wait_ge(S["mv", L], after(i + 1))
                act.activation(sd[:], mv[:, :, 1], ACT.Sqrt, bias=eps_ln).then_inc(S["sd", L], 1)

            def x_copies(L, i, banks):
                act.wait_ge(S["xlo", L], after(i))
                act.wait_ge(kv_ps if L == 0 else v_ps, after(TPC * i))
                for k in range(KT):
                    act.wait_ge(S["xt_ps", L], after(2 * i + k + 1))
                    act.activation(xt[:, k, :], PS[banks[k]][:], ACT.Copy).then_inc(S["xt_sb", L], 1)

            def moe(L):
                n_items = NT[L] * CPH
                w0c = 0 if L == 0 else 2 * KT * P
                wh, sg, hf, hh = (MB[L][n] for n in ("wh", "sg", "hf", "hh"))

                def split(h, turn, n):
                    slot = n % RING
                    wait_landed(act, L, h, turn, n)
                    src = ring0 if L == 0 else ring1
                    act.activation(wh[:, slot, :], src[:, slot, w0c:WCOLS], ACT.Copy).then_inc(S["wh_ready", L], 1)

                def silu(h, base, k):
                    act.wait_ge(S["g_ps", L], after(h * n_items + base + k + 1))
                    act.activation(sg[:, k % 2, :], PS[(3 * k) % 4][:], ACT.Silu).then_inc(S["silu", L], 1)

                def high_part(h, base, k):
                    act.wait_ge(S["h", L], after(h * n_items + base + k + 1))
                    act.wait_ge(S["down", L], after(h * (n_items + OPEN) + OPEN + base + k - 3))
                    act.activation(hh[:, k % 4, :], hf[:, k % 2, :], ACT.Copy).then_inc(S["hh", L], 1)

                body = RING * CPH
                split(0, 0, 0)
                with act.Fori(0, HALVES) as h:
                    silu(h, 0, 0)
                    with act.Fori(0, NT[L] // RING) as p:
                        for j in range(RING):
                            act.wait_ge(S["down", L], after(h * (n_items + OPEN) + OPEN + p * body + (j - 2) * CPH))
                            split(h, p, j + 1)
                            for k in range(j * CPH, (j + 1) * CPH):
                                silu(h, p * body, k + 1)
                                high_part(h, p * body, k)
                    for k in range(NT[L] // RING * body, n_items):
                        if k + 1 < n_items:
                            silu(h, 0, k + 1)
                        high_part(h, 0, k)
                    act.wait_ge(S["y_ps", L], after(h + 1))
                    for n in range(2 * CPH):
                        act.activation(g_[:, ds(h * (CPH * TPC) + 2 * n, 2), :],
                                       PS[4 + n][:].rearrange("p (t d) -> p t d", t=2),
                                       ACT.Silu).then_inc(S["y_read", L], 1)

            def linear_attention(i, more):
                act.wait_ge(qT_ready, after(2 * i))
                act.wait_ge(nd_ps, after(2 * i))
                for m in range(2):
                    act.wait_ge(q_ps, after(2 * i + m + 1))
                    act.activation(qT[:, m, :], PS[4 + m][:], ACT.Relu, bias=c0[:, m:m + 1]).then_inc(qr_sb, 1)
                if more:
                    deviation(0, i + 1)
                act.wait_ge(kvm_ps, after(2 * i))
                for t in range(TPC):
                    act.wait_ge(kv_sb, after(TPC * i + t + 1))
                    act.activation(kn[:, t, :], kb[:, t, :], ACT.Relu,
                                   scale=cf[:, C_DCOL + t % 2:C_DCOL + t % 2 + 1]).then_inc(k_ready, 1)
                act.wait_ge(S["lsub", 0], after(i + 1))
                act.activation(ex[:, :, 0:E0], lsub[:], ACT.Exp)
                act.activation(ex[:, :, E0:G0], lg[:, :, E0:G0], ACT.Exp, scale=-1.0).then_inc(S["ex", 0], 1)
                if more:
                    x_copies(0, i + 1, (3, 2))
                act.wait_ge(S["s_ps", 0], after(2 * i))
                for b in range(2):
                    act.wait_ge(aT_ps, after(2 * i + b + 1))
                    act.activation(aT[:, :, b * SEQ:(b + 1) * SEQ], PS[b][:].rearrange("p (m n) -> p m n", m=2),
                                   ACT.Copy).then_inc(aT_sb, 1)

            act.activation(unused_act[:], eps_ln, ACT.Sqrt)
            deviation(0, 0)
            x_copies(0, 0, (3, 2))
            act.wait_ge(s_a0, 48)
            with act.Fori(0, NCH - 1) as i:
                linear_attention(i, True)
            linear_attention(NCH - 1, False)
            moe(0)

            act.wait_ge(s_a1, 48)

            def exp_scores(i, b, V):
                bb, g, kt = 2 * i + b, V // 2, V % 2
                q0 = kt * P
                act.wait_ge(st_ps, after(8 * bb + V + 1))
                act.wait_ge(pv_ps, after(4 * bb + max(g - 1, 0)))
                for r in range(2):
                    ins = act.activation(pe_[:, g % 2, kt, 2 * r:2 * r + 2, q0:SEQ],
                                         PS[2 * (V % 2) + r][:].rearrange("p (j n) -> p j n", j=2)[:, :, q0:SEQ],
                                         ACT.Exp, scale=1.0 / HD)
                ins.then_inc(exd, 1)

            def sums_copies(i, b):
                bb = 2 * i + b
                for n in range(2):
                    act.wait_ge(pv_ps, after(4 * bb + 2 * n + 2))
                    if n == 0:
                        act.wait_ge(on_ps, after(2 * bb))
                    act.activation(ot[:, 2 * n:2 * n + 2, :], PS[4 + n][:].rearrange("p (g n) -> p g n", g=2),
                                   ACT.Copy).then_inc(ot_sb, 1)

            def outputs_copy(i, b):
                act.wait_ge(at_ps, after(2 * i + b + 1))
                if b == 0:
                    act.wait_ge(S["s_ps", 1], after(2 * i))
                act.activation(aoT[:, :, b * SEQ:(b + 1) * SEQ],
                               PS[OUT_BANK[b]][:].rearrange("p (m n) -> p m n", m=2), ACT.Copy).then_inc(at_sb, 1)

            def stack_q(i, a):
                for j in range(4):
                    t = 4 * a + j
                    act.wait_ge(spread_ps, after(16 * i + 8 * a + j + 1))
                    act.activation(QS[:, t, :], PS[2 + j][:], ACT.Identity,
                                   bias=cf[:, C_SLOPE + t:C_SLOPE + t + 1]).then_inc(q_stacked, 1)

            def attention(i, more):
                act.wait_ge(spread_ps, after(16 * i))
                for n in range(4):
                    act.wait_ge(proj_ps, after(4 * i + n + 1))
                    if n >= 2:
                        act.wait_ge(spread_ps, after(16 * i + 4 * (n - 1)))
                    bias = 2 * (n % 2) + n // 2
                    act.activation(part_h[:, n % 2, :], PS[6 + n % 2][:], ACT.Identity,
                                   bias=c1[:, bias:bias + 1]).then_inc(high_ready, 1)
                    if n == 1:
                        act.wait_ge(st_ps, after(16 * i))
                        stack_q(i, 0)
                stack_q(i, 1)
                act.wait_ge(pv_ps, after(8 * i))
                act.wait_ge(S["dp", 1], after(i))
                for t in range(TPC):
                    act.wait_ge(v_ps, after(TPC * i + t + 1))
                    bank = PS[V_BANK[t]]
                    act.activation(ex[:, t, 0:E1], bank[:, D:D + E1], ACT.Exp, scale=-1.0).then_inc(S["ex", 1], 1)
                    act.activation(v1[:, t, :, 0:HD], bank[:, 0:D].rearrange("p (h e) -> p h e", h=H),
                                   ACT.Copy).then_inc(v_sb, 1)
                for V in range(8):
                    exp_scores(i, 0, V)
                    if V == 5 and more:
                        deviation(1, i + 1)
                sums_copies(i, 0)
                for V in range(8):
                    exp_scores(i, 1, V)
                    if V == 5:
                        outputs_copy(i, 0)
                sums_copies(i, 1)
                if more:
                    x_copies(1, i + 1, (7, 6))
                outputs_copy(i, 1)

            deviation(1, 0)
            x_copies(1, 0, (7, 6))
            act.wait_ge(spread_set, 1)
            with act.Fori(0, NCH - 1) as i:
                attention(i, True)
            attention(NCH - 1, False)
            moe(1)

        @block.vector
        def _(dve):
            prime(dve, [S[n, L] for L in (0, 1) for n in
                        ("mv", "xn", "xlo", "s_sb", "dp", "dt_sb", "chunk_vec", "us", "h", "hl")]
                  + [S[n, 0] for n in ("lg_read", "lsub", "wl_ready")]
                  + [qT_ready, kv_sb, kvm_ready, an_ready, low_ready, k_stacked, front_vec, ln_vec, sm_read,
                     m2_ready, mt_sb, ao_ready])
            dve.wait_ge(s_cf, 16)

            def hold():
                dve.memset(unused_vec[:], 0.0)

            class Steps:

                def __init__(self, sem_, base):
                    self.sem, self.base, self.n = sem_, base, 0

                def __call__(self, ins):
                    self.n += 1
                    ins.then_inc(self.sem, 1)
                    dve.wait_ge(self.sem, after(self.base + self.n))

            def statistics(L, i, step):
                hold()
                for t in range(TPC):
                    ins = dve.bn_stats(stats[:, t, :], x[:, ds(i * TPC + t, 1), :].rearrange("p a d -> p (a d)"))
                step(ins)
                dve.wait_ge(S["sd", L], after(i))
                hold()
                for t in range(TPC):
                    ins = dve.bn_aggr(mv[:, t, :], stats[:, t, :])
                ins.then_inc(S["mv", L], 1)

            def normalise(L, i, step):
                dve.wait_ge(S["sd", L], after(i + 1))
                step(dve.reciprocal(rs[:], sd[:]))
                dve.wait_ge(S["xt_ps", L], after(2 * i))
                for t in range(TPC):
                    dve.tensor_scalar(xn[:, t, :], x[:, ds(i * TPC + t, 1), :].rearrange("p a d -> p (a d)"),
                                      mv[:, t, 0:1], rs[:, t:t + 1], ALU.subtract, ALU.mult).then_inc(S["xn", L], 1)

            def split_x(L, i, step):
                hi, lo = (xh32, xl32) if L == 0 else (xh16, xl16)
                dve.wait_ge(S["xt_sb", L], after(2 * i + 2))
                step(dve.tensor_copy(hi[:, :, ds(i * CH, CH)], xt[:]))
                hv = hi[:, :, ds(i * CH, CH)]
                if L == 0:
                    hv = xh32f[:, :, ds(i * CH, CH)]
                dve.tensor_tensor(lo[:, :, ds(i * CH, CH)], xt[:], hv, ALU.subtract).then_inc(S["xlo", L], 1)

            def result(L, i, bank, row):
                for n in range(2):
                    dve.wait_ge(S["s_ps", L], after(2 * i + n + 1))
                    dve.tensor_tensor(s_[:, ds(i * TPC + 2 * n, 2), :], PS[bank + n][:].rearrange("p (t d) -> p t d", t=2),
                                      row.unsqueeze(1).to_broadcast([P, 2, D]), ALU.add).then_inc(S["s_sb", L], 1)

            def routing(L, i, step):
                e, n = NE[L], GR[L]
                dve.wait_ge(S["ex", L], after(i + 1 if L == 0 else TPC * (i + 1)))
                if L == 0:
                    step(dve.tensor_reduce(exs[:, :, 0], ex[:, :, 0:E0], AX.X, ALU.add))
                    step(dve.reciprocal(wsum[:], exs[:]))
                    step(dve.tensor_tensor(pr[:, :, 0:E0], ex[:, :, 0:E0], wsum[:].to_broadcast([P, TPC, E0]), ALU.mult))
                    step(dve.tensor_scalar(ex[:, :, E0:G0], ex[:, :, E0:G0], 1.0, None, ALU.add))
                    step(dve.reciprocal(dw[:, :, E0:G0], ex[:, :, E0:G0]))
                else:
                    step(dve.tensor_scalar(ex[:, :, 0:E1], ex[:, :, 0:E1], 1.0, None, ALU.add))
                    step(dve.reciprocal(pr[:, :, 0:E1], ex[:, :, 0:E1]))
                hold()
                for t in range(TPC):
                    ins = dve.max(top[:, t, :], pr[:, t, 0:e])
                step(ins)
                hold()
                for t in range(TPC):
                    ins = dve.max_index(topi[:, t, :], top[:, t, :], pr[:, t, 0:e])
                step(ins)
                step(dve.tensor_copy(topf[:], topi[:, :, 0:2]))
                step(dve.tensor_tensor(exs[:], top[:, :, 0:1], top[:, :, 1:2], ALU.add))
                step(dve.reciprocal(wsum[:], exs[:]))
                step(dve.tensor_tensor(wtop[:], top[:, :, 0:2], wsum[:].to_broadcast([P, TPC, 2]), ALU.mult))
                for r in range(2):
                    ins = dve.tensor_tensor(hot[:, r, :, 0:e], cf[:, C_IOTA:C_IOTA + e].unsqueeze(1).to_broadcast([P, TPC, e]),
                                            topf[:, :, r:r + 1].to_broadcast([P, TPC, e]), ALU.is_equal)
                step(ins)
                for r in range(2):
                    ins = dve.tensor_tensor(hot[:, r, :, 0:e], hot[:, r, :, 0:e],
                                            wtop[:, :, r:r + 1].to_broadcast([P, TPC, e]), ALU.mult)
                step(ins)
                step(dve.tensor_tensor(dw[:, :, 0:e], hot[:, 0, :, 0:e], hot[:, 1, :, 0:e], ALU.add))
                if L == 1:
                    step(dve.memset(dw[:, :, e:n], 1.0))
                dve.wait_ge(S["dt_ps", L], after(i))
                step(dve.tensor_copy(dp[:, :, 0:n], dw[:, :, 0:n]))
                step(dve.tensor_tensor(dres[:, :, 0:n], dw[:, :, 0:n], dp[:, :, 0:n], ALU.subtract))
                step(dve.tensor_copy(dp[:, :, n:2 * n], dres[:, :, 0:n]))
                dve.tensor_tensor(dp[:, :, 2 * n:3 * n], dres[:, :, 0:n], dp[:, :, n:2 * n], ALU.subtract)\
                   .then_inc(S["dp", L], 1)

            def routing_out(L, i):
                dve.wait_ge(S["dt_ps", L], after(i + 1))
                n = PARTS * GR[L]
                dve.tensor_copy(dT[0:n, ds(i * CH, CH)], PS[DT_BANK[L]][:].bitcast(BF16)[0:n, 0:CH]).then_inc(S["dt_sb", L], 1)

            def moe(L):
                n_items = NT[L] * CPH
                wl, sg, hf, hl = (MB[L][n] for n in ("wl", "sg", "hf", "hl"))
                whf, hhf = MB[L]["wh"].bitcast(F32), MB[L]["hh"].bitcast(F32)

                def split(h, turn, n):
                    slot = n % RING
                    wait_landed(dve, L, h, turn, n)
                    dve.wait_ge(S["wh_ready", L], splits(L, h, turn * RING + n))
                    dve.tensor_tensor(wl[:, slot, :], ring0[:, slot, :], whf[:, slot, :], ALU.subtract)\
                       .then_inc(S["wl_ready", L], 1)

                def product(h, base, k):
                    it = h * n_items + base + k
                    dve.wait_ge(S["hl", L], after(it - 1) if k else after(h * n_items))
                    dve.wait_ge(S["silu", L], after(it + 1))
                    dve.wait_ge(S["u_ps", L], after(it + 1))
                    dve.tensor_tensor(hf[:, k % 2, :], PS[(3 * k + 1) % 4][:], sg[:, k % 2, :], ALU.mult)\
                       .then_inc(S["us", L], 1)
                    dve.wait_ge(S["us", L], after(it + 1))
                    dve.wait_ge(S["r_ps", L], after(it + 1))
                    dve.tensor_tensor(hf[:, k % 2, :], PS[(3 * k + 2) % 4][:], hf[:, k % 2, :], ALU.mult)\
                       .then_inc(S["h", L], 1)

                def low_part(h, base, k):
                    it = h * n_items + base + k
                    dve.wait_ge(S["down", L], after(h * (n_items + OPEN) + OPEN + base + k - 3))
                    dve.wait_ge(S["hh", L], after(it + 1))
                    dve.tensor_tensor(hl[:, k % 4, :], hf[:, k % 2, :], hhf[:, k % 4, :], ALU.subtract)\
                       .then_inc(S["hl", L], 1)

                body = RING * CPH
                if L == 0:
                    split(0, 0, 0)
                with dve.Fori(0, HALVES) as h:
                    product(h, 0, 0)
                    with dve.Fori(0, NT[L] // RING) as p:
                        for j in range(RING):
                            if L == 0:
                                split(h, p, j + 1)
                            for k in range(j * CPH, (j + 1) * CPH):
                                product(h, p * body, k + 1)
                                low_part(h, p * body, k)
                    for k in range(NT[L] // RING * body, n_items):
                        if k + 1 < n_items:
                            product(h, 0, k + 1)
                        low_part(h, 0, k)

            xh32f = xh32.bitcast(F32)

            def linear_attention(i, more):
                step = Steps(S["chunk_vec", 0], i * N_STEPS[0])
                ahead = Steps(ln_vec, (i + 1) * N_LN)
                if more:
                    statistics(0, i + 1, ahead)
                for m in range(2):
                    dve.wait_ge(qr_sb, after(2 * i + m + 1))
                    qq = qT[:, m, :].rearrange("p (b n) -> p b n", b=2)
                    dve.tensor_tensor(qq, qq, cf[:, C_DROW:C_DROW + SEQ].unsqueeze(1).to_broadcast([P, 2, SEQ]),
                                      ALU.mult).then_inc(qT_ready, 1)
                dve.wait_ge(k_ready, after(TPC * i))
                dve.wait_ge(kvm_ps, after(2 * i))
                dve.wait_ge(S["ex", 0], after(i))
                for t in range(TPC):
                    bank = KV_BANK[t % 2]
                    dve.wait_ge(kv_ps, after(TPC * i + t + 1))
                    dve.tensor_tensor(kb[:, t, :], PS[bank][:, 0:D], r0[:, 0:D], ALU.add)
                    ins = dve.tensor_copy(lg[:, t, 0:G0], PS[bank][:, D:D + G0])
                    if t == TPC - 1:
                        ins.then_inc(S["lg_read", 0], 1)
                    dve.tensor_tensor(vo[:, t, :, 0:P], PS[bank + 1][:, 0:D].rearrange("p (m n) -> p m n", m=2),
                                      r0[:, D:2 * D].rearrange("p (m n) -> p m n", m=2), ALU.add).then_inc(kv_sb, 1)
                if more:
                    normalise(0, i + 1, ahead)
                dve.wait_ge(S["lg_read", 0], after(i + 1))
                step(dve.tensor_reduce(lmax[:, :, 0], lg[:, :, 0:E0], AX.X, ALU.max))
                dve.tensor_tensor(lsub[:], lg[:, :, 0:E0], lmax[:].to_broadcast([P, TPC, E0]),
                                  ALU.subtract).then_inc(S["lsub", 0], 1)
                dve.wait_ge(nd_ps, after(2 * i))
                for b in range(2):
                    dve.wait_ge(kvm_ps, after(2 * i + b + 1))
                    src = PS[b][:].rearrange("p (m n) -> p m n", m=2)
                    dve.tensor_tensor(kvm[:, b, :, 0:P], src[:, :, 0:P],
                                      cf[:, C_BD:C_BD + P].unsqueeze(1).to_broadcast([P, 2, P]), ALU.mult)
                    dve.tensor_tensor(kvm[:, b, :, P:VO], src[:, :, P:VO],
                                      cf[:, C_BD:C_BD + P:HD].unsqueeze(1).to_broadcast([P, 2, H // 2]),
                                      ALU.mult).then_inc(kvm_ready, 1)
                dve.wait_ge(aT_ps, after(2 * i))
                for b in range(2):
                    dve.wait_ge(nd_ps, after(2 * i + b + 1))
                    for t in (2 * b, 2 * b + 1):
                        ins = dve.tensor_scalar(den[:, t, :, 0].rearrange("p (m n) -> p m n", m=2),
                                                PS[4 + t][:].rearrange("p (m n) -> p m n", m=2)[:, :, P:VO],
                                                EPS_Z, None, ALU.add)
                    step(ins)
                    step(dve.reciprocal(rden[:, 2 * b:2 * b + 2], den[:, 2 * b:2 * b + 2]))
                    for t in (2 * b, 2 * b + 1):
                        ins = dve.tensor_tensor(an[:, t, :].rearrange("p (m h e) -> p m h e", m=2, e=HD),
                                                PS[4 + t][:].rearrange("p (m n) -> p m n", m=2)[:, :, 0:P]
                                                .rearrange("p m (h e) -> p m h e", e=HD),
                                                rden[:, t].rearrange("p (m h) o -> p m h o", m=2)
                                                .to_broadcast([P, 2, H // 2, HD]), ALU.mult)
                    ins.then_inc(an_ready, 1)
                routing(0, i, step)
                result(0, i, 2, r0[:, 2 * D:3 * D])
                routing_out(0, i)
                if more:
                    split_x(0, i + 1, ahead)
                    assert ahead.n == N_LN, ahead.n
                assert step.n == N_STEPS[0], step.n

            ahead = Steps(ln_vec, 0)
            dve.wait_ge(s_x0, 16)
            statistics(0, 0, ahead)
            normalise(0, 0, ahead)
            split_x(0, 0, ahead)
            dve.wait_ge(s_a0, 48)
            dve.wait_ge(s_x, 16 * (NCH - 1))
            dve.wait_ge(s_zero, 3)
            with dve.Fori(0, NCH - 1) as i:
                linear_attention(i, True)
            linear_attention(NCH - 1, False)
            dve.wait_ge(S["s_ps", 0], after(2 * NCH))
            moe(0)

            dve.wait_ge(s_a1, 48)
            dve.wait_ge(S["y_ps", 0], after(HALVES))
            dve.memset(v1[:, :, :, HD:2 * HD], 1.0).then_inc(ones_set, 1)
            part_hf = part_h.bitcast(F32)

            def low_part_of(i, n):
                bias = 2 * (n % 2) + n // 2
                dve.wait_ge(high_ready, after(4 * i + n + 1))
                if n < 2:
                    dve.wait_ge(spread_ps, after(16 * i))
                else:
                    dve.wait_ge(spread_ps, after(16 * i + 4 * (n - 1)))
                dve.scalar_tensor_tensor(out=part_l[:, n % 2, :], in0=PS[6 + n % 2][:], scalar=c1[:, bias:bias + 1],
                                         in1=part_hf[:, n % 2, :], op0=ALU.add, op1=ALU.subtract).then_inc(low_ready, 1)

            def stack_k(i, a):
                for j in range(4):
                    t = 4 * a + j
                    dve.wait_ge(spread_ps, after(16 * i + 8 * a + 4 + j + 1))
                    dve.tensor_tensor(KS[:, t, :].rearrange("p (b n) -> p b n", b=2),
                                      PS[2 + j][:].rearrange("p (b n) -> p b n", b=2),
                                      cf[:, C_POS:C_POS + SEQ].unsqueeze(1).to_broadcast([P, 2, SEQ]),
                                      ALU.add).then_inc(k_stacked, 1)

            def maxima(i, b, U):
                bb, g, qt = 2 * i + b, U // 2, U % 2
                bank0 = score_bank(b, U)
                dve.wait_ge(sm_ps, after(8 * bb + U + 1))
                for r in range(2):
                    src = PS[bank0 + r][:].rearrange("p (j n) -> p j n", j=2)[:, :, 0:(qt + 1) * P]
                    ins = dve.tensor_reduce(mneg[:, qt, 4 * g + r:4 * g + 4:2], src, AX.X, ALU.max, negate=True)
                ins.then_inc(sm_read, 1)

            def max_parts(i, b, step):
                bb = 2 * i + b
                dve.wait_ge(sm_read, after(8 * bb + 8))
                dve.wait_ge(mt_ps, after(bb))
                step(dve.tensor_copy(m2[:, :, 0:H], mneg[:]))
                step(dve.tensor_tensor(mres[:], mneg[:], m2[:, :, 0:H], ALU.subtract))
                dve.tensor_copy(m2[:, :, H:2 * H], mres[:]).then_inc(m2_ready, 1)

            def read_max(i, b):
                bb = 2 * i + b
                dve.wait_ge(mt_ps, after(bb + 1))
                dve.wait_ge(st_ps, after(8 * bb))
                dve.tensor_copy(mT[0:2 * H, :], PS[MAX_BANK[b]][:].bitcast(BF16)[0:2 * H, 0:SEQ]).then_inc(mt_sb, 1)

            def divide(i, b, step):
                bb = 2 * i + b
                dve.wait_ge(at_ps, after(bb))
                for qt in range(2):
                    dve.wait_ge(on_ps, after(2 * bb + qt + 1))
                    src = PS[SUM_BANK[b] + qt][:].rearrange("p (h e) -> p h e", h=H)
                    step(dve.reciprocal(orc[:, qt, :, :], src[:, :, HD:HD + 1]))
                    dve.tensor_tensor(ao[:, qt, :].rearrange("p (h e) -> p h e", h=H), src[:, :, 0:HD],
                                      orc[:, qt, :, :].to_broadcast([P, H, HD]), ALU.mult).then_inc(ao_ready, 1)

            def attention(i, more):
                step = Steps(S["chunk_vec", 1], i * N_STEPS[1])
                ahead = Steps(front_vec, (i + 1) * N_FRONT)
                low_part_of(i, 0)
                low_part_of(i, 1)
                low_part_of(i, 2)
                dve.wait_ge(st_ps, after(16 * i))
                stack_k(i, 0)
                low_part_of(i, 3)
                maxima(i, 0, 0)
                maxima(i, 0, 1)
                stack_k(i, 1)
                for U in range(2, 8):
                    maxima(i, 0, U)
                max_parts(i, 0, step)
                read_max(i, 0)
                for U in range(8):
                    maxima(i, 1, U)
                    if U == 1 and more:
                        dve.wait_ge(x_updated, after(i + 2))
                        statistics(1, i + 1, ahead)
                max_parts(i, 1, step)
                read_max(i, 1)
                divide(i, 0, step)
                if more:
                    normalise(1, i + 1, ahead)
                routing(1, i, step)
                routing_out(1, i)
                divide(i, 1, step)
                result(1, i, 0, vbias)
                if more:
                    split_x(1, i + 1, ahead)
                    assert ahead.n == N_FRONT, ahead.n
                assert step.n == N_STEPS[1], step.n

            ahead = Steps(front_vec, 0)
            dve.wait_ge(x_updated, after(1))
            statistics(1, 0, ahead)
            dve.wait_ge(vbias_ps, 1)
            vbias = r1[:]
            dve.tensor_tensor(vbias, vbias, PS[0][:, 0:D], ALU.add).then_inc(vbias_ready, 1)
            normalise(1, 0, ahead)
            dve.wait_ge(spread_landed, 16)
            dve.tensor_copy(spread.rearrange("p a b n -> p (a b n)"), spread_stage).then_inc(spread_set, 1)
            split_x(1, 0, ahead)
            dve.wait_ge(vbias_ready, 1)
            with dve.Fori(0, NCH - 1) as i:
                attention(i, True)
            attention(NCH - 1, False)
            moe(1)
            last = xn[:].rearrange("p (b t) d -> p b t d", b=2)
            for n in range(2 * CPH):
                dve.wait_ge(S["y_read", 1], after(2 * CPH + n + 1))
                tiles = slice(2 * (2 * CPH + n), 2 * (2 * CPH + n) + 2)
                if n >= 2:
                    dve.wait_ge(last_x, n - 1)
                dve.tensor_tensor(last[:, n % 2], s_[:, tiles, :], g_[:, tiles, :], ALU.mult).then_inc(last_gated, 1)
                dve.wait_ge(last_gated, n + 1)
                dve.tensor_tensor(x[:, tiles, :], x[:, tiles, :], last[:, n % 2], ALU.add).then_inc(last_x, 1)


N_STEPS = {0: 22, 1: 23}
N_LN = 3
N_FRONT = 3


def kernel(**inp):
    import numpy as np
    import ml_dtypes
    import concourse.bacc as _bacc
    from concourse import mybir as _mybir
    from concourse.bass_utils import run_bass_kernel_spmd as _run

    a = {k: np.asarray(v) for k, v in inp.items()}
    f32, bf16 = np.float32, ml_dtypes.bfloat16

    def kxm(w):
        return w.reshape(2, 128, -1).transpose(1, 0, 2).reshape(128, -1)

    def cols(v):
        return v.reshape(-1, 128).T

    x = a["L0_attn_x"].reshape(-1, 256)
    router0 = np.concatenate([a["L0_ffn_router_weight"].T, a["L0_ffn_shared_gate_w"].T], 1)
    kv = np.concatenate([a["L0_attn_Wk"].T, router0, a["L0_attn_Wv"].T], 1)
    a0 = np.concatenate([kxm(a["L0_attn_Wq"].T), kxm(kv), kxm(a["L0_attn_Wo"].T)], 1)
    c0 = cols(a["L0_attn_bq"])
    r0 = np.concatenate([a["L0_attn_bk"], a["L0_attn_bv"], a["L0_attn_bo"]])
    wqkv, bqkv = a["L1_attn_w_qkv"], a["L1_attn_b_qkv"]
    v_router = np.concatenate([wqkv[:, 512:768], a["L1_ffn_gate_w"].T], 1)
    a1 = np.concatenate([kxm(wqkv[:, 0:256]), kxm(wqkv[:, 256:512]), kxm(v_router), kxm(a["L1_attn_w_proj"])], 1)
    c1 = cols(bqkv)
    r1 = a["L1_attn_b_proj"]

    def tiles(gate, up, down):
        n = n_tiles(gate.shape[0])

        def pad(w):
            o = np.zeros((n * 128, 256), w.dtype)
            o[0:w.shape[0]] = w
            return o.reshape(n, 128, 256)
        t = [pad(w).reshape(n, 128, 2, 128).transpose(0, 3, 2, 1).reshape(n, 128, 256) for w in (gate, up)]
        return np.ascontiguousarray(np.concatenate(t + [pad(down)], 2))

    gu, dn = a["L0_ffn_gate_up_proj"], a["L0_ffn_down_proj"]
    inner0 = gu.shape[1] // 2
    w0 = tiles(np.concatenate([gu[:, :inner0].reshape(-1, 256), a["L0_ffn_sh_gate_w"]]),
               np.concatenate([gu[:, inner0:].reshape(-1, 256), a["L0_ffn_sh_up_w"]]),
               np.concatenate([dn.transpose(0, 2, 1).reshape(-1, 256), a["L0_ffn_sh_down_w"].T]))
    inner1 = a["L1_ffn_w1"].shape[1]
    w1 = tiles(np.concatenate([a["L1_ffn_w1"].reshape(-1, 256), a["L1_ffn_sw1"]]),
               np.concatenate([a["L1_ffn_w3"].reshape(-1, 256), a["L1_ffn_sw3"]]),
               np.concatenate([a["L1_ffn_w2"].transpose(0, 2, 1).reshape(-1, 256), a["L1_ffn_sw2"].T]))

    def selector(inner, experts, shared):
        owner = np.concatenate([np.repeat(np.arange(experts), inner), np.full(shared, experts)])
        o = np.zeros((128, n_tiles(len(owner)) * 128), bf16)
        for part in range(PARTS):
            o[part * (experts + 1) + owner, np.arange(len(owner))] = 1
        return o

    cf = np.zeros((128, N_CF), f32)
    pos = np.arange(SEQ, dtype=f32)
    decay = np.exp(-pos / SEQ).astype(f32)
    p = np.arange(128)
    cf[:, C_ID:C_ID + 128] = np.eye(128)
    cf[:, C_DCOL:C_DCOL + 2] = decay.reshape(2, 128).T
    cf[:, C_DROW:C_DROW + SEQ] = decay
    cf[:, C_BD:C_BD + 128] = (p[:, None] // HD == p[None, :] // HD)
    cf[:, C_IOTA:C_IOTA + E1] = np.arange(E1)
    slope = (HD * np.float32(2.0 ** (-0.5 * np.arange(1, H + 1)))).astype(f32)
    slope_h = np.array([np.float32(np.round(v * 2.0 ** (12 - np.frexp(v)[1])) * 2.0 ** (np.frexp(v)[1] - 12))
                        for v in slope.astype(np.float64)])
    for r in range(2):
        row = 64 * r + 3 * HD
        cf[row:row + 2, C_POS:C_POS + SEQ] = pos
        for j, part in enumerate((slope_h, slope - slope_h)):
            cf[row + j, C_SLOPE:C_SLOPE + H // 2] = part[r::2]
    cf[:, C_EPS] = EPS_LN
    cbs = [np.eye(128), np.where(p[None, :] > p[:, None], -1e30, 0), np.where(p[None, :] < p[:, None], -1e30, 0),
           selector(inner0, E0, a["L0_ffn_sh_gate_w"].shape[0]), selector(inner1, E1, a["L1_ffn_sw1"].shape[0])]
    selm = np.zeros((128, H, 128))
    for h in range(H):
        selm[h, h] = selm[H + h, h] = 1
    spread = np.zeros((128, 4, 4, 128))
    for m, places in enumerate(((0, 2), (1,), (0, 1), (2,))):
        for row in range(128):
            for place in places:
                spread[row, m, row // 32, 64 * (row % 32 // HD) + place * HD + row % HD] = 1
    cbs += [selm.reshape(128, -1), np.zeros((128, 128))]
    cb = np.concatenate([c.astype(bf16) for c in cbs], 1)

    nc = _bacc.Bacc("TRN2", target_bir_lowering=False, num_devices=1)
    arrays, args = {}, []
    for name, v in (("x", x), ("cf", cf), ("cb", cb), ("a0", a0), ("c0", c0), ("r0", r0), ("w0", w0), ("a1", a1),
                    ("c1", c1), ("r1", r1), ("w1", w1), ("spread", spread.reshape(128, -1).astype(bf16))):
        v = np.ascontiguousarray(v)
        arrays[f"in_{name}"] = v
        args.append(nc.dram_tensor(f"in_{name}", v.shape, _mybir.dt.from_np(v.dtype), kind="ExternalInput").ap())
    out = nc.dram_tensor("out_0", x.shape, _mybir.dt.float32, kind="ExternalOutput").ap()
    two_block_kernel(nc, *args, out)
    r = _run(nc, [arrays], core_ids=[0])
    return r.results[0]["out_0"].reshape(a["L0_attn_x"].shape)
```
